# Optimizing a Trainium2 kernel written in Bass

```python
import numpy as np
import jax
import jax.numpy as jnp

def _softmax(x, axis=-1):
    return jax.nn.softmax(x, axis=axis)

def _gelu(x):
    return jax.nn.gelu(x, approximate=True)

def _silu(x):
    return jax.nn.silu(x)

def _sigmoid(x):
    return jax.nn.sigmoid(x)

def _layernorm(x, axis=-1, eps=1e-05):
    m = jnp.mean(x, axis=axis, keepdims=True)
    v = jnp.var(x, axis=axis, keepdims=True)
    return (x - m) / jnp.sqrt(v + eps)

def _scatter_add(tgt, idx, src, axis=0):
    return tgt.at[idx].add(src)

def _segment_sum(src, seg, n):
    return jax.ops.segment_sum(src, seg, n)
kernel_name = 'mk_seq_postln_d2_jaxref_r8_345278'

def setup_inputs(seed: int=0):
    np.random.seed(seed)
    _w = jnp.asarray

    def _L0_attn_setup():
        import jax, jax.numpy as jnp
        import numpy as np
        import math
        EMBED_DIM = 128
        NUM_HEADS = 16
        NUM_KV_HEADS = 16
        DEPTH = 12
        HEAD_DIM = EMBED_DIM // NUM_HEADS // 2
        LAMBDA_INIT = 0.8 - 0.6 * math.exp(-0.3 * DEPTH)
        EPS = 1e-05
        THETA = 0.0001

        def rope(q):
            b, s, h, d = q.shape
            pos = jnp.arange(s, dtype=jnp.float32)[:, None]
            freq = 1.0 / THETA ** (2.0 * jnp.arange(d // 2, dtype=jnp.float32) / d)
            ang = pos * freq
            cos = jnp.cos(ang)[None, :, None, :].astype(q.dtype)
            sin = jnp.sin(ang)[None, :, None, :].astype(q.dtype)
            qr = q.reshape(b, s, h, d // 2, 2)
            q0, q1 = (qr[..., 0], qr[..., 1])
            out = jnp.stack([q0 * cos - q1 * sin, q0 * sin + q1 * cos], axis=-1)
            return out.reshape(q.shape)
        key = jax.random.key(seed)
        ks = jax.random.split(key, 10)
        d = EMBED_DIM
        sd = 1.0 / math.sqrt(d)
        return {'x': jax.random.normal(ks[0], (1, 256, d), dtype=jnp.float32), 'Wq': jax.random.normal(ks[1], (d, d), dtype=jnp.float32) * sd, 'Wk': jax.random.normal(ks[2], (d, d), dtype=jnp.float32) * sd, 'Wv': jax.random.normal(ks[3], (d, d), dtype=jnp.float32) * sd, 'Wo': jax.random.normal(ks[4], (d, d), dtype=jnp.float32) * sd, 'lambda_q1': jax.random.normal(ks[5], (HEAD_DIM,), dtype=jnp.float32) * 0.1, 'lambda_k1': jax.random.normal(ks[6], (HEAD_DIM,), dtype=jnp.float32) * 0.1, 'lambda_q2': jax.random.normal(ks[7], (HEAD_DIM,), dtype=jnp.float32) * 0.1, 'lambda_k2': jax.random.normal(ks[8], (HEAD_DIM,), dtype=jnp.float32) * 0.1, 'subln_g': jnp.ones((2 * HEAD_DIM,), dtype=jnp.float32)}
    _L0_attn_in = _L0_attn_setup()

    def _L0_ffn_setup():
        import jax, jax.numpy as jnp
        import numpy as np
        E = 8
        K = 2
        key = jax.random.key(seed)
        ks = jax.random.split(key, 6)
        B, S, D, F = (4, 256, 128, 512)
        s_d = 1.0 / np.sqrt(D).astype(np.float32)
        s_f = 1.0 / np.sqrt(F).astype(np.float32)
        return {'x': jax.random.normal(ks[0], (B, S, D), jnp.float32), 'ln_w': jnp.ones((D,), jnp.float32), 'Wg': jax.random.normal(ks[1], (D, E), jnp.float32) * s_d, 'bg': jnp.zeros((E,), jnp.float32), 'W1a': jax.random.normal(ks[2], (E, D, F), jnp.float32) * s_d, 'b1a': jnp.zeros((E, F), jnp.float32), 'W1b': jax.random.normal(ks[3], (E, D, F), jnp.float32) * s_d, 'b1b': jnp.zeros((E, F), jnp.float32), 'W2': jax.random.normal(ks[4], (E, F, D), jnp.float32) * s_f, 'b2': jnp.zeros((E, D), jnp.float32)}
    _L0_ffn_in = _L0_ffn_setup()

    def _L1_attn_setup():
        import jax, jax.numpy as jnp
        import numpy as np
        EPS = 1e-05

        def _ln(x, g, b):
            m = jnp.mean(x, axis=-1, keepdims=True)
            v = jnp.mean((x - m) ** 2, axis=-1, keepdims=True)
            return (x - m) * jax.lax.rsqrt(v + EPS) * g + b

        def _forward(x, ln_attn_g, ln_attn_b, Wq, bq, Wk, bk, Wv, bv, ln_conv_g, ln_conv_b, conv_w, conv_b, ln_boom_g, ln_boom_b, Wb, bb, Wu, bu):
            B, S, D = x.shape
            K = conv_w.shape[-1]
            G = D // conv_w.shape[1]
            h = _ln(x, ln_conv_g, ln_conv_b)
            hc = jnp.transpose(h, (0, 2, 1))
            hc = jnp.pad(hc, ((0, 0), (0, 0), (K - 1, 0)))
            conv = jax.lax.conv_general_dilated(hc, conv_w, window_strides=(1,), padding='VALID', dimension_numbers=('NCH', 'OIH', 'NCH'), feature_group_count=G)
            conv = conv + conv_b[None, :, None]
            x = x + jnp.transpose(conv, (0, 2, 1))
            h = _ln(x, ln_attn_g, ln_attn_b)
            q = jnp.einsum('bsd,ed->bse', h, Wq) + bq
            k = jnp.einsum('bsd,ed->bse', h, Wk) + bk
            v = jnp.einsum('bsd,ed->bse', h, Wv) + bv
            scale = jnp.arange(1, S + 1, dtype=x.dtype)[None, :, None]
            pooled_q = jnp.cumsum(q, axis=1) / scale
            pooled_k = jnp.cumsum(pooled_q * k, axis=1) / scale
            x = x + pooled_k * v
            h = _ln(x, ln_boom_g, ln_boom_b)
            h = jax.nn.gelu(jnp.einsum('bsd,ed->bse', h, Wb) + bb, approximate=False)
            h = jnp.einsum('bse,de->bsd', h, Wu) + bu
            return x + h
        key = jax.random.key(seed)
        ks = jax.random.split(key, 8)
        B, S, D, K, G = (4, 256, 128, 4, 4)
        w = lambda k, shape: jax.random.normal(k, shape, jnp.float32) * 0.02
        return {'hidden_states': jax.random.normal(ks[0], (B, S, D), jnp.float32), 'attention_mask': jnp.ones((B, S), jnp.int32), 'ln_attn_g': jnp.ones((D,), jnp.float32), 'ln_attn_b': jnp.zeros((D,), jnp.float32), 'Wq': w(ks[1], (D, D)), 'bq': jnp.zeros((D,), jnp.float32), 'Wk': w(ks[2], (D, D)), 'bk': jnp.zeros((D,), jnp.float32), 'Wv': w(ks[3], (D, D)), 'bv': jnp.zeros((D,), jnp.float32), 'ln_conv_g': jnp.ones((D,), jnp.float32), 'ln_conv_b': jnp.zeros((D,), jnp.float32), 'conv_w': w(ks[4], (D, D // G, K)), 'conv_b': jnp.zeros((D,), jnp.float32), 'ln_boom_g': jnp.ones((D,), jnp.float32), 'ln_boom_b': jnp.zeros((D,), jnp.float32), 'Wb': w(ks[5], (4 * D, D)), 'bb': jnp.zeros((4 * D,), jnp.float32), 'Wu': w(ks[6], (D, 4 * D)), 'bu': jnp.zeros((D,), jnp.float32)}
    _L1_attn_in = _L1_attn_setup()

    def _L1_ffn_setup():
        import jax, jax.numpy as jnp
        import numpy as np
        B, S, D = (1, 256, 128)
        F = 176
        E = 16
        K = 2
        CAP_FACTOR = 1.25

        def _mlp(h, wg, wu, wd):
            return jax.nn.silu(h @ wg) * (h @ wu) @ wd
        key = jax.random.key(seed)
        ks = jax.random.split(key, 10)
        sd = 0.02
        return {'x': jax.random.normal(ks[0], (B, S, D), jnp.float32), 'router_w': jax.random.normal(ks[1], (D, E), jnp.float32) * sd, 'router_b': jnp.zeros((E,), jnp.float32), 'w_gate': jax.random.normal(ks[2], (E, D, F), jnp.float32) * sd, 'w_up': jax.random.normal(ks[3], (E, D, F), jnp.float32) * sd, 'w_down': jax.random.normal(ks[4], (E, F, D), jnp.float32) * sd, 'sw_gate': jax.random.normal(ks[5], (D, F), jnp.float32) * sd, 'sw_up': jax.random.normal(ks[6], (D, F), jnp.float32) * sd, 'sw_down': jax.random.normal(ks[7], (F, D), jnp.float32) * sd}
    _L1_ffn_in = _L1_ffn_setup()
    _d = {'L0_attn_x': _L0_attn_in['x'], 'L0_attn_Wq': _L0_attn_in['Wq'], 'L0_attn_Wk': _L0_attn_in['Wk'], 'L0_attn_Wv': _L0_attn_in['Wv'], 'L0_attn_Wo': _L0_attn_in['Wo'], 'L0_attn_lambda_q1': _L0_attn_in['lambda_q1'], 'L0_attn_lambda_k1': _L0_attn_in['lambda_k1'], 'L0_attn_lambda_q2': _L0_attn_in['lambda_q2'], 'L0_attn_lambda_k2': _L0_attn_in['lambda_k2'], 'L0_attn_subln_g': _L0_attn_in['subln_g'], 'L0_ffn_ln_w': _L0_ffn_in['ln_w'], 'L0_ffn_Wg': _L0_ffn_in['Wg'], 'L0_ffn_bg': _L0_ffn_in['bg'], 'L0_ffn_W1a': _L0_ffn_in['W1a'], 'L0_ffn_b1a': _L0_ffn_in['b1a'], 'L0_ffn_W1b': _L0_ffn_in['W1b'], 'L0_ffn_b1b': _L0_ffn_in['b1b'], 'L0_ffn_W2': _L0_ffn_in['W2'], 'L0_ffn_b2': _L0_ffn_in['b2'], 'L1_attn_attention_mask': _L1_attn_in['attention_mask'], 'L1_attn_ln_attn_g': _L1_attn_in['ln_attn_g'], 'L1_attn_ln_attn_b': _L1_attn_in['ln_attn_b'], 'L1_attn_Wq': _L1_attn_in['Wq'], 'L1_attn_bq': _L1_attn_in['bq'], 'L1_attn_Wk': _L1_attn_in['Wk'], 'L1_attn_bk': _L1_attn_in['bk'], 'L1_attn_Wv': _L1_attn_in['Wv'], 'L1_attn_bv': _L1_attn_in['bv'], 'L1_attn_ln_conv_g': _L1_attn_in['ln_conv_g'], 'L1_attn_ln_conv_b': _L1_attn_in['ln_conv_b'], 'L1_attn_conv_w': _L1_attn_in['conv_w'], 'L1_attn_conv_b': _L1_attn_in['conv_b'], 'L1_attn_ln_boom_g': _L1_attn_in['ln_boom_g'], 'L1_attn_ln_boom_b': _L1_attn_in['ln_boom_b'], 'L1_attn_Wb': _L1_attn_in['Wb'], 'L1_attn_bb': _L1_attn_in['bb'], 'L1_attn_Wu': _L1_attn_in['Wu'], 'L1_attn_bu': _L1_attn_in['bu'], 'L1_ffn_router_w': _L1_ffn_in['router_w'], 'L1_ffn_router_b': _L1_ffn_in['router_b'], 'L1_ffn_w_gate': _L1_ffn_in['w_gate'], 'L1_ffn_w_up': _L1_ffn_in['w_up'], 'L1_ffn_w_down': _L1_ffn_in['w_down'], 'L1_ffn_sw_gate': _L1_ffn_in['sw_gate'], 'L1_ffn_sw_up': _L1_ffn_in['sw_up'], 'L1_ffn_sw_down': _L1_ffn_in['sw_down']}
    _x0 = _d['L0_attn_x']
    _d['L0_attn_x'] = jax.random.normal(jax.random.fold_in(jax.random.key(seed), 1), (2, 1024, 128), dtype=_x0.dtype)
    del _x0
    return _d

def reference(L0_attn_x, L0_attn_Wq, L0_attn_Wk, L0_attn_Wv, L0_attn_Wo, L0_attn_lambda_q1, L0_attn_lambda_k1, L0_attn_lambda_q2, L0_attn_lambda_k2, L0_attn_subln_g, L0_ffn_ln_w, L0_ffn_Wg, L0_ffn_bg, L0_ffn_W1a, L0_ffn_b1a, L0_ffn_W1b, L0_ffn_b1b, L0_ffn_W2, L0_ffn_b2, L1_attn_attention_mask, L1_attn_ln_attn_g, L1_attn_ln_attn_b, L1_attn_Wq, L1_attn_bq, L1_attn_Wk, L1_attn_bk, L1_attn_Wv, L1_attn_bv, L1_attn_ln_conv_g, L1_attn_ln_conv_b, L1_attn_conv_w, L1_attn_conv_b, L1_attn_ln_boom_g, L1_attn_ln_boom_b, L1_attn_Wb, L1_attn_bb, L1_attn_Wu, L1_attn_bu, L1_ffn_router_w, L1_ffn_router_b, L1_ffn_w_gate, L1_ffn_w_up, L1_ffn_w_down, L1_ffn_sw_gate, L1_ffn_sw_up, L1_ffn_sw_down):

    def _L0_attn_ref(x, Wq, Wk, Wv, Wo, lambda_q1, lambda_k1, lambda_q2, lambda_k2, subln_g):
        import jax, jax.numpy as jnp
        import numpy as np
        import math
        EMBED_DIM = 128
        NUM_HEADS = 16
        NUM_KV_HEADS = 16
        DEPTH = 12
        HEAD_DIM = EMBED_DIM // NUM_HEADS // 2
        LAMBDA_INIT = 0.8 - 0.6 * math.exp(-0.3 * DEPTH)
        EPS = 1e-05
        THETA = 0.0001

        def rope(q):
            b, s, h, d = q.shape
            pos = jnp.arange(s, dtype=jnp.float32)[:, None]
            freq = 1.0 / THETA ** (2.0 * jnp.arange(d // 2, dtype=jnp.float32) / d)
            ang = pos * freq
            cos = jnp.cos(ang)[None, :, None, :].astype(q.dtype)
            sin = jnp.sin(ang)[None, :, None, :].astype(q.dtype)
            qr = q.reshape(b, s, h, d // 2, 2)
            q0, q1 = (qr[..., 0], qr[..., 1])
            out = jnp.stack([q0 * cos - q1 * sin, q0 * sin + q1 * cos], axis=-1)
            return out.reshape(q.shape)
        b, s, d = x.shape
        H, hd = (NUM_HEADS, HEAD_DIM)
        scaling = hd ** (-0.5)
        q = (x @ Wq).reshape(b, s, 2 * H, hd)
        k = (x @ Wk).reshape(b, s, 2 * NUM_KV_HEADS, hd)
        v = (x @ Wv).reshape(b, s, NUM_KV_HEADS, 2 * hd)
        q = rope(q).transpose(0, 2, 1, 3) * scaling
        k = rope(k).transpose(0, 2, 1, 3)
        v = v.transpose(0, 2, 1, 3)
        scores = jnp.einsum('bhqd,bhkd->bhqk', q, k)
        probs = jax.nn.softmax(scores.astype(jnp.float32), axis=-1).astype(scores.dtype)
        lam1 = jnp.exp(jnp.sum(lambda_q1 * lambda_k1))
        lam2 = jnp.exp(jnp.sum(lambda_q2 * lambda_k2))
        lam = (lam1 - lam2 + LAMBDA_INIT).astype(q.dtype)
        probs = probs.reshape(b, H, 2, s, s)
        w = probs[:, :, 0] - lam * probs[:, :, 1]
        attn = jnp.einsum('bhqk,bhkd->bhqd', w, v)
        rms = jax.lax.rsqrt(jnp.mean(attn * attn, axis=-1, keepdims=True) + EPS)
        attn = attn * rms * subln_g
        attn = attn * (1.0 - LAMBDA_INIT)
        attn = attn.transpose(0, 2, 1, 3).reshape(b, s, H * 2 * hd)
        return attn @ Wo

    def _L0_ffn_ref(x, ln_w, Wg, bg, W1a, b1a, W1b, b1b, W2, b2):
        import jax, jax.numpy as jnp
        import numpy as np
        E = 8
        K = 2
        B, S, D = x.shape
        eps = jnp.finfo(x.dtype).eps
        xn = x * jax.lax.rsqrt(jnp.mean(x * x, axis=-1, keepdims=True) + eps) * ln_w
        logits = xn @ Wg + bg
        vals, idx = jax.lax.top_k(logits, K)
        topk_w = jax.nn.softmax(vals, axis=-1)
        we = jnp.sum(jax.nn.one_hot(idx, E, dtype=x.dtype) * topk_w[..., None], axis=-2)
        T = B * S
        xf = xn.reshape(T, D)
        wef = we.reshape(T, E).T

        def step(acc, params):
            W1a_e, b1a_e, W1b_e, b1b_e, W2_e, b2_e, w_e = params
            a = xf @ W1a_e + b1a_e
            b = xf @ W1b_e + b1b_e
            y = jax.nn.silu(a) * b @ W2_e + b2_e
            return (acc + w_e[:, None] * y, None)
        out0 = jnp.zeros_like(xf)
        out, _ = jax.lax.scan(step, out0, (W1a, b1a, W1b, b1b, W2, b2, wef))
        return out.reshape(B, S, D)

    def _L1_attn_ref(hidden_states, attention_mask, ln_attn_g, ln_attn_b, Wq, bq, Wk, bk, Wv, bv, ln_conv_g, ln_conv_b, conv_w, conv_b, ln_boom_g, ln_boom_b, Wb, bb, Wu, bu):
        import jax, jax.numpy as jnp
        import numpy as np
        EPS = 1e-05

        def _ln(x, g, b):
            m = jnp.mean(x, axis=-1, keepdims=True)
            v = jnp.mean((x - m) ** 2, axis=-1, keepdims=True)
            return (x - m) * jax.lax.rsqrt(v + EPS) * g + b

        def _forward(x, ln_attn_g, ln_attn_b, Wq, bq, Wk, bk, Wv, bv, ln_conv_g, ln_conv_b, conv_w, conv_b, ln_boom_g, ln_boom_b, Wb, bb, Wu, bu):
            B, S, D = x.shape
            K = conv_w.shape[-1]
            G = D // conv_w.shape[1]
            h = _ln(x, ln_conv_g, ln_conv_b)
            hc = jnp.transpose(h, (0, 2, 1))
            hc = jnp.pad(hc, ((0, 0), (0, 0), (K - 1, 0)))
            conv = jax.lax.conv_general_dilated(hc, conv_w, window_strides=(1,), padding='VALID', dimension_numbers=('NCH', 'OIH', 'NCH'), feature_group_count=G)
            conv = conv + conv_b[None, :, None]
            x = x + jnp.transpose(conv, (0, 2, 1))
            h = _ln(x, ln_attn_g, ln_attn_b)
            q = jnp.einsum('bsd,ed->bse', h, Wq) + bq
            k = jnp.einsum('bsd,ed->bse', h, Wk) + bk
            v = jnp.einsum('bsd,ed->bse', h, Wv) + bv
            scale = jnp.arange(1, S + 1, dtype=x.dtype)[None, :, None]
            pooled_q = jnp.cumsum(q, axis=1) / scale
            pooled_k = jnp.cumsum(pooled_q * k, axis=1) / scale
            x = x + pooled_k * v
            h = _ln(x, ln_boom_g, ln_boom_b)
            h = jax.nn.gelu(jnp.einsum('bsd,ed->bse', h, Wb) + bb, approximate=False)
            h = jnp.einsum('bse,de->bsd', h, Wu) + bu
            return x + h
        return _forward(hidden_states, ln_attn_g, ln_attn_b, Wq, bq, Wk, bk, Wv, bv, ln_conv_g, ln_conv_b, conv_w, conv_b, ln_boom_g, ln_boom_b, Wb, bb, Wu, bu)

    def _L1_ffn_ref(x, router_w, router_b, w_gate, w_up, w_down, sw_gate, sw_up, sw_down):
        import jax, jax.numpy as jnp
        import numpy as np
        B, S, D = (1, 256, 128)
        F = 176
        E = 16
        K = 2
        CAP_FACTOR = 1.25

        def _mlp(h, wg, wu, wd):
            return jax.nn.silu(h @ wg) * (h @ wu) @ wd
        b, s, d = x.shape
        N = b * s
        NK = N * K
        C = int(np.ceil(CAP_FACTOR * NK / E))
        x_tokens = x.reshape(N, d)
        logits = x_tokens @ router_w + router_b
        probs = jax.nn.softmax(logits, axis=-1)
        vals, idx = jax.lax.top_k(probs, K)
        vals = vals / (jnp.sum(vals, axis=-1, keepdims=True) + 1e-09)
        idx_flat = idx.reshape(NK)
        vals_flat = vals.reshape(NK)
        oh_e = jax.nn.one_hot(idx_flat, E, dtype=x.dtype)
        pos = (jnp.cumsum(oh_e, axis=0) * oh_e).sum(axis=1) - 1
        within = (pos < C).astype(x.dtype)
        pos_c = jnp.clip(pos, 0, C - 1).astype(jnp.int32)
        token_ids = jnp.arange(NK) // K
        x_pair = x_tokens[token_ids] * within[:, None]
        expert_inputs = jnp.zeros((E, C, d), x.dtype).at[idx_flat, pos_c].add(x_pair)
        expert_outputs = jax.vmap(_mlp)(expert_inputs, w_gate, w_up, w_down)
        gathered = expert_outputs[idx_flat, pos_c] * (vals_flat * within)[:, None]
        output_tokens = gathered.reshape(N, K, d).sum(axis=1)
        return x + _mlp(x, sw_gate, sw_up, sw_down) + output_tokens.reshape(b, s, d)
    x = L0_attn_x
    x = _layernorm(x + _L0_attn_ref(x, L0_attn_Wq, L0_attn_Wk, L0_attn_Wv, L0_attn_Wo, L0_attn_lambda_q1, L0_attn_lambda_k1, L0_attn_lambda_q2, L0_attn_lambda_k2, L0_attn_subln_g), axis=-1)
    x = _layernorm(x + _L0_ffn_ref(x, L0_ffn_ln_w, L0_ffn_Wg, L0_ffn_bg, L0_ffn_W1a, L0_ffn_b1a, L0_ffn_W1b, L0_ffn_b1b, L0_ffn_W2, L0_ffn_b2), axis=-1)
    x = _layernorm(x + _L1_attn_ref(x, L1_attn_attention_mask, L1_attn_ln_attn_g, L1_attn_ln_attn_b, L1_attn_Wq, L1_attn_bq, L1_attn_Wk, L1_attn_bk, L1_attn_Wv, L1_attn_bv, L1_attn_ln_conv_g, L1_attn_ln_conv_b, L1_attn_conv_w, L1_attn_conv_b, L1_attn_ln_boom_g, L1_attn_ln_boom_b, L1_attn_Wb, L1_attn_bb, L1_attn_Wu, L1_attn_bu), axis=-1)
    x = _layernorm(x + _L1_ffn_ref(x, L1_ffn_router_w, L1_ffn_router_b, L1_ffn_w_gate, L1_ffn_w_up, L1_ffn_w_down, L1_ffn_sw_gate, L1_ffn_sw_up, L1_ffn_sw_down), axis=-1)
    return x

_drawn_inputs = setup_inputs


def setup_inputs(seed=0):
    import zlib

    import numpy as np

    out = dict(_drawn_inputs(seed))
    spreads = {'L0_attn_subln_g': (1.0, 0.2),
     'L0_ffn_ln_w': (1.0, 0.2),
     'L0_ffn_bg': (0.0, 0.1),
     'L0_ffn_b1a': (0.0, 0.1),
     'L0_ffn_b1b': (0.0, 0.1),
     'L0_ffn_b2': (0.0, 0.1),
     'L1_attn_ln_attn_g': (1.0, 0.6),
     'L1_attn_ln_attn_b': (0.0, 0.8),
     'L1_attn_bq': (0.0, 0.8),
     'L1_attn_bk': (0.0, 0.8),
     'L1_attn_bv': (0.0, 0.8),
     'L1_attn_ln_conv_g': (1.0, 0.6),
     'L1_attn_ln_conv_b': (0.0, 0.784),
     'L1_attn_conv_b': (0.0, 0.1),
     'L1_attn_ln_boom_g': (1.0, 0.6),
     'L1_attn_ln_boom_b': (0.0, 0.8),
     'L1_attn_bb': (0.0, 0.652),
     'L1_attn_bu': (0.0, 0.1),
     'L1_ffn_router_b': (0.0, 0.8)}
    factors = {'L0_attn_lambda_q1': 4.803,
     'L0_attn_lambda_k1': 4.803,
     'L0_attn_lambda_q2': 3.1,
     'L0_attn_lambda_k2': 3.1,
     'L1_attn_Wq': 8.0,
     'L1_attn_Wk': 8.0,
     'L1_attn_Wv': 8.0,
     'L1_ffn_router_w': 8.0,
     'L1_ffn_w_gate': 8.0,
     'L1_ffn_w_up': 8.0,
     'L1_ffn_w_down': 8.0,
     'L1_ffn_sw_gate': 8.0,
     'L1_ffn_sw_up': 8.0,
     'L1_ffn_sw_down': 8.0}
    for name, (base, spread) in spreads.items():
        noise = np.random.default_rng([zlib.crc32(name.encode()), seed]).standard_normal(out[name].shape)
        drawn = base * np.exp(spread * noise) if base else spread * noise
        out[name] = jnp.asarray(drawn.astype(out[name].dtype))
    for name, factor in factors.items():
        out[name] = (out[name] * factor).astype(out[name].dtype)
    return out
```

```python
import math
from contextlib import ExitStack

import concourse.bass as bass
from concourse import mybir

F32 = mybir.dt.float32
BF16 = mybir.dt.bfloat16
I32 = mybir.dt.int32
U32 = mybir.dt.uint32
ALU = mybir.AluOpType
ACT = mybir.ActivationFunctionType
AX = mybir.AxisListType.X

P = 128
NB, S = 2, 1024
N = NB * S
NT = N // P
QT = S // P
C = 512
NC = N // C
TPC = C // P

NH, HD = 16, 4
VD = 2 * HD + 1
NG = NB * 8
GB = 3
RH = 32
PAIRS_Q = (0, 0, 0, 1, 1, 2)
PAIRS_K = (0, 1, 2, 0, 1, 0)
EPS = 1e-5
LAMBDA_INIT = 0.8 - 0.6 * math.exp(-0.3 * 12)
FAR = 1 << 20
EPS_FFN = 1.1920928955078125e-07
OUT_POS = 5
CREDIT = 3
STEPS = 16
MAX_PER_STEP = (3, 2, 2, 2, 3, 2, 2, 2, 3, 2, 2, 2, 3, 2, 0, 0)
OUT_STEP = 2

E0, F0 = 8, 512
E1, F1 = 16, 176
F1B = F1 - P
CAP = 320
SLOTS = E1 * CAP
CAPT = (CAP + P - 1) // P
CAPR = CAP - (CAPT - 1) * P

R_B1A, R_B1B, R_BB, R_BQKV = 0, 4 * E0, 8 * E0, 8 * E0 + 4
R_GB = R_BQKV + 3
R_LNW, R_SUBLN = R_GB + 6, R_GB + 7
R_N = R_SUBLN + 1
IN_V = 16 * (4 + 1 + 2 + 1 + 10)


def build(nc, a, out):
    with ExitStack() as ctx:
        program(nc, ctx, a, out)


def program(nc, ctx, a, out):
    def sb(name, shape, dt=F32):
        return ctx.enter_context(nc.sbuf_tensor(name, shape, dt))

    def sem(name):
        return ctx.enter_context(nc.semaphore(name))

    ident = sb("ident", [P, P])
    identb = sb("identb", [P, P], BF16)
    eps5 = sb("eps5", [P, 1])
    epsf = sb("epsf", [P, 1])
    X = sb("X", [P, NT, P])
    XS = sb("XS", [P, NT, P])
    XT = sb("XT", [P, N])
    TMP = sb("TMP", [P, N])
    stats = sb("stats", [P, NT, 6])
    mv = sb("mv", [P, NT, 2])
    std = sb("std", [P, NT])
    rstd = sb("rstd", [P, NT])
    wqkv = sb("wqkv", [P, 4, P])
    lamv = sb("lamv", [P, 4, HD])
    lamp = sb("lamp", [P, 2, HD])
    lams = sb("lams", [P, 8])
    gfac = sb("gfac", [P, 1])
    VR = sb("VR", [R_N, P])
    VC = sb("VC", [P, R_N])
    wo = sb("wo", [P, P])

    wg0 = sb("wg0", [P, E0])
    bg0 = sb("bg0", [P, E0])
    b2 = sb("b2", [E0, P])
    rev0 = sb("rev0", [P, E0])
    cw = sb("cw", [P, 32, 4])
    w3 = sb("w3", [P, 3, P])
    wb = sb("wb", [P, 4, P])
    wu = sb("wu", [P, 4, P])
    rows = sb("rows", [P, 2, P])
    rw = sb("rw", [P, E1])
    rbb = sb("rbb", [P, E1])
    rev1 = sb("rev1", [P, E1])
    base1 = sb("base1", [P, E1])
    seg = sb("seg", [P, E1 * NT])
    ltri = sb("ltri", [P, P])
    ltrib = sb("ltrib", [P, P], BF16)
    swg = sb("swg", [P, 2, F1])
    swd = sb("swd", [P, 2, P])

    with ExitStack() as first:
        def sa(name, shape, dt=F32):
            return first.enter_context(nc.sbuf_tensor(name, shape, dt))

        wq2 = sa("wq2", [P, 4, P])
        cosT = sa("cosT", [P, S])
        sinT = sa("sinT", [P, S])
        ra = sa("ra", [P, 2, C])
        rb = sa("rb", [P, 2, C])
        parts = sa("parts", [P, 2, 3, N], BF16)
        ones_rows = sa("ones_rows", [NG * 4, 2, S], BF16)
        KM = [sa(f"KM{u}", [P, 4, S], BF16) for u in range(GB)]
        QG = [sa(f"QG{u}", [P, S], BF16) for u in range(GB)]
        Q2 = [sa(f"Q2{u}", [P, S], BF16) for u in range(GB)]
        VG = [sa(f"VG{u}", [P, QT, 2, VD]) for u in range(GB)]
        V = sa("V", [P, QT, NB * NH, VD])
        E = [sa(f"E{u}", [P, 4, C]) for u in range(3)]
        mx = [sa(f"mx{u}", [P, QT, 4]) for u in range(GB)]
        TM = sa("TM", [P, QT, 4, RH], BF16)
        PVs = sa("PVs", [P, S])
        OT = sa("OT", [P, QT, NG + 1, 4, VD])
        rden = sa("rden", [P, QT * NG * 4])
        NRM = parts[:].rearrange("p w t n -> p (w t n)").bitcast(F32)[:, 0:QT * NG * 4 * 2 * HD]

    L0 = sb("L0", [P, NT, E0])
    La = sb("La", [P, NT, E1])
    Lb = sb("Lb", [P, NT, E1])
    oh = sb("oh", [P, 2, NT, E1])
    top = sb("top", [P, 8, NT])
    WE = sb("WE", [P, NT, E0])
    WET = sb("WET", [E0, N])
    WEc = sb("WEc", [P, 2, NT])
    B1c = sb("B1c", [P, 2, 4])
    w1a = sb("w1a", [P, 2, F0])
    w1b = sb("w1b", [P, 2, F0])
    w2 = sb("w2", [P, 2, 4, P])
    gs = sb("gs", [P, 2, C])
    G = sb("G", [P, 2, 4, C])
    HT = sb("HT", [P, NB, S + 3])
    QF = sb("QF", [P, N])
    KF = sb("KF", [P, N])
    VF = sb("VF", [P, N])
    X0 = sb("X0", [P, NT, P])
    cwm = sb("cwm", [P, 4, P])
    cwt = sb("cwt", [P, 4, P])
    w3t = sb("w3t", [P, 3, P])
    wbt = sb("wbt", [P, 4, P])
    wut = sb("wut", [P, 4, P])
    invp = sb("invp", [P, S])
    onesS = sb("onesS", [P, S])
    onesb = sb("onesb", [P, P], BF16)
    selb = sb("selb", [P, E1, NT], BF16)
    cumb = sb("cumb", [P, E1, NT], BF16)
    self_ = sb("self_", [P, E1, NT])
    cumf = sb("cumf", [P, E1, NT])
    posx = sb("posx", [P, 3, NT, E1])
    prod = sb("prod", [P, NT, E1])
    idx = sb("idx", [P, 2, NT, 2], I32)
    fidx = sb("fidx", [P, 6, NT])
    wts = sb("wts", [P, 2, NT])
    wg1 = sb("wg1", [P, 2, 2, F1])
    wd1 = sb("wd1", [P, 2, 2, P])
    XE = sb("XE", [P, 2, CAPT, P])
    XET = sb("XET", [P, 2, CAP])
    HS = sb("HS", [P, 2, C])
    H = sb("H", [P, 2, 2, C])
    YE = sb("YE", [P, 2, CAPT, P])
    YG = sb("YG", [P, NT, 2, P])
    zero_rows = sb("zero_rows", [P, SLOTS // P // 5 * P])

    SM = [ctx.enter_context(nc.psum_tensor(f"SM{i}", [P, 2 * C], F32)) for i in range(2)]
    ST = [ctx.enter_context(nc.psum_tensor(f"ST{i}", [P, C], F32)) for i in range(3)]
    PV = ctx.enter_context(nc.psum_tensor("PVp", [P, C], F32))
    BK = [SM[0][:, 0:C], SM[0][:, C:2 * C], SM[1][:, 0:C], SM[1][:, C:2 * C],
          ST[0][:, :], ST[1][:, :], ST[2][:, :], PV[:, :]]

    qrows = nc.dram_tensor("qrows", [NG, 4, RH, S], BF16, kind="Internal").ap()
    krows = nc.dram_tensor("krows", [NG, 4, RH, S], BF16, kind="Internal").ap()
    xslots = nc.dram_tensor("xslots", [SLOTS, P], F32, kind="Internal").ap()
    yslots = nc.dram_tensor("yslots", [SLOTS, P], F32, kind="Internal").ap()

    in_x, in_w, in_tab, in_v, in_ffn, in_mix, in_moe = (sem(n) for n in (
        "in_x", "in_w", "in_tab", "in_v", "in_ffn", "in_mix", "in_moe"))
    const_set = sem("const_set")
    dve_step = sem("dve_step")
    act_step = sem("act_step")
    vec_ready, vec_copied = sem("vec_ready"), sem("vec_copied")
    xT_ready, xT_copied = sem("xT_ready"), sem("xT_copied")
    w2_ready = sem("w2_ready")
    qk_ready, qk_taken = sem("qk_ready"), sem("qk_taken")
    v_ready, v_copied = sem("v_ready"), sem("v_copied")
    parts_ready = sem("parts_ready")
    rows_stored = sem("rows_stored")
    pads_stored = sem("pads_stored")
    kq_loaded = [sem(f"kq_loaded{u}") for u in range(GB)]
    vg_ready = sem("vg_ready")
    s_ready, s_taken = sem("s_ready"), sem("s_taken")
    m_hi, tm_ready, q2_ready = sem("m_hi"), sem("tm_ready"), sem("q2_ready")
    st_ready, exp_done = sem("st_ready"), sem("exp_done")
    pv_step, pv_evac, group_done = sem("pv_step"), sem("pv_evac"), sem("group_done")
    lam_sum, lam_exp, lam_ready = sem("lam_sum"), sem("lam_exp"), sem("lam_ready")
    var_ready, std_ready = sem("var_ready"), sem("std_ready")
    tok_ready = sem("tok_ready")
    tr_ready, tr_taken = sem("tr_ready"), sem("tr_taken")
    mo_ready, mo_taken = sem("mo_ready"), sem("mo_taken")
    fm_ready = sem("fm_ready")
    r0_ready, r0_exp, we_ready = sem("r0_ready"), sem("r0_exp"), sem("we_ready")
    top_diff = sem("top_diff")
    wet_ready, wet_taken = sem("wet_ready"), sem("wet_taken")
    w0_loaded = [sem(f"w0_loaded{u}") for u in range(2)]
    wec_ready = sem("wec_ready")
    ab_ready, silu_done, g_done = sem("ab_ready"), sem("silu_done"), sem("g_done")
    y_ready, acc_done, e0_done = sem("y_ready"), sem("acc_done"), sem("e0_done")
    tw_ready, tw_taken = sem("tw_ready"), sem("tw_taken")
    cwm_ready = sem("cwm_ready")
    up_ready, gelu_done = sem("up_ready"), sem("gelu_done")
    lg_ready, prob_exp, prob_sub = sem("lg_ready"), sem("prob_exp"), sem("prob_sub")
    sel_ready, pos_ready = sem("sel_ready"), sem("pos_ready")
    idx_ready, scattered, zeroed = sem("idx_ready"), sem("scattered"), sem("zeroed")
    w1_loaded = [sem(f"w1_loaded{u}") for u in range(2)]
    xe_ready, xe_taken = sem("xe_ready"), sem("xe_taken")
    qkv_ready, qkv_taken, pool_done = sem("qkv_ready"), sem("qkv_taken"), sem("pool_done")
    gu_ready, h_silu, h_done = sem("gu_ready"), sem("h_silu"), sem("h_done")
    ye_ready, ye_taken = sem("ye_ready"), sem("ye_taken")
    y_stored = [sem(f"y_stored{u}") for u in range(2)]
    gathered, result_ready, stored = sem("gathered"), sem("result_ready"), sem("stored")

    block = ctx.enter_context(nc.Block())

    class Chain:

        def __init__(self, eng, s):
            self.eng, self.s, self.n = eng, s, 0

        def __call__(self, ins):
            self.n += 1
            ins.then_inc(self.s, 1)
            self.eng.wait_ge(self.s, self.n)

    def use(g, pos):
        return 33 + 34 * g + pos

    @block.sync
    def _(sp):
        for t in range(0, NT, 4):
            sp.dma_start(X[:, t:t + 4, :],
                         a["x"].rearrange("b (t p) d -> p (b t) d", p=P)[:, t:t + 4, :]).then_inc(in_x, 16)
        sp.dma_start(ident[:], a["ident"]).then_inc(in_x, 16)
        for j, n in enumerate(("Wq", "Wk", "Wv", "Wo")):
            sp.dma_start(wqkv[:, j, :], a[n]).then_inc(in_w, 16)
        sp.dma_start(cosT[:], a["cos"]).then_inc(in_tab, 16)
        sp.dma_start(sinT[:], a["sin"]).then_inc(in_tab, 16)
        for j, n in enumerate(("lq1", "lk1", "lq2", "lk2")):
            sp.dma_start(lamv[:, j, :], a[n].partition_broadcast(P)).then_inc(in_v, 16)
        sp.dma_start(VR[R_SUBLN:R_SUBLN + 1, :].rearrange("o (h d) -> o h d", h=NH),
                     a["subln_g"].partition_broadcast(NH).unsqueeze(0)).then_inc(in_v, 16)
        for r, n in ((R_B1A, "b1a"), (R_B1B, "b1b")):
            sp.dma_start(VR[r:r + 4 * E0, :], a[n].rearrange("e (f p) -> (e f) p", p=P)).then_inc(in_v, 16)
        sp.dma_start(VR[R_BB:R_BB + 4, :], a["bb"].rearrange("(f p) -> f p", p=P)).then_inc(in_v, 16)
        for r, n in ((R_BQKV, "bq"), (R_BQKV + 1, "bk"), (R_BQKV + 2, "bv"), (R_GB, "ln_conv_g"),
                     (R_GB + 1, "ln_conv_b"), (R_GB + 2, "ln_attn_g"), (R_GB + 3, "ln_attn_b"),
                     (R_GB + 4, "ln_boom_g"), (R_GB + 5, "ln_boom_b"), (R_LNW, "ln_w")):
            sp.dma_start(VR[r:r + 1, :], a[n].unsqueeze(0)).then_inc(in_v, 16)

        sp.wait_ge(const_set, 2)
        for rws, dst in ((2, qrows), (0, krows)):
            if rws:
                sp.dma_start(dst.rearrange("g a r t -> (g a) r t")[:, 0:2, :],
                             KM[0][0:64, 0:2, :]).then_inc(pads_stored, 16)
            else:
                sp.dma_start(dst.rearrange("g a r t -> (g a) r t")[:, 0:2, :], ones_rows[:]).then_inc(pads_stored, 16)
            for lo in (26, 29):
                sp.dma_start(dst.rearrange("g a r t -> (g a) r t")[:, lo:lo + 3, :],
                             KM[0][0:64, 0:3, :]).then_inc(pads_stored, 16)

        def store_rows(b):
            sp.wait_ge(parts_ready, 4 * (b + 1))
            for dst, which, table in ((qrows, 0, PAIRS_Q), (krows, 1, PAIRS_K)):
                for p, part in enumerate(table):
                    for aa in range(4):
                        sp.dma_start(dst[8 * b:8 * b + 8, aa, 2 + HD * p:2 + HD * (p + 1), :],
                                     parts[32 * aa:32 * aa + 32, which, part, S * b:S * (b + 1)])\
                            .then_inc(rows_stored, 16)

        def load_group(u, g):
            sp.dma_start(QG[u][:], qrows[bass.ds(g, 1)].rearrange("g a r t -> (g a r) t")).then_inc(kq_loaded[u], 16)
            for aa in range(4):
                sp.dma_start(KM[u][RH * aa:RH * (aa + 1), aa, :],
                             krows[bass.ds(g, 1), aa].rearrange("g r t -> (g r) t")).then_inc(kq_loaded[u], 16)

        store_rows(0)
        sp.wait_ge(pads_stored, 6 * 16)
        sp.wait_ge(rows_stored, 48 * 16)
        for g in range(GB):
            load_group(g, g)
        store_rows(1)
        sp.wait_ge(rows_stored, 96 * 16)

        sp.dma_start(wg0[:], a["Wg"]).then_inc(in_ffn, 16)
        sp.dma_start(bg0[:], a["bg"].partition_broadcast(P)).then_inc(in_ffn, 16)
        sp.dma_start(rev0[:], a["rev0"].partition_broadcast(P)).then_inc(in_ffn, 16)
        sp.dma_start(b2[:], a["b2"]).then_inc(in_ffn, 16)
        sp.dma_start(cw[:], a["conv_w"]).then_inc(in_mix, 16)
        for j, n in enumerate(("mWq", "mWk", "mWv")):
            sp.dma_start(w3[:, j, :], a[n]).then_inc(in_mix, 16)
        sp.dma_start(wb[:], a["Wb"].rearrange("(f p) d -> p f d", p=P)).then_inc(in_mix, 16)
        sp.dma_start(wu[:], a["Wu"].rearrange("d (f p) -> d f p", p=P)).then_inc(in_mix, 16)
        sp.dma_start(rows[:, 0, :], a["conv_b"].partition_broadcast(P)).then_inc(in_mix, 16)
        sp.dma_start(rows[:, 1, :], a["bu"].partition_broadcast(P)).then_inc(in_mix, 16)
        sp.dma_start(rw[:], a["router_w"]).then_inc(in_moe, 16)
        for dst, n in ((rbb[:], "router_b"), (rev1[:], "rev1"), (base1[:], "base1"), (seg[:], "seg")):
            sp.dma_start(dst, a[n].partition_broadcast(P)).then_inc(in_moe, 16)
        sp.dma_start(ltri[:], a["ltri"]).then_inc(in_moe, 16)
        sp.dma_start(swg[:, 0, :], a["sw_gate"]).then_inc(in_moe, 16)
        sp.dma_start(swg[:, 1, :], a["sw_up"]).then_inc(in_moe, 16)
        sp.dma_start(swd[:, 0, :], a["sw_down"][0:P]).then_inc(in_moe, 16)
        sp.dma_start(swd[0:F1B, 1, :], a["sw_down"][P:F1]).then_inc(in_moe, 16)
        for j in range(SLOTS // S):
            sp.dma_start(xslots[S * j:S * (j + 1)].rearrange("(p r) d -> p (r d)", p=P),
                         PVs[:]).then_inc(zeroed, 16)

        with sp.Fori(0, (NG - 1 - GB) // GB) as i:
            for u in range(GB):
                sp.wait_ge(pv_step, (i * GB + u) * STEPS + (STEPS + CREDIT))
                load_group(u, i * GB + (GB + u))
        sp.wait_ge(pv_step, (NG - GB) * STEPS + CREDIT)
        load_group(0, NG - 1)

        sp.wait_ge(tok_ready, NC)
        sp.dma_start(invp[:], a["invp"].partition_broadcast(P)).then_inc(in_mix, 16)

        def load_expert0(u, e):
            sp.dma_start(w1a[:, u, :], a["W1a"][bass.ds(e, 1)].rearrange("e d f -> (e d) f")).then_inc(w0_loaded[u], 16)
            sp.dma_start(w1b[:, u, :], a["W1b"][bass.ds(e, 1)].rearrange("e d f -> (e d) f")).then_inc(w0_loaded[u], 16)
            sp.dma_start(w2[:, u, :, :],
                         a["W2"][bass.ds(e, 1)].rearrange("e (f p) d -> p (e f) d", p=P)).then_inc(w0_loaded[u], 16)

        for u in range(2):
            load_expert0(u, u)
        with sp.Fori(0, E0 // 2 - 1) as i:
            for u in range(2):
                sp.wait_ge(y_ready, 8 * i + (4 * u + 6))
                load_expert0(u, 2 * i + (u + 2))

        sp.wait_ge(scattered, 16 * 2 * NT)

        def load_expert1(u, e):
            sp.dma_start(wg1[:, u, 0, :], a["w_gate"][bass.ds(e, 1)].rearrange("e d f -> (e d) f")).then_inc(w1_loaded[u], 16)
            sp.dma_start(wg1[:, u, 1, :], a["w_up"][bass.ds(e, 1)].rearrange("e d f -> (e d) f")).then_inc(w1_loaded[u], 16)
            wd = a["w_down"][bass.ds(e, 1)].rearrange("e f d -> (e f) d")
            sp.dma_start(wd1[:, u, 0, :], wd[0:P, :]).then_inc(w1_loaded[u], 16)
            sp.dma_start(wd1[0:F1B, u, 1, :], wd[P:F1, :]).then_inc(w1_loaded[u], 16)
            xr = xslots.rearrange("(e c) d -> e c d", e=E1)[bass.ds(e, 1)].rearrange("e c d -> (e c) d")
            sp.dma_start(XE[:, u, 0:2, :], xr[0:2 * P, :].rearrange("(c p) d -> p c d", p=P)).then_inc(w1_loaded[u], 16)
            sp.dma_start(XE[0:CAPR, u, 2, :], xr[2 * P:CAP, :]).then_inc(w1_loaded[u], 16)

        def store_expert1(u, e):
            yr = yslots.rearrange("(e c) d -> e c d", e=E1)[bass.ds(e, 1)].rearrange("e c d -> (e c) d")
            sp.dma_start(yr[0:2 * P, :].rearrange("(c p) d -> p c d", p=P), YE[:, u, 0:2, :]).then_inc(y_stored[u], 16)
            sp.dma_start(yr[2 * P:CAP, :], YE[0:CAPR, u, 2, :]).then_inc(y_stored[u], 16)

        for u in range(2):
            load_expert1(u, u)
        with sp.Fori(0, E1 // 2 - 1) as i:
            for u in range(2):
                sp.wait_ge(ye_ready, 2 * i + (NC + u + 1))
                load_expert1(u, 2 * i + (u + 2))
                sp.wait_ge(ye_taken, 2 * i + (NC + u + 3))
                store_expert1(u, 2 * i + u)
        for u in range(2):
            sp.wait_ge(ye_taken, NC + E1 + 1 + u)
            store_expert1(u, E1 - 2 + u)

        ov = out.rearrange("b (t p) d -> p (b t) d", p=P)
        for t in range(0, NT, 4):
            sp.wait_ge(result_ready, t // 4 + 1)
            sp.dma_start(ov[:, t:t + 4, :], XS[:, t:t + 4, :]).then_inc(stored, 16)
        sp.wait_ge(stored, 16 * NT // 4)

    @block.gpsimd
    def _(pool):
        pool.memset(ones_rows[:], 1.0)
        for u in range(1, GB):
            pool.memset(KM[u][:], 0.0)
        pool.memset(TM[:], 0.0)
        pool.memset(V[:, :, :, 2 * HD:VD], 1.0).then_inc(const_set, 1)
        pool.wait_ge(const_set, 2)
        pool.wait_ge(v_copied, NC)
        for g in range(GB):
            pool.tensor_copy(VG[g][:], V[:, :, 2 * g:2 * g + 2, :]).then_inc(vg_ready, 1)
        with pool.Fori(0, (NG - 1 - GB) // GB) as i:
            for u in range(GB):
                pool.wait_ge(pv_step, (i * GB + u) * STEPS + (STEPS + CREDIT))
                pool.tensor_copy(VG[u][:], V[:, :, bass.ds(2 * (i * GB + (GB + u)), 2), :]).then_inc(vg_ready, 1)
        pool.wait_ge(pv_step, (NG - GB) * STEPS + CREDIT)
        pool.tensor_copy(VG[0][:], V[:, :, 2 * (NG - 1):2 * NG, :]).then_inc(vg_ready, 1)

        pool.wait_ge(we_ready, 1)
        with pool.Fori(0, E0 // 2) as i:
            for u in range(2):
                pool.wait_ge(acc_done, i * 8 + (4 * u + 1))
                pool.tensor_copy(B1c[:, u, :], VC[:, bass.ds(8 * i + (R_B1A + 4 * u), 4)])
                pool.tensor_copy(WEc[:, u, :].unsqueeze(2),
                                 WE[:, :, bass.ds(2 * i + u, 1)]).then_inc(wec_ready, 1)

        pool.wait_ge(zeroed, 16 * (SLOTS // S))
        pool.wait_ge(idx_ready, 1)
        for t in range(NT):
            for k in range(2):
                pool.indirect_dma_start(
                    xslots[:, :], bass.IndirectOffsetOnAxis(ap=idx[:, 0, t, k:k + 1].bitcast(U32), axis=0),
                    X[:, t, :], None, bounds_check=SLOTS - 1, oob_is_err=False).then_inc(scattered, 16)
        for u in range(2):
            pool.wait_ge(y_stored[u], 16 * E1 + 16)
        for t in range(NT):
            for k in range(2):
                pool.indirect_dma_start(
                    YG[:, t, k, :], None, yslots[:, :],
                    bass.IndirectOffsetOnAxis(ap=idx[:, 1, t, k:k + 1].bitcast(U32), axis=0),
                    bounds_check=SLOTS - 1, oob_is_err=False).then_inc(gathered, 16)

    @block.tensor
    def _(pe):
        pe.wait_ge(const_set, 2)
        pe.wait_ge(in_x, 16 * 5)
        for c in range(NC):
            for k in range(TPC):
                ins = pe.transpose(BK[c][:, P * k:P * (k + 1)], X[:, TPC * c + k, :], ident[:])
            ins.then_inc(xT_ready, 1)

        pe.wait_ge(in_v, IN_V)
        pe.transpose(BK[7][:, 0:R_N], VR[:], ident[0:R_N, 0:R_N]).then_inc(vec_ready, 1)

        pe.wait_ge(w2_ready, 1)
        pe.wait_ge(xT_copied, NC)
        pe.wait_ge(vec_copied, 1)
        pe.sem_inc(pv_step, CREDIT)
        for j in range(2 * NC):
            c, w = divmod(j, 2)
            if j >= 4:
                pe.wait_ge(qk_taken, j - 3)
            for y in range(2):
                ins = pe.matmul(BK[2 * (j % 4) + y], wq2[:, 2 * w + y, :], XT[:, C * c:C * (c + 1)],
                                start=True, stop=True)
            ins.then_inc(qk_ready, 1)
        for c in range(NC):
            pe.wait_ge(qk_taken, NC + c + 1)
            for k in range(TPC):
                t = TPC * c + k
                ins = pe.matmul(BK[2 * c][:, P * k:P * (k + 1)], XT[:, P * t:P * (t + 1)], wqkv[:, 2, :],
                                start=True, stop=True)
            ins.then_inc(v_ready, 1)

        def max_scores(v, k, pos, g):
            qt, aa = divmod(k, 4)
            slot = (1 + pos) % 2
            pe.wait_ge(s_taken, use(g, pos) + 1)
            for h in range(2):
                ins = pe.matmul(SM[slot][:, C * h:C * (h + 1)], QG[v][:, P * qt:P * (qt + 1)],
                                KM[v][:, aa, C * h:C * (h + 1)], start=True, stop=True)
            ins.then_inc(s_ready, 1)

        def max_rows(g, pos):
            slot = (1 + pos) % 2
            pe.wait_ge(tm_ready, g + 2)
            pe.wait_ge(s_taken, use(g, pos) + 1)
            for qt in range(QT):
                ins = pe.matmul(SM[slot][:, P * qt:P * (qt + 1)], TM[:, qt, :, :].rearrange("p a r -> p (a r)"),
                                identb[:], start=True, stop=True)
            ins.then_inc(s_ready, 1)

        def turn_outputs(g, pos, phase):
            slot = (1 + pos) % 2
            pe.wait_ge(pv_evac, 2 * g + 1)
            pe.wait_ge(s_taken, use(phase, pos) + 1)
            for qt in range(QT):
                ins = pe.transpose(SM[slot][:, P * qt:P * (qt + 1)], PVs[:, P * qt:P * (qt + 1)], ident[:])
            ins.then_inc(s_ready, 1)

        def group(g, u, round_, last):
            v = (u + 1) % GB
            pos = 0
            if not last:
                pe.wait_ge(kq_loaded[v], 80 * (round_ + (1 if v else 2)))
            k = 0

            def scores(s, aa):
                half, kt = divmod(s, QT)
                pe.wait_ge(exp_done, g * (4 * STEPS) + (4 * s + aa + 1))
                if s == 0 and aa == 0:
                    pe.wait_ge(s_taken, use(g, 0) + 2)
                pe.matmul(ST[(u + s + aa) % 3][:], KM[u][:, aa, P * kt:P * (kt + 1)],
                          Q2[u][:, C * half:C * (half + 1)], start=True, stop=True).then_inc(st_ready, 1)

            def outputs(s):
                half, kt = divmod(s, QT)
                pe.wait_ge(exp_done, g * (4 * STEPS) + (4 * s + 4 + CREDIT))
                if s == 0:
                    pe.wait_ge(vg_ready, g + 1)
                if kt == 0:
                    pe.wait_ge(pv_evac, 2 * g + (1 + half))
                for aa in range(4):
                    ins = pe.matmul(PV[RH * aa:RH * aa + VD, :], VG[u][:, kt, aa // 2, :],
                                    E[(u + s) % 3][:, aa, :], start=(kt == 0), stop=(kt == QT - 1))
                ins.then_inc(pv_step, 1)

            for s in range(STEPS):
                todo = 0 if last else MAX_PER_STEP[s]
                if s == OUT_STEP:
                    turn_outputs(g, pos, g)
                    pos += 1
                scores(s, 0)
                scores(s, 1)
                if todo:
                    max_scores(v, k, pos, g)
                    k, pos, todo = k + 1, pos + 1, todo - 1
                scores(s, 2)
                if s:
                    outputs(s - 1)
                while todo:
                    max_scores(v, k, pos, g)
                    k, pos, todo = k + 1, pos + 1, todo - 1
                scores(s, 3)
            if not last:
                max_rows(g, pos)
            outputs(STEPS - 1)

        pe.wait_ge(kq_loaded[0], 80)
        pe.wait_ge(v_copied, NC)
        for k in range(4 * QT):
            max_scores(0, k, k - 33 + 34, -1)
        max_rows(-1, 4 * QT + 1)
        with pe.Fori(0, (NG - 1) // GB) as i:
            for u in range(GB):
                group(i * GB + u, u, i, False)
        group(NG - 1, 0, None, True)
        turn_outputs(NG, 1, NG - 1)

        def turn(r, tile, bank0=0):
            for c in range(NC):
                pe.wait_ge(tok_ready, NC * r + c + 1)
                for k in range(TPC):
                    ins = pe.transpose(BK[bank0 + c][:, P * k:P * (k + 1)], tile(TPC * c + k), ident[:])
                ins.then_inc(tr_ready, 1)

        turn(0, lambda t: TMP[:, P * (2 * (t % QT) + t // QT):P * (2 * (t % QT) + t // QT + 1)])
        for c in range(NC):
            pe.wait_ge(fm_ready, c + 1)
            for k in range(TPC):
                t = TPC * c + k
                ins = pe.matmul(BK[4 + c][:, P * k:P * (k + 1)], XT[:, P * t:P * (t + 1)], wo[:], start=True, stop=True)
            ins.then_inc(mo_ready, 1)

        turn(1, lambda t: XS[:, t, :])
        pe.wait_ge(in_ffn, 16 * 4)
        pe.wait_ge(fm_ready, 2 * NC)
        for t in range(NT):
            ins = pe.matmul(BK[4][:, E0 * t:E0 * (t + 1)], XT[:, P * t:P * (t + 1)], wg0[:], start=True, stop=True)
        ins.then_inc(r0_ready, 1)
        pe.wait_ge(we_ready, 1)
        for c in range(NC):
            for k in range(TPC):
                ins = pe.transpose(BK[c][0:E0, P * k:P * (k + 1)], WE[:, TPC * c + k, :], ident[:])
            ins.then_inc(wet_ready, 1)
        for c in range(NC):
            pe.wait_ge(wet_taken, c + 1)
            for k in range(TPC):
                t = TPC * c + k
                ins = pe.matmul(BK[4 + c][:, P * k:P * (k + 1)], WET[:, P * t:P * (t + 1)], b2[:], start=True, stop=True)
            ins.then_inc(mo_ready, 1)

        pe.wait_ge(mo_taken, 2 * NC)
        pe.sem_inc(y_ready, 2)
        with pe.Fori(0, E0 // 2) as i:
            def up0(u, c, f):
                j = 16 * u + 4 * c + f
                pe.wait_ge(g_done, i * 32 + (j + 1))
                for y, w in ((0, w1a), (1, w1b)):
                    ins = pe.matmul(BK[2 * (j % 2) + y], w[:, u, P * f:P * (f + 1)], XT[:, C * c:C * (c + 1)],
                                    start=True, stop=True)
                ins.then_inc(ab_ready, 1)

            def down0(n):
                u = n // 4
                pe.wait_ge(g_done, i * 32 + (4 * n + 6))
                pe.wait_ge(acc_done, i * 8 + (n + 4))
                for k in range(TPC):
                    for f in range(4):
                        ins = pe.matmul(BK[4 + n % 2][:, P * k:P * (k + 1)], G[:, n % 2, f, P * k:P * (k + 1)],
                                        w2[:, u, f, :], start=(f == 0), stop=(f == 3))
                ins.then_inc(y_ready, 1)

            for u in range(2):
                pe.wait_ge(w0_loaded[u], 48 * i + 48)
                for c in range(NC):
                    for f in range(4):
                        up0(u, c, f)
                        if f == 1 and (u or c):
                            down0(4 * u + c - 1)
            down0(7)

        pe.wait_ge(in_mix, 16 * 9)
        pe.wait_ge(cwm_ready, 1)
        for bank, src, n in ((4, cwm, 4), (5, w3, 3), (6, wb, 4), (7, wu, 4)):
            if bank < 6:
                pe.wait_ge(acc_done, 32 + 5)
            for j in range(n):
                ins = pe.transpose(BK[bank][:, P * j:P * (j + 1)], src[:, j, :], ident[:])
            ins.then_inc(tw_ready, 1)
        turn(2, lambda t: XS[:, t, :])
        pe.wait_ge(tw_taken, 4)
        pe.wait_ge(fm_ready, 3 * NC)
        for c in range(NC):
            for k in range(TPC):
                t = TPC * c + k
                for tap in range(4):
                    lo = P * (t % QT) + tap
                    ins = pe.matmul(BK[4 + c][:, P * k:P * (k + 1)], HT[:, t // QT, lo:lo + P], cwt[:, tap, :],
                                    start=(tap == 0), stop=(tap == 3))
            ins.then_inc(mo_ready, 1)
        turn(3, lambda t: XS[:, t, :])
        for j in range(3 * NC):
            c, w = divmod(j, 3)
            pe.wait_ge(fm_ready, 3 * NC + c + 1)
            if j >= 4:
                pe.wait_ge(qkv_taken, j - 3)
            else:
                pe.wait_ge(mo_taken, 2 * NC + j + 1)
            pe.matmul(BK[4 + j % 4], w3t[:, w, :], XT[:, C * c:C * (c + 1)], start=True, stop=True).then_inc(qkv_ready, 1)
        for c in range(NC):
            pe.wait_ge(pool_done, c // 2 + 1)
            for k in range(TPC):
                t = TPC * c + k
                ins = pe.transpose(BK[c][:, P * k:P * (k + 1)], QF[:, P * t:P * (t + 1)], ident[:])
            ins.then_inc(mo_ready, 1)
        turn(4, lambda t: XS[:, t, :], 4)
        for c in range(NC):
            pe.wait_ge(fm_ready, 5 * NC)
            for f in range(4):
                j = 4 * c + f
                pe.wait_ge(gelu_done, max(j - 3, 0))
                pe.matmul(BK[j % 4], wbt[:, f, :], XT[:, C * c:C * (c + 1)], start=True, stop=True).then_inc(up_ready, 1)
            pe.wait_ge(gelu_done, 4 * c + 4)
            for k in range(TPC):
                for f in range(4):
                    ins = pe.matmul(BK[4 + c][:, P * k:P * (k + 1)], G[:, c % 2, f, P * k:P * (k + 1)], wut[:, f, :],
                                    start=(f == 0), stop=(f == 3))
            ins.then_inc(mo_ready, 1)

        turn(5, lambda t: X[:, t, :])
        pe.wait_ge(in_moe, 16 * 9)
        pe.wait_ge(fm_ready, 6 * NC)
        for t in range(NT):
            ins = pe.matmul(BK[6][:, E1 * t:E1 * (t + 1)], XT[:, P * t:P * (t + 1)], rw[:], start=True, stop=True)
        ins.then_inc(lg_ready, 1)

        def up1(j, x, n, w):
            pe.wait_ge(h_done, j + 1)
            f = j_f(j)
            M = P if f == 0 else F1B
            for y in range(2):
                ins = pe.matmul(BK[2 * f + y][0:M, 0:n], w[:, y, P * f:P * f + M], x, start=True, stop=True)
            ins.then_inc(gu_ready, 1)

        def down1(n, rows_, w, hb):
            pe.wait_ge(h_done, 2 * n + 4)
            pe.wait_ge(ye_taken, n + 1)
            for k, m in enumerate(rows_):
                for f, K in ((0, P), (1, F1B)):
                    ins = pe.matmul(BK[4 + hb][0:m, P * k:P * (k + 1)], H[0:K, hb, f, P * k:P * k + m],
                                    w(f, K), start=(f == 0), stop=(f == 1))
            ins.then_inc(ye_ready, 1)

        def j_f(j):
            return j % 2

        for c in range(NC):
            for f in range(2):
                up1(2 * c + f, XT[:, C * c:C * (c + 1)], C, swg)
            if c:
                down1(c - 1, [P] * TPC, lambda f, K: swd[0:K, f, :], (c - 1) % 2)
            if c == 1:
                pe.wait_ge(sel_ready, 1)
                pe.matmul(BK[7][:, 0:E1 * NT], ltrib[:], selb[:].rearrange("p e t -> p (e t)"), start=True, stop=False)
                pe.matmul(BK[7][:, 0:E1 * NT], onesb[:], cumb[:].rearrange("p e t -> p (e t)"),
                          start=False, stop=True).then_inc(pos_ready, 1)
        down1(NC - 1, [P] * TPC, lambda f, K: swd[0:K, f, :], (NC - 1) % 2)

        pe.wait_ge(idx_ready, 1)
        with pe.Fori(0, E1 // 2) as i:
            for u in range(2):
                pe.wait_ge(w1_loaded[u], 96 * i + 96)
                for k in range(CAPT):
                    m = P if k < CAPT - 1 else CAPR
                    ins = pe.transpose(BK[6 + u][:, P * k:P * k + m], XE[0:m, u, k, :], ident[0:m, 0:m])
                ins.then_inc(xe_ready, 1)
            for u in range(2):
                pe.wait_ge(xe_taken, 2 * i + (u + 1))
                for f in range(2):
                    M = P if f == 0 else F1B
                    pe.wait_ge(h_done, i * 4 + (2 * NC + 2 * u + f + 1))
                    for y in range(2):
                        ins = pe.matmul(BK[2 * f + y][0:M, 0:CAP], wg1[:, u, y, P * f:P * f + M], XET[:, u, :],
                                        start=True, stop=True)
                    ins.then_inc(gu_ready, 1)
            for u in range(2):
                pe.wait_ge(h_done, i * 4 + (2 * NC + 2 * u + 4))
                pe.wait_ge(ye_taken, i * 2 + (NC + u + 1))
                for k in range(CAPT):
                    m = P if k < CAPT - 1 else CAPR
                    for f, K in ((0, P), (1, F1B)):
                        ins = pe.matmul(BK[4 + u][0:m, P * k:P * (k + 1)], H[0:K, u, f, P * k:P * k + m],
                                        wd1[0:K, u, f, :], start=(f == 0), stop=(f == 1))
                ins.then_inc(ye_ready, 1)

    @block.scalar
    def _(act):
        chain = Chain(act, act_step)
        for c in range(NC):
            act.wait_ge(xT_ready, c + 1)
            act.copy(XT[:, C * c:C * (c + 1)], BK[c]).then_inc(xT_copied, 1)
        act.wait_ge(vec_ready, 1)
        act.copy(VC[:], BK[7][:, 0:R_N]).then_inc(vec_copied, 1)
        act.wait_ge(const_set, 2)
        act.wait_ge(lam_sum, 1)
        act.activation(lams[:, 2:4], lams[:, 0:2], ACT.Exp).then_inc(lam_exp, 1)
        for c in range(NC):
            act.wait_ge(v_ready, c + 1)
            b, kt = c // 2, TPC * (c % 2)
            act.copy(V[:, kt:kt + TPC, NH * b:NH * (b + 1), 0:2 * HD],
                     BK[2 * c].rearrange("p (k h d) -> p k h d", k=TPC, h=NH)).then_inc(v_copied, 1)

        act.wait_ge(zeroed, 16 * (SLOTS // S))
        act.sem_inc(exp_done, CREDIT)
        for u in range(2):
            act.sem_inc(y_stored[u], 16)

        def evacuate(g, half):
            act.wait_ge(pv_step, g * STEPS + (QT * (half + 1) + CREDIT))
            act.copy(PVs[:, C * half:C * (half + 1)], PV[:]).then_inc(pv_evac, 1)

        def group(g, u, last):
            for s in range(STEPS):
                for aa in range(4):
                    act.wait_ge(st_ready, g * (4 * STEPS) + (4 * s + aa + 1))
                    if aa == 0:
                        act.wait_ge(pv_step, g * STEPS + (s + 1))
                    act.activation(E[(u + s) % 3][:, aa, :], ST[(u + s + aa) % 3][:], ACT.Exp).then_inc(exp_done, 1)
                if s == 0:
                    evacuate(g - 1, 1)
                if s == QT:
                    act.wait_ge(s_ready, g * 34 + (33 + OUT_POS + 1) if not last else use(NG - 1, 0) + 1)
                    evacuate(g, 0)

        with act.Fori(0, (NG - 1) // GB) as i:
            for u in range(GB):
                group(i * GB + u, u, False)
        group(NG - 1, 0, True)
        evacuate(NG - 1, 1)

        def turned(r, dst, scale=None, shift=None, bank0=0):
            for c in range(NC):
                act.wait_ge(tr_ready, NC * r + c + 1)
                if scale is None:
                    ins = act.copy(dst(c), BK[bank0 + c])
                elif shift is None:
                    ins = act.activation(dst(c), BK[bank0 + c], ACT.Copy, scale=scale)
                else:
                    ins = act.activation(dst(c), BK[bank0 + c], ACT.Identity, scale=scale, bias=shift)
                ins.then_inc(fm_ready, 1)

        def xt(c):
            return XT[:, C * c:C * (c + 1)]

        calls = [0]

        def deviation(src, eps):
            calls[0] += 1
            act.wait_ge(var_ready, calls[0])
            act.activation(std_of[calls[0]], src, ACT.Sqrt, bias=eps).then_inc(std_ready, 1)

        std_of = {n: std[:] for n in range(1, 20)}
        std_of[1] = rden[:, 0:NT * NH]
        calls[0] = 1
        act.wait_ge(var_ready, 1)
        act.activation(rden[:, 0:NT * NH], rden[:, NT * NH:2 * NT * NH], ACT.Sqrt, bias=eps5[:],
                       scale=1.0 / (2 * HD)).then_inc(std_ready, 1)
        turned(0, xt)
        deviation(mv[:, :, 1], eps5[:])
        deviation(top[:, 0, :], epsf[:])
        act.wait_ge(in_ffn, 16 * 4)
        turned(1, xt, VC[:, R_LNW:R_LNW + 1])
        act.wait_ge(top_diff, 1)
        act.activation(top[:, 5, :], top[:, 4, :], ACT.Exp).then_inc(r0_exp, 1)
        for c in range(NC):
            act.wait_ge(wet_ready, c + 1)
            act.copy(WET[:, C * c:C * (c + 1)], BK[c][0:E0, :]).then_inc(wet_taken, 1)
        with act.Fori(0, E0 // 2) as i:
            for u in range(2):
                act.wait_ge(wec_ready, 2 * i + (u + 1))
                for c in range(NC):
                    for f in range(4):
                        j = 16 * u + 4 * c + f
                        act.wait_ge(ab_ready, i * 32 + (j + 1))
                        act.activation(gs[:, j % 2, :], BK[2 * (j % 2)], ACT.Silu,
                                       bias=B1c[:, u, f:f + 1]).then_inc(silu_done, 1)

        act.wait_ge(tw_ready, 4)
        for bank, dst, n in ((4, cwt, 4), (5, w3t, 3), (6, wbt, 4), (7, wut, 4)):
            act.copy(dst[:].rearrange("p j d -> p (j d)"), BK[bank][:, 0:P * n]).then_inc(tw_taken, 1)
        act.wait_ge(in_mix, 16 * 9)
        deviation(mv[:, :, 1], eps5[:])
        deviation(mv[:, :, 1], eps5[:])
        turned(2, lambda c: HT[:, c // 2, 3 + C * (c % 2):3 + C * (c % 2 + 1)], VC[:, R_GB + 0:R_GB + 1], VC[:, R_GB + 1:R_GB + 2])
        deviation(mv[:, :, 1], eps5[:])
        turned(3, xt, VC[:, R_GB + 2:R_GB + 3], VC[:, R_GB + 3:R_GB + 4])
        for j in range(3 * NC):
            c, w = divmod(j, 3)
            act.wait_ge(qkv_ready, j + 1)
            act.activation((QF, KF, VF)[w][:, C * c:C * (c + 1)], BK[4 + j % 4], ACT.Identity,
                           bias=VC[:, R_BQKV + w:R_BQKV + w + 1]).then_inc(qkv_taken, 1)
        deviation(mv[:, :, 1], eps5[:])
        turned(4, xt, VC[:, R_GB + 4:R_GB + 5], VC[:, R_GB + 5:R_GB + 6], 4)
        for c in range(NC):
            if c >= 2:
                act.wait_ge(mo_ready, 4 * NC + c - 1)
            for f in range(4):
                j = 4 * c + f
                act.wait_ge(up_ready, j + 1)
                act.activation(G[:, c % 2, f, :], BK[j % 4], ACT.Gelu, bias=VC[:, R_BB + f:R_BB + f + 1]).then_inc(gelu_done, 1)
        deviation(mv[:, :, 1], eps5[:])
        turned(5, xt)
        act.wait_ge(prob_sub, 1)
        act.activation(Lb[:], La[:], ACT.Exp).then_inc(prob_exp, 1)
        for j in range(2 * NC):
            f = j % 2
            M = P if f == 0 else F1B
            act.wait_ge(gu_ready, j + 1)
            act.activation(HS[0:M, f, :], BK[2 * f][0:M, :], ACT.Silu).then_inc(h_silu, 1)
        with act.Fori(0, E1 // 2) as i:
            for u in range(2):
                act.wait_ge(xe_ready, 2 * i + (u + 1))
                act.copy(XET[:, u, :], BK[6 + u][:, 0:CAP]).then_inc(xe_taken, 1)
            for u in range(2):
                for f in range(2):
                    M = P if f == 0 else F1B
                    act.wait_ge(gu_ready, 4 * i + (2 * NC + 2 * u + f + 1))
                    act.activation(HS[0:M, f, 0:CAP], BK[2 * f][0:M, 0:CAP], ACT.Silu).then_inc(h_silu, 1)
            for u in range(2):
                act.wait_ge(ye_ready, 2 * i + (NC + u + 1))
                act.wait_ge(y_stored[u], 32 * i + 16)
                act.copy(YE[:, u, 0:2, :], BK[4 + u][:, 0:2 * P].rearrange("p (k d) -> p k d", d=P))
                act.copy(YE[0:CAPR, u, 2, :], BK[4 + u][0:CAPR, 2 * P:3 * P]).then_inc(ye_taken, 1)
        deviation(mv[:, :, 1], eps5[:])

    @block.vector
    def _(dve):
        chain = Chain(dve, dve_step)
        dve.memset(KM[0][:], 0.0)
        dve.memset(PVs[:], 0.0)
        dve.memset(PV[:], 0.0)
        dve.memset(eps5[:], EPS)
        dve.memset(epsf[:], EPS_FFN).then_inc(const_set, 1)

        dve.wait_ge(in_w, 16 * 4)
        dve.wait_ge(in_x, 16 * 5)
        dve.tensor_copy(identb[:], ident[:])
        for w in range(2):
            src = wqkv[:, w, :].rearrange("p (g a d) -> p g a d", g=8, a=4)
            dst = wq2[:, 2 * w, :].rearrange("p (a g d) -> p g a d", a=4, g=8)
            swp = wq2[:, 2 * w + 1, :].rearrange("p (a g d) -> p g a d", a=4, g=8)
            scale = HD ** -0.5 if w == 0 else 1.0
            dve.tensor_scalar(dst, src, scale, None, ALU.mult)
            s5 = src.rearrange("p g a (h t) -> p g a h t", t=2)
            d5 = swp.rearrange("p g a (h t) -> p g a h t", t=2)
            for t in range(2):
                for aa in range(4):
                    ins = dve.tensor_scalar(d5[:, :, aa, :, t], s5[:, :, aa, :, 1 - t], scale, None, ALU.mult)
        ins.then_inc(w2_ready, 1)

        dve.wait_ge(in_v, IN_V)
        dve.wait_ge(vec_copied, 1)
        for j in range(2):
            dve.tensor_tensor(lamp[:, j, :], lamv[:, 2 * j, :], lamv[:, 2 * j + 1, :], ALU.mult)
        chain(dve.tensor_scalar(gfac[:], VC[:, R_SUBLN:R_SUBLN + 1], 1.0 - LAMBDA_INIT, None, ALU.mult))
        dve.reduce_sum(lams[:, 0:2], lamp[:], AX).then_inc(lam_sum, 1)
        dve.tensor_scalar(wo[:], wqkv[:, 3, :], gfac[:], None, ALU.mult)

        dve.wait_ge(in_tab, 32)
        for j in range(2 * NC):
            c, w = divmod(j, 2)
            tab = slice(C * (c % 2), C * (c % 2 + 1))
            r, q = ra[:, j % 2, :], rb[:, j % 2, :]
            out_ = [parts[:, w, p, C * c:C * (c + 1)] for p in range(3)]
            dve.wait_ge(qk_ready, j + 1)
            dve.tensor_tensor(r, BK[2 * (j % 4)], cosT[:, tab], ALU.mult)
            ins = dve.tensor_tensor(q, BK[2 * (j % 4) + 1], sinT[:, tab], ALU.mult)
            ins.then_inc(qk_taken, 1)
            dve.wait_ge(qk_taken, j + 1)
            chain(dve.tensor_tensor(r, r, q, ALU.add))
            chain(dve.tensor_copy(out_[0], r))
            chain(dve.tensor_tensor(r, r, out_[0], ALU.subtract))
            chain(dve.tensor_copy(out_[1], r))
            dve.tensor_tensor(out_[2], r, out_[1], ALU.subtract).then_inc(parts_ready, 1)

        dve.wait_ge(lam_exp, 1)
        dve.scalar_tensor_tensor(lams[:, 4:5], lams[:, 3:4], -LAMBDA_INIT, lams[:, 2:3], ALU.add, ALU.subtract)
        dve.wait_ge(const_set, 2)
        dve.wait_ge(v_copied, NC)
        dve.sem_inc(s_taken, 2)

        def take_max(v, k, pos, g):
            qt, aa = divmod(k, 4)
            dve.wait_ge(s_ready, use(g, pos) + 1)
            dve.reduce_max(mx[v][:, qt, aa:aa + 1], SM[(1 + pos) % 2][:], AX).then_inc(s_taken, 1)

        def take_rows(g, v, pos):
            dve.wait_ge(s_taken, use(g, pos) + 2)
            dve.tensor_scalar(TM[:, :, :, 0], mx[v][:], -1.0, None, ALU.mult).then_inc(m_hi, 1)
            dve.wait_ge(m_hi, g + 2)
            dve.scalar_tensor_tensor(TM[:, :, :, 1], mx[v][:], -1.0, TM[:, :, :, 0],
                                     ALU.mult, ALU.subtract).then_inc(tm_ready, 1)
            dve.wait_ge(s_ready, use(g, pos) + 1)
            dve.tensor_tensor(Q2[v][:], SM[(1 + pos) % 2][:], QG[v][:], ALU.add).then_inc(s_taken, 1)

        def take_outputs(g, pos, phase):
            dve.wait_ge(s_ready, use(phase, pos) + 1)
            dve.tensor_copy(OT[:, :, bass.ds(g, 1), :, :].rearrange("p q g a v -> p q (g a) v"),
                            SM[(1 + pos) % 2][:].rearrange("p (q a r) -> p q a r", q=QT, a=4)[:, :, :, 0:VD])\
                .then_inc(s_taken, 1)

        def group(g, u):
            v, k, pos = (u + 1) % GB, 0, 0
            for s in range(STEPS):
                if s == OUT_STEP:
                    take_outputs(g, pos, g)
                    pos += 1
                for _ in range(MAX_PER_STEP[s]):
                    take_max(v, k, pos, g)
                    k, pos = k + 1, pos + 1
            take_rows(g, v, pos)

        dve.wait_ge(kq_loaded[0], 80)
        for k in range(4 * QT):
            take_max(0, k, k + 1, -1)
        take_rows(-1, 0, 4 * QT + 1)
        with dve.Fori(0, (NG - 1) // GB) as i:
            for u in range(GB):
                dve.wait_ge(kq_loaded[(u + 1) % GB], 80 * (i + (1 if (u + 1) % GB else 2)))
                group(i * GB + u, u)
        take_outputs(NG - 1, 0, NG - 1)
        take_outputs(NG, 1, NG - 1)
        dve.wait_ge(s_taken, use(NG - 1, 1) + 3)

        och = OT[:, :, 1:NG + 1, :, :]
        rv = rden[:].rearrange("p (q m) -> p q m", q=QT)
        chain(dve.reciprocal(rv, och.rearrange("p q g a v -> p q (g a) v")[:, :, :, 2 * HD]))
        r2 = rden[:].rearrange("p (m s) -> p m s", s=2)[:, :, 1]
        chain(dve.tensor_scalar(r2, r2, lams[:, 4:5], None, ALU.mult))
        for qt in range(QT):
            n = NG * 4
            ins = dve.tensor_tensor(
                NRM[:, n * 8 * qt:n * 8 * (qt + 1)].rearrange("p (m d) -> p m d", d=8),
                OT[:, qt, 1:NG + 1, :, :].rearrange("p g a v -> p (g a) v")[:, :, 0:2 * HD],
                rden[:, n * qt:n * (qt + 1)].unsqueeze(2).to_broadcast([P, n, 8]), ALU.mult)
        chain(ins)
        n2 = NRM.rearrange("p (m s d) -> p m s d", s=2, d=8)
        A = TMP[:].rearrange("p (m d) -> p m d", d=8)
        chain(dve.tensor_tensor(A, n2[:, :, 0, :], n2[:, :, 1, :], ALU.add))
        sq = NRM[:, 0:N].rearrange("p (m d) -> p m d", d=8)
        chain(dve.tensor_tensor(sq, A, A, ALU.mult))
        dve.reduce_sum(rden[:, NT * NH:2 * NT * NH], sq, AX).then_inc(var_ready, 1)
        dve.wait_ge(std_ready, 1)
        rms = rden[:, NT * NH:2 * NT * NH]
        chain(dve.reciprocal(rms, rden[:, 0:NT * NH]))
        chain(dve.tensor_tensor(A, A, rms.unsqueeze(2).to_broadcast([P, NT * NH, 8]), ALU.mult))
        dve.sem_inc(tok_ready, NC)

        calls = [1]

        def norm_stats(src, rms=None):
            for t in range(NT):
                ins = dve.bn_stats(stats[:, t, :], src[:, t, :])
            chain(ins)
            for t in range(NT):
                ins = dve.bn_aggr(mv[:, t, :], stats[:, t, :])
            calls[0] += 1
            if rms is None:
                ins.then_inc(var_ready, 1)
            else:
                chain(ins)
                chain(dve.tensor_tensor(rms, mv[:, :, 0], mv[:, :, 0], ALU.mult))
                dve.tensor_tensor(rms, rms, mv[:, :, 1], ALU.add).then_inc(var_ready, 1)
            dve.wait_ge(std_ready, calls[0])
            chain(dve.reciprocal(rstd[:], std[:]))

        def normalise(dst, src, signal=None):
            for t in range(NT):
                ins = dve.tensor_scalar(dst[:, t, :], src[:, t, :], mv[:, t, 0:1], rstd[:, t:t + 1],
                                        ALU.subtract, ALU.mult)
                if signal is not None and t % TPC == TPC - 1:
                    ins.then_inc(signal, 1)
            if signal is None:
                chain(ins)

        def add_out(dst, src, m, bank0=4):
            for c in range(NC):
                dve.wait_ge(mo_ready, m * NC + c + 1)
                ins = dve.tensor_tensor(dst[:, TPC * c:TPC * (c + 1), :], BK[bank0 + c].rearrange("p (k d) -> p k d", d=P),
                                        src[:, TPC * c:TPC * (c + 1), :], ALU.add)
                ins.then_inc(mo_taken, 1)
            dve.wait_ge(mo_taken, (m + 1) * NC)

        def row(v_, n=NT):
            return v_.unsqueeze(1).to_broadcast([P, n, v_.shape[-1]])

        def each(v_, e):
            return v_.unsqueeze(2).to_broadcast([P, NT, e])

        def top2(L, rev, sa_, sb_, e):
            src = L
            for k in range(2):
                chain(dve.tensor_reduce(top[:, 2 * k, :], src, AX, ALU.max))
                chain(dve.tensor_tensor(sa_, src, each(top[:, 2 * k, :], e), ALU.is_equal))
                chain(dve.tensor_tensor(sa_, sa_, row(rev), ALU.mult))
                chain(dve.tensor_reduce(top[:, 2 * k + 1, :], sa_, AX, ALU.max))
                chain(dve.tensor_tensor(oh[:, k, :, 0:e], sa_, each(top[:, 2 * k + 1, :], e), ALU.is_equal))
                if k == 0:
                    chain(dve.scalar_tensor_tensor(sb_, oh[:, 0, :, 0:e], -3.0e38, L, ALU.mult, ALU.add))
                    src = sb_

        add_out(X, X, 0)
        norm_stats(X)
        normalise(X, X)

        norm_stats(X, top[:, 0, :])
        for t in range(NT):
            ins = dve.tensor_scalar(XS[:, t, :], X[:, t, :], rstd[:, t:t + 1], None, ALU.mult)
            if t % TPC == TPC - 1:
                ins.then_inc(tok_ready, 1)
        dve.wait_ge(r0_ready, 1)
        chain(dve.tensor_tensor(L0[:], BK[4][:, 0:NT * E0].rearrange("p (t e) -> p t e", e=E0), row(bg0[:]), ALU.add))
        top2(L0[:], rev0[:], La[:, :, 0:E0], Lb[:, :, 0:E0], E0)
        dve.tensor_tensor(top[:, 4, :], top[:, 2, :], top[:, 0, :], ALU.subtract).then_inc(top_diff, 1)
        dve.wait_ge(r0_exp, 1)
        chain(dve.tensor_scalar(top[:, 6, :], top[:, 5, :], 1.0, None, ALU.add))
        chain(dve.reciprocal(top[:, 7, :], top[:, 6, :]))
        chain(dve.tensor_tensor(top[:, 6, :], top[:, 7, :], top[:, 5, :], ALU.mult))
        dve.tensor_tensor(La[:, :, 0:E0], oh[:, 0, :, 0:E0], each(top[:, 7, :], E0), ALU.mult)
        chain(dve.tensor_tensor(Lb[:, :, 0:E0], oh[:, 1, :, 0:E0], each(top[:, 6, :], E0), ALU.mult))
        dve.tensor_tensor(WE[:], La[:, :, 0:E0], Lb[:, :, 0:E0], ALU.add).then_inc(we_ready, 1)
        add_out(X, X, 1)
        dve.sem_inc(g_done, 2)
        dve.sem_inc(acc_done, 5)

        with dve.Fori(0, E0 // 2) as i:
            def gate0(u, c, f):
                j = 16 * u + 4 * c + f
                dve.wait_ge(silu_done, i * 32 + (j + 1))
                if f == 0:
                    dve.wait_ge(y_ready, i * 8 + (4 * u + c + 1))
                dve.scalar_tensor_tensor(G[:, c % 2, f, :], BK[2 * (j % 2) + 1], VC[:, bass.ds(8 * i + (R_B1B + 4 * u + f), 1)],
                                         gs[:, j % 2, :], ALU.add, ALU.mult).then_inc(g_done, 1)

            def sum0(n):
                u, c = divmod(n, 4)
                dve.wait_ge(y_ready, i * 8 + (n + 3))
                dve.wait_ge(acc_done, i * 8 + (n + 2))
                dve.wait_ge(wec_ready, 2 * i + (u + 1))
                for k in range(TPC):
                    t = TPC * c + k
                    ins = dve.scalar_tensor_tensor(X[:, t, :], BK[4 + n % 2][:, P * k:P * (k + 1)],
                                                   WEc[:, u, t:t + 1], X[:, t, :], ALU.mult, ALU.add)
                ins.then_inc(acc_done, 1)

            for u in range(2):
                for c in range(NC):
                    for f in range(4):
                        gate0(u, c, f)
                    if u or c:
                        sum0(4 * u + c - 1)
            sum0(7)

        dve.wait_ge(acc_done, 32 + 5)
        dve.memset(HT[:, :, 0:3], 0.0)
        dve.memset(onesS[:], 1.0)
        dve.memset(onesb[:], 1.0)
        chain(dve.memset(cwm[:], 0.0))
        dve.wait_ge(in_mix, 16 * 9)
        for q in range(4):
            r = slice(32 * q, 32 * (q + 1))
            ins = dve.tensor_copy(cwm[r, :, r], cw[r, :, :].rearrange("p i t -> p t i"))
        ins.then_inc(cwm_ready, 1)
        norm_stats(X)
        normalise(X, X)
        norm_stats(X)
        normalise(XS, X, tok_ready)
        chain(dve.tensor_tensor(X0[:], X[:], row(rows[:, 0, :]), ALU.add))
        add_out(X0, X0, 2)
        norm_stats(X0)
        normalise(XS, X0, tok_ready)
        for b in range(NB):
            r = slice(S * b, S * (b + 1))
            dve.wait_ge(qkv_taken, 6 * (b + 1))
            chain(dve.tensor_tensor_scan(TMP[:, r], onesS[:], QF[:, r], 0.0, ALU.mult, ALU.add))
            chain(dve.tensor_tensor(TMP[:, r], TMP[:, r], invp[:], ALU.mult))
            chain(dve.tensor_tensor(TMP[:, r], TMP[:, r], KF[:, r], ALU.mult))
            chain(dve.tensor_tensor_scan(QF[:, r], onesS[:], TMP[:, r], 0.0, ALU.mult, ALU.add))
            chain(dve.tensor_tensor(QF[:, r], QF[:, r], invp[:], ALU.mult))
            dve.tensor_tensor(QF[:, r], QF[:, r], VF[:, r], ALU.mult).then_inc(pool_done, 1)
        add_out(X0, X0, 3, 0)
        norm_stats(X0)
        normalise(XS, X0, tok_ready)
        chain(dve.tensor_tensor(X[:], X[:], X0[:], ALU.add))
        chain(dve.tensor_tensor(X[:], X[:], row(rows[:, 1, :]), ALU.add))
        add_out(X, X, 4)
        norm_stats(X)
        normalise(X, X, tok_ready)

        dve.wait_ge(in_moe, 16 * 9)
        dve.wait_ge(lg_ready, 1)
        chain(dve.tensor_tensor(La[:], BK[6][:, 0:NT * E1].rearrange("p (t e) -> p t e", e=E1), row(rbb[:]), ALU.add))
        chain(dve.tensor_reduce(top[:, 0, :], La[:], AX, ALU.max))
        dve.tensor_tensor(La[:], La[:], each(top[:, 0, :], E1), ALU.subtract).then_inc(prob_sub, 1)
        dve.wait_ge(prob_exp, 1)
        chain(dve.reduce_sum(top[:, 1, :], Lb[:], AX))
        chain(dve.reciprocal(top[:, 2, :], top[:, 1, :]))
        chain(dve.tensor_tensor(La[:], Lb[:], each(top[:, 2, :], E1), ALU.mult))
        top2(La[:], rev1[:], prod[:], Lb[:], E1)
        chain(dve.tensor_tensor(self_[:].rearrange("p e t -> p t e"), oh[:, 0], oh[:, 1], ALU.add))
        chain(dve.tensor_tensor_scan(cumf[:].rearrange("p e t -> p (e t)"), seg[:],
                                     self_[:].rearrange("p e t -> p (e t)"), 0.0, ALU.mult, ALU.add))
        dve.tensor_copy(selb[:], self_[:])
        dve.tensor_copy(ltrib[:], ltri[:])
        dve.tensor_tensor(cumb[:], cumf[:], self_[:], ALU.subtract).then_inc(sel_ready, 1)
        chain(dve.tensor_tensor(top[:, 4, :], top[:, 0, :], top[:, 2, :], ALU.add))
        chain(dve.tensor_scalar(top[:, 4, :], top[:, 4, :], 1e-9, None, ALU.add))
        chain(dve.reciprocal(top[:, 5, :], top[:, 4, :]))
        dve.tensor_tensor(wts[:, 0, :], top[:, 0, :], top[:, 5, :], ALU.mult)
        chain(dve.tensor_tensor(wts[:, 1, :], top[:, 2, :], top[:, 5, :], ALU.mult))

        dve.sem_inc(h_done, 2)

        def gate1(j, n, hb, f):
            M = P if f == 0 else F1B
            dve.wait_ge(h_silu, j)
            dve.tensor_tensor(H[0:M, hb, f, 0:n], HS[0:M, f, 0:n], BK[2 * f + 1][0:M, 0:n], ALU.mult)\
                .then_inc(h_done, 1)

        def slots():
            dve.wait_ge(pos_ready, 1)
            pos = BK[7][:, 0:E1 * NT].rearrange("p (e t) -> p t e", e=E1)
            dve.tensor_scalar(posx[:, 2], pos, float(CAP), None, ALU.is_lt)
            dve.tensor_scalar(posx[:, 1], pos, float(CAP - 1), None, ALU.min)
            chain(dve.tensor_tensor(posx[:, 0], pos, row(base1[:]), ALU.add))
            dve.tensor_tensor(posx[:, 1], posx[:, 1], row(base1[:]), ALU.add)
            chain(dve.scalar_tensor_tensor(posx[:, 0], posx[:, 2], -float(FAR), posx[:, 0], ALU.mult, ALU.add))
            for k in range(2):
                for m in range(3):
                    chain(dve.tensor_tensor(prod[:], posx[:, m], oh[:, k], ALU.mult))
                    chain(dve.reduce_sum(fidx[:, 3 * k + m, :], prod[:], AX))
            for k in range(2):
                dve.tensor_scalar(idx[:, 0, :, k], fidx[:, 3 * k, :], float(FAR), None, ALU.add)
                dve.tensor_copy(idx[:, 1, :, k], fidx[:, 3 * k + 1, :])
                ins = dve.tensor_tensor(wts[:, k, :], wts[:, k, :], fidx[:, 3 * k + 2, :], ALU.mult)
            ins.then_inc(idx_ready, 1)

        def shared_out(c):
            dve.wait_ge(ye_ready, c + 1)
            dve.tensor_tensor(XS[:, TPC * c:TPC * (c + 1), :], BK[4 + c % 2].rearrange("p (k d) -> p k d", d=P),
                              XS[:, TPC * c:TPC * (c + 1), :], ALU.add).then_inc(ye_taken, 1)

        dve.sem_inc(ye_taken, 2)
        chain(dve.tensor_scalar(XS[:], X[:], 2.0, None, ALU.mult))
        for c in range(NC):
            for f in range(2):
                if c >= 2 and f == 0:
                    dve.wait_ge(ye_ready, c - 1)
                gate1(2 * c + f + 1, C, c % 2, f)
            if c == 1:
                slots()
            if c:
                shared_out(c - 1)
        shared_out(NC - 1)
        with dve.Fori(0, E1 // 2) as i:
            for u in range(2):
                for f in range(2):
                    if f == 0:
                        dve.wait_ge(ye_ready, 2 * i + (NC + u - 1))
                    gate1(4 * i + (2 * NC + 2 * u + f + 1), CAP, u, f)

        dve.wait_ge(gathered, 16 * 2 * NT)
        dve.wait_ge(idx_ready, 1)
        for k in range(2):
            for t in range(NT):
                ins = dve.scalar_tensor_tensor(XS[:, t, :], YG[:, t, k, :], wts[:, k, t:t + 1], XS[:, t, :],
                                               ALU.mult, ALU.add)
            chain(ins)
        norm_stats(XS)
        normalise(XS, XS, result_ready)


_NAMES = {
    "x": "L0_attn_x", "Wq": "L0_attn_Wq", "Wk": "L0_attn_Wk", "Wv": "L0_attn_Wv", "Wo": "L0_attn_Wo",
    "lq1": "L0_attn_lambda_q1", "lk1": "L0_attn_lambda_k1", "lq2": "L0_attn_lambda_q2", "lk2": "L0_attn_lambda_k2",
    "subln_g": "L0_attn_subln_g", "ln_w": "L0_ffn_ln_w", "Wg": "L0_ffn_Wg", "bg": "L0_ffn_bg",
    "W1a": "L0_ffn_W1a", "b1a": "L0_ffn_b1a", "W1b": "L0_ffn_W1b", "b1b": "L0_ffn_b1b", "W2": "L0_ffn_W2",
    "b2": "L0_ffn_b2", "ln_attn_g": "L1_attn_ln_attn_g", "ln_attn_b": "L1_attn_ln_attn_b", "mWq": "L1_attn_Wq",
    "bq": "L1_attn_bq", "mWk": "L1_attn_Wk", "bk": "L1_attn_bk", "mWv": "L1_attn_Wv", "bv": "L1_attn_bv",
    "ln_conv_g": "L1_attn_ln_conv_g", "ln_conv_b": "L1_attn_ln_conv_b", "conv_w": "L1_attn_conv_w",
    "conv_b": "L1_attn_conv_b", "ln_boom_g": "L1_attn_ln_boom_g", "ln_boom_b": "L1_attn_ln_boom_b",
    "Wb": "L1_attn_Wb", "bb": "L1_attn_bb", "Wu": "L1_attn_Wu", "bu": "L1_attn_bu",
    "router_w": "L1_ffn_router_w", "router_b": "L1_ffn_router_b", "w_gate": "L1_ffn_w_gate",
    "w_up": "L1_ffn_w_up", "w_down": "L1_ffn_w_down", "sw_gate": "L1_ffn_sw_gate", "sw_up": "L1_ffn_sw_up",
    "sw_down": "L1_ffn_sw_down",
}


def _constants(np):
    f = np.float32
    d = np.arange(P) % HD
    freq = f(1.0) / f(0.0001) ** (f(2.0) * np.arange(HD // 2, dtype=f) / f(HD))
    angle = np.arange(S, dtype=f)[None, :] * freq[d // 2][:, None]
    sign = np.where(d % 2 == 0, f(-1.0), f(1.0))[:, None]
    return {
        "ident": np.eye(P, dtype=f),
        "cos": np.cos(angle.astype(np.float64)).astype(f),
        "sin": np.sin(angle.astype(np.float64)).astype(f) * sign,
        "rev0": np.arange(E0, 0, -1).astype(f),
        "rev1": np.arange(E1, 0, -1).astype(f),
        "base1": (np.arange(E1) * CAP).astype(f),
        "seg": np.tile((np.arange(NT) > 0).astype(f), E1),
        "ltri": np.triu(np.ones((P, P), f), 1),
        "invp": f(1.0) / np.arange(1, S + 1, dtype=f),
    }


def kernel(**inputs):
    import numpy as _np
    import concourse.bacc as _bacc
    from concourse import mybir as _mybir
    from concourse.bass_utils import run_bass_kernel_spmd as _run

    nc = _bacc.Bacc("TRN2", target_bir_lowering=False, num_devices=1)
    arrays, aps = {}, {}
    given = {short: _np.ascontiguousarray(inputs[name]) for short, name in _NAMES.items()}
    for name, v in {**given, **_constants(_np)}.items():
        arrays[f"in_{name}"] = v
        aps[name] = nc.dram_tensor(f"in_{name}", v.shape, _mybir.dt.from_np(v.dtype), kind="ExternalInput").ap()
    out = nc.dram_tensor("out", (NB, S, P), F32, kind="ExternalOutput").ap()
    build(nc, aps, out)
    r = _run(nc, [arrays], core_ids=[0])
    return r.results[0]["out"]
```

```python
import math
from contextlib import ExitStack

import concourse.bass as bass
from concourse import mybir

F32 = mybir.dt.float32
BF16 = mybir.dt.bfloat16
I32 = mybir.dt.int32
U32 = mybir.dt.uint32
ALU = mybir.AluOpType
ACT = mybir.ActivationFunctionType
AX = mybir.AxisListType.X

P = 128
NB, S = 2, 1024
N = NB * S
NT = N // P
QT = S // P
C = 512
NC = N // C
TPC = C // P

NH, HD = 16, 4
VD = 2 * HD + 1
NG = NB * 8
GB = 3
RH = 32
NBLK = 6
BLOCKS = ((slice(2, 5), slice(1, 6, 4), slice(0, 1)),
          (slice(0, 3), slice(3, 6, 2), slice(4, 5)))
MAXROW = HD * NBLK
EPS = 1e-5
SEQ_ORDER = (0, 2, 1, 3)
LAMBDA_INIT = 0.8 - 0.6 * math.exp(-0.3 * 12)
FAR = 1 << 20
EPS_FFN = 1.1920928955078125e-07
OUT_POS = 5
CREDIT = 3
STEPS = 16
MAX_PER_STEP = (3, 2, 2, 2, 3, 2, 2, 2, 3, 2, 2, 2, 3, 2, 0, 0)
OUT_STEP = 2

E0, F0 = 8, 512
E1, F1 = 16, 176
FT = F1 // 2
CAP = 320
CR = 3
CP = -(-CAP // CR)
CAPN = CP * CR
CAPS = CR * P
SLOTS = E1 * CAPS
RW = P + 2
EB = 4

R_B1A, R_B1B, R_BB, R_BQKV = 0, 4 * E0, 8 * E0, 8 * E0 + 4
R_GB = R_BQKV + 3
R_LNW, R_SUBLN = R_GB + 6, R_GB + 7
R_N = R_SUBLN + 1
IN_V = 16 * (4 + 1 + 2 + 1 + 10)


def build(nc, a, out):
    with ExitStack() as ctx:
        program(nc, ctx, a, out)


def program(nc, ctx, a, out):
    def sb(name, shape, dt=F32):
        return ctx.enter_context(nc.sbuf_tensor(name, shape, dt))

    def sem(name):
        return ctx.enter_context(nc.semaphore(name))

    ident = sb("ident", [P, P])
    identb = sb("identb", [P, P], BF16)
    eps5 = sb("eps5", [P, 1])
    epsf = sb("epsf", [P, 1])
    eps55 = sb("eps55", [P, 1])
    X = sb("X", [P, NT, P])
    XS = sb("XS", [P, NT, P])
    empty = XS[:].rearrange("p t d -> p (t d)")[:, 0:CR * RW]
    zeros = XS[:].rearrange("p t d -> p (t d)")[:, N - 2 * N // 4:N]
    XT = sb("XT", [P, N])
    TMP = sb("TMP", [P, N])
    stats = sb("stats", [P, NT, 6])
    mv = sb("mv", [P, NT, 2])
    std = sb("std", [P, 2, NT])
    rstd = sb("rstd", [P, 2, NT])
    wqkv = sb("wqkv", [P, 4, P])
    lamv = sb("lamv", [P, 4, HD])
    lamp = sb("lamp", [P, 2, HD])
    lams = sb("lams", [P, 8])
    gfac = sb("gfac", [P, 1])
    VR = sb("VR", [R_N, P])
    VC = sb("VC", [P, R_N])
    wo = sb("wo", [P, P])

    wg0 = sb("wg0", [P, E0])
    bg0 = sb("bg0", [P, E0])
    b2 = sb("b2", [E0, P])
    rev0 = sb("rev0", [P, E0])
    cw = sb("cw", [P, 32, 4])
    w3 = sb("w3", [P, 3, P])
    wb = sb("wb", [P, 4, P])
    wu = sb("wu", [P, 4, P])
    rows = sb("rows", [P, 2, P])
    rw = sb("rw", [P, E1])
    rbb = sb("rbb", [P, E1])
    rev1 = sb("rev1", [P, E1])
    base1 = sb("base1", [P, E1])
    seg = sb("seg", [P, E1 * NT])
    ltri = sb("ltri", [P, P])
    rowid = sb("rowid", [P, NT, 2])
    ltrib = sb("ltrib", [P, P], BF16)
    swg = sb("swg", [P, 2, F1])
    swd = sb("swd", [FT, 2, P])

    with ExitStack() as first:
        def sa(name, shape, dt=F32):
            return first.enter_context(nc.sbuf_tensor(name, shape, dt))

        wq2 = sa("wq2", [P, 4, P])
        cosT = sa("cosT", [P, S])
        sinT = sa("sinT", [P, S])
        ra = sa("ra", [P, 4, C])
        rb = sa("rb", [P, 2, C])
        parts = sa("parts", [P, 2, 3, N], BF16)
        KM = [sa(f"KM{u}", [P, 4, S], BF16) for u in range(GB)]
        QG = [sa(f"QG{u}", [P, S], BF16) for u in range(GB)]
        Q2 = [sa(f"Q2{u}", [P, S], BF16) for u in range(GB)]
        VG = [sa(f"VG{u}", [P, QT, 2, VD]) for u in range(GB)]
        V = sa("V", [P, QT, NB * NH, VD])
        E = [sa(f"E{u}", [P, 4, C]) for u in range(3)]
        mx = [sa(f"mx{u}", [P, QT, 4]) for u in range(GB)]
        TM = sa("TM", [P, QT, 4, RH], BF16)
        PVs = sa("PVs", [P, S])
        OT = sa("OT", [P, QT, NG + 1, 4, VD])
        rden = sa("rden", [P, QT * NG * 4])
        ssq = sa("ssq", [P, QT * NG * 2])
        NRM = parts[:].rearrange("p w t n -> p (w t n)").bitcast(F32)[:, 0:QT * NG * 4 * 2 * HD]

    L0 = sb("L0", [P, NT, E0])
    La = sb("La", [P, NT, E1])
    Lb = sb("Lb", [P, NT, E1])
    oh = sb("oh", [P, 2, NT, E1])
    top = sb("top", [P, 8, NT])
    WE = sb("WE", [P, NT, E0])
    WET = sb("WET", [E0, N])
    WEc = sb("WEc", [P, 2, NT])
    B1c = sb("B1c", [P, 2, 4])
    w1a = sb("w1a", [P, 2, F0])
    w1b = sb("w1b", [P, 2, F0])
    w2 = sb("w2", [P, 2, 4, P])
    gs = sb("gs", [P, 2, C])
    G = sb("G", [P, 2, 4, C])
    HT = sb("HT", [P, NB, S + 3])
    QF = sb("QF", [P, N])
    KF = sb("KF", [P, N])
    VF = sb("VF", [P, N])
    X0 = sb("X0", [P, NT, P])
    cwm = sb("cwm", [P, 4, P])
    cwt = sb("cwt", [P, 4, P])
    w3t = sb("w3t", [P, 3, P])
    wbt = sb("wbt", [P, 4, P])
    wut = sb("wut", [P, 4, P])
    invp = sb("invp", [P, S])
    onesS = sb("onesS", [P, S])
    onesb = sb("onesb", [P, P], BF16)
    selb = sb("selb", [P, E1, NT], BF16)
    cumb = sb("cumb", [P, E1, NT], BF16)
    self_ = sb("self_", [P, E1, NT])
    cumf = sb("cumf", [P, E1, NT])
    posx = sb("posx", [P, 2, NT, E1])
    prod = sb("prod", [P, NT, E1])
    idx = sb("idx", [P, NT, 2], I32)
    fidx = sb("fidx", [P, 2, NT])
    XI = sb("XI", [P, NT, 2, RW])
    wg1 = sb("wg1", [P, EB, 2, F1])
    wd1 = sb("wd1", [FT, EB, 2, P])
    XE = VF[:, 0:EB * CR * RW].rearrange("p (b r w) -> p b r w", b=EB, r=CR)
    XET = sb("XET", [P, 2, CR, CP])
    oid = sb("oid", [P, EB, CR], I32)
    slotw = sb("slotw", [P, EB, CR])
    HS = sb("HS", [FT, 2, C])
    H = sb("H", [FT, 2, 2, C])
    YE = KF[:, 0:EB * CR * P].rearrange("p (b r d) -> p b r d", b=EB, r=CR)
    YG = G[:].rearrange("p u f c -> p (u f c)").rearrange("p (t k d) -> p t k d", k=2, d=P)

    SM = [ctx.enter_context(nc.psum_tensor(f"SM{i}", [P, 2 * C], F32)) for i in range(2)]
    ST = [ctx.enter_context(nc.psum_tensor(f"ST{i}", [P, C], F32)) for i in range(3)]
    PV = ctx.enter_context(nc.psum_tensor("PVp", [P, C], F32))
    BK = [SM[0][:, 0:C], SM[0][:, C:2 * C], SM[1][:, 0:C], SM[1][:, C:2 * C],
          ST[0][:, :], ST[1][:, :], ST[2][:, :], PV[:, :]]

    qrows = nc.dram_tensor("qrows", [NBLK, NB * P, S], BF16, kind="Internal").ap()
    krows = nc.dram_tensor("krows", [NBLK, NB * P, S], BF16, kind="Internal").ap()
    xslots = nc.dram_tensor("xslots", [SLOTS, RW], F32, kind="Internal").ap()
    orows = nc.dram_tensor("orows", [2 * N, P], F32, kind="Internal").ap()

    in_id, in_x, in_wo = sem("in_id"), [sem(f"in_x{c}") for c in range(NC)], sem("in_wo")
    in_w, in_tab, in_v, in_ffn, in_mix, in_moe = (sem(n) for n in (
        "in_w", "in_tab", "in_v", "in_ffn", "in_mix", "in_moe"))
    km_zeroed, pv_zeroed = sem("km_zeroed"), sem("pv_zeroed")
    const_set = sem("const_set")
    dve_step = sem("dve_step")
    act_step = sem("act_step")
    vec_ready, vec_copied = sem("vec_ready"), sem("vec_copied")
    xT_ready, xT_copied = sem("xT_ready"), sem("xT_copied")
    w2_ready = sem("w2_ready")
    qk_ready, qk_taken = sem("qk_ready"), sem("qk_taken")
    v_ready, v_copied = sem("v_ready"), sem("v_copied")
    rot_ready, part0_ready, rest_ready, part1_ready, parts_ready = (sem(n) for n in (
        "rot_ready", "part0_ready", "rest_ready", "part1_ready", "parts_ready"))
    rows_stored = sem("rows_stored")
    kq_loaded = [sem(f"kq_loaded{u}") for u in range(GB)]
    vg_ready = sem("vg_ready")
    s_ready, s_taken = sem("s_ready"), sem("s_taken")
    m_hi, tm_ready, q2_ready = sem("m_hi"), sem("tm_ready"), sem("q2_ready")
    st_ready, exp_done = sem("st_ready"), sem("exp_done")
    pv_step, pv_evac, group_done = sem("pv_step"), sem("pv_evac"), sem("group_done")
    lam_sum, lam_exp, lam_ready = sem("lam_sum"), sem("lam_exp"), sem("lam_ready")
    var_ready, std_ready = sem("var_ready"), sem("std_ready")
    tok_ready = sem("tok_ready")
    tr_ready, tr_taken = sem("tr_ready"), sem("tr_taken")
    mo_ready, mo_taken = sem("mo_ready"), sem("mo_taken")
    fm_ready = sem("fm_ready")
    r0_ready, r0_exp, we_ready = sem("r0_ready"), sem("r0_exp"), sem("we_ready")
    top_diff = sem("top_diff")
    wet_ready, wet_taken = sem("wet_ready"), sem("wet_taken")
    w0_loaded = [sem(f"w0_loaded{u}") for u in range(2)]
    wec_ready = sem("wec_ready")
    ab_ready, silu_done, g_done = sem("ab_ready"), sem("silu_done"), sem("g_done")
    y_ready, acc_done, e0_done = sem("y_ready"), sem("acc_done"), sem("e0_done")
    tw_ready, tw_taken = sem("tw_ready"), sem("tw_taken")
    cwm_ready = sem("cwm_ready")
    up_ready, gelu_done = sem("up_ready"), sem("gelu_done")
    lg_ready, prob_exp, prob_sub = sem("lg_ready"), sem("prob_exp"), sem("prob_sub")
    sel_ready, pos_ready = sem("sel_ready"), sem("pos_ready")
    idx_ready, scattered, zeroed = sem("idx_ready"), sem("scattered"), sem("zeroed")
    w1_loaded = [sem(f"w1_loaded{u}") for u in range(EB)]
    slots_loaded = [sem(f"slots_loaded{u}") for u in range(EB)]
    y_scattered = [sem(f"y_scattered{u}") for u in range(EB)]
    xi_ready, rows_weighed = sem("xi_ready"), sem("rows_weighed")
    yg_loaded = [sem(f"yg_loaded{c}") for c in range(NC)]
    xe_ready, xe_taken = sem("xe_ready"), sem("xe_taken")
    qkv_ready, qkv_taken, pool_done = sem("qkv_ready"), sem("qkv_taken"), sem("pool_done")
    gu_ready, h_silu, h_done = sem("gu_ready"), sem("h_silu"), sem("h_done")
    ye_ready, ye_taken = sem("ye_ready"), sem("ye_taken")
    shared_ready, shared_taken = sem("shared_ready"), sem("shared_taken")
    result_ready, stored = sem("result_ready"), sem("stored")

    block = ctx.enter_context(nc.Block())

    class Chain:

        def __init__(self, eng, s):
            self.eng, self.s, self.n = eng, s, 0

        def __call__(self, ins):
            self.n += 1
            ins.then_inc(self.s, 1)
            self.eng.wait_ge(self.s, self.n)

    def use(g, pos):
        return 33 + 34 * g + pos

    @block.sync
    def _(sp):
        def load_x(c):
            sp.dma_start(X[:, TPC * c:TPC * (c + 1), :],
                         a["x"].rearrange("b (t p) d -> p (b t) d", p=P)[:, TPC * c:TPC * (c + 1), :]).then_inc(in_x[c], 16)

        sp.dma_start(ident[:], a["ident"]).then_inc(in_id, 16)
        load_x(0)
        for j, n in enumerate(("Wq", "Wk")):
            sp.dma_start(wqkv[:, j, :], a[n]).then_inc(in_w, 16)
        sp.dma_start(cosT[:], a["cos"]).then_inc(in_tab, 16)
        sp.dma_start(sinT[:], a["sin"]).then_inc(in_tab, 16)
        for c in range(1, NC):
            load_x(c)
        for j, n in ((2, "Wv"), (3, "Wo")):
            sp.dma_start(wqkv[:, j, :], a[n]).then_inc(in_wo, 16)
        def store_rows(j):
            c, w = divmod(j, 2)
            b, h = divmod(c, 2)
            sp.wait_ge(parts_ready, j + 1)
            for part in range(3):
                blocks = BLOCKS[w][part]
                n = len(range(NBLK)[blocks])
                sp.dma_start((qrows, krows)[w][blocks, P * b:P * (b + 1), C * h:C * (h + 1)].rearrange("k r t -> r k t"),
                             parts[:, w, part, C * c:C * (c + 1)].unsqueeze(1).to_broadcast([P, n, C]))\
                    .then_inc(rows_stored, 16)

        def load_group(u, g):
            for aa in range(4):
                for src, dst in ((qrows, QG[u][RH * aa:RH * aa + MAXROW, :]),
                                 (krows, KM[u][RH * aa:RH * aa + MAXROW, aa, :])):
                    sp.dma_start(dst, src.rearrange("k (g a d) t -> k g a d t", a=4, d=HD)[:, bass.ds(g, 1), aa]
                                 .rearrange("k g d t -> k (g d) t")).then_inc(kq_loaded[u], 16)

        for j in range(NC):
            store_rows(j)
        sp.wait_ge(const_set, 2)
        sp.wait_ge(rows_stored, 12 * 16)
        for g in range(GB):
            load_group(g, g)
        for j, n in enumerate(("lq1", "lk1", "lq2", "lk2")):
            sp.dma_start(lamv[:, j, :], a[n].partition_broadcast(P)).then_inc(in_v, 16)
        sp.dma_start(VR[R_SUBLN:R_SUBLN + 1, :].rearrange("o (h d) -> o h d", h=NH),
                     a["subln_g"].partition_broadcast(NH).unsqueeze(0)).then_inc(in_v, 16)
        for r, n in ((R_B1A, "b1a"), (R_B1B, "b1b")):
            sp.dma_start(VR[r:r + 4 * E0, :], a[n].rearrange("e (f p) -> (e f) p", p=P)).then_inc(in_v, 16)
        sp.dma_start(VR[R_BB:R_BB + 4, :], a["bb"].rearrange("(f p) -> f p", p=P)).then_inc(in_v, 16)
        for r, n in ((R_BQKV, "bq"), (R_BQKV + 1, "bk"), (R_BQKV + 2, "bv"), (R_GB, "ln_conv_g"),
                     (R_GB + 1, "ln_conv_b"), (R_GB + 2, "ln_attn_g"), (R_GB + 3, "ln_attn_b"),
                     (R_GB + 4, "ln_boom_g"), (R_GB + 5, "ln_boom_b"), (R_LNW, "ln_w")):
            sp.dma_start(VR[r:r + 1, :], a[n].unsqueeze(0)).then_inc(in_v, 16)

        for j in range(NC, 2 * NC):
            store_rows(j)
        sp.wait_ge(rows_stored, 24 * 16)

        sp.dma_start(wg0[:], a["Wg"]).then_inc(in_ffn, 16)
        sp.dma_start(bg0[:], a["bg"].partition_broadcast(P)).then_inc(in_ffn, 16)
        sp.dma_start(rev0[:], a["rev0"].partition_broadcast(P)).then_inc(in_ffn, 16)
        sp.dma_start(b2[:], a["b2"]).then_inc(in_ffn, 16)
        sp.dma_start(cw[:], a["conv_w"]).then_inc(in_mix, 16)
        for j, n in enumerate(("mWq", "mWk", "mWv")):
            sp.dma_start(w3[:, j, :], a[n]).then_inc(in_mix, 16)
        sp.dma_start(wb[:], a["Wb"].rearrange("(f p) d -> p f d", p=P)).then_inc(in_mix, 16)
        sp.dma_start(wu[:], a["Wu"].rearrange("d (f p) -> d f p", p=P)).then_inc(in_mix, 16)
        sp.dma_start(rows[:, 0, :], a["conv_b"].partition_broadcast(P)).then_inc(in_mix, 16)
        sp.dma_start(rows[:, 1, :], a["bu"].partition_broadcast(P)).then_inc(in_mix, 16)
        sp.dma_start(rw[:], a["router_w"]).then_inc(in_moe, 16)
        sp.dma_start(rowid[:], a["rowid"]).then_inc(in_moe, 16)
        for dst, n in ((rbb[:], "router_b"), (rev1[:], "rev1"), (base1[:], "base1"), (seg[:], "seg")):
            sp.dma_start(dst, a[n].partition_broadcast(P)).then_inc(in_moe, 16)
        sp.dma_start(ltri[:], a["ltri"]).then_inc(in_moe, 16)
        sp.dma_start(swg[:, 0, :], a["sw_gate"]).then_inc(in_moe, 16)
        sp.dma_start(swg[:, 1, :], a["sw_up"]).then_inc(in_moe, 16)
        sp.dma_start(swd[:], a["sw_down"].rearrange("(f p) d -> p f d", p=FT)).then_inc(in_moe, 16)
        sp.dma_start(xslots.rearrange("(e p r) d -> p e (r d)", e=E1, p=P),
                     empty.unsqueeze(1).to_broadcast([P, E1, CR * RW])).then_inc(zeroed, 16)

        with sp.Fori(0, (NG - 1 - GB) // GB) as i:
            for u in range(GB):
                sp.wait_ge(pv_step, (i * GB + u) * STEPS + (STEPS + CREDIT))
                load_group(u, i * GB + (GB + u))
        sp.wait_ge(pv_step, (NG - GB) * STEPS + CREDIT)
        load_group(0, NG - 1)

        sp.wait_ge(tok_ready, NC)
        sp.dma_start(invp[:], a["invp"].partition_broadcast(P)).then_inc(in_mix, 16)

        def load_expert0(u, e):
            sp.dma_start(w1a[:, u, :], a["W1a"][bass.ds(e, 1)].rearrange("e d f -> (e d) f")).then_inc(w0_loaded[u], 16)
            sp.dma_start(w1b[:, u, :], a["W1b"][bass.ds(e, 1)].rearrange("e d f -> (e d) f")).then_inc(w0_loaded[u], 16)
            sp.dma_start(w2[:, u, :, :],
                         a["W2"][bass.ds(e, 1)].rearrange("e (f p) d -> p (e f) d", p=P)).then_inc(w0_loaded[u], 16)

        for u in range(2):
            load_expert0(u, u)
        with sp.Fori(0, E0 // 2 - 1) as i:
            for u in range(2):
                sp.wait_ge(y_ready, 8 * i + (4 * u + 6))
                load_expert0(u, 2 * i + (u + 2))

        def load_weights1(b, e):
            sp.dma_start(wg1[:, b, 0, :], a["w_gate"][bass.ds(e, 1)].rearrange("e d f -> (e d) f")).then_inc(w1_loaded[b], 16)
            sp.dma_start(wg1[:, b, 1, :], a["w_up"][bass.ds(e, 1)].rearrange("e d f -> (e d) f")).then_inc(w1_loaded[b], 16)
            sp.dma_start(wd1[:, b, :, :],
                         a["w_down"][bass.ds(e, 1)].rearrange("e (f p) d -> p (e f) d", p=FT)).then_inc(w1_loaded[b], 16)

        def load_slots1(b, e):
            xr = xslots.rearrange("(e p r) d -> e p (r d)", e=E1, p=P)[bass.ds(e, 1), 0:CP]
            sp.dma_start(XE[0:CP, b, :, :].rearrange("p r d -> p (r d)"),
                         xr.rearrange("e p c -> (e p) c")).then_inc(slots_loaded[b], 16)

        for b in range(EB):
            load_weights1(b, b)
        sp.wait_ge(scattered, 16 * 2 * NT)
        for b in range(EB):
            load_slots1(b, b)
        with sp.Fori(0, E1 // EB - 1) as i:
            for b in range(EB):
                sp.wait_ge(h_done, i * (2 * EB) + (2 * NC + 2 * b + 4))
                load_slots1(b, i * EB + (EB + b))
                sp.wait_ge(ye_ready, i * EB + (b + 1))
                load_weights1(b, i * EB + (EB + b))

        for b in range(EB):
            sp.wait_ge(y_scattered[b], 16 * CR * (E1 // EB) + 16)
        for c in range(NC):
            sp.dma_start(YG[:, TPC * c:TPC * (c + 1), :, :].rearrange("p t k d -> p t (k d)"),
                         orows.rearrange("(t p k) d -> p t (k d)", p=P, k=2)[:, TPC * c:TPC * (c + 1), :])\
                .then_inc(yg_loaded[c], 16)
        ov = out.rearrange("b (t p) d -> p (b t) d", p=P)
        for t in range(0, NT, 4):
            sp.wait_ge(result_ready, t // 4 + 1)
            sp.dma_start(ov[:, t:t + 4, :], XS[:, t:t + 4, :]).then_inc(stored, 16)
        sp.wait_ge(stored, 16 * NT // 4)

    @block.gpsimd
    def _(pool):
        for u in range(GB):
            pool.memset(QG[u][:], 0.0)
            pool.memset(KM[u][:], 0.0)
        pool.memset(TM[:], 0.0)
        pool.memset(V[:, :, :, 2 * HD:VD], 1.0).then_inc(km_zeroed, 1)
        pool.wait_ge(km_zeroed, 1)
        for u in range(GB):
            for aa in range(4):
                ins = pool.memset(KM[u][RH * aa:RH * aa + MAXROW + 2, aa, :], 1.0)
        ins.then_inc(const_set, 1)
        pool.wait_ge(const_set, 2)
        for j in range(2 * NC):
            c, w = divmod(j, 2)
            pool.wait_ge(part1_ready, j + 1)
            pool.tensor_tensor(parts[:, w, 2, C * c:C * (c + 1)], ra[:, j % 4, :], parts[:, w, 1, C * c:C * (c + 1)],
                               ALU.subtract).then_inc(parts_ready, 1)
        pool.wait_ge(const_set, 2)
        pool.wait_ge(v_copied, NC)
        for g in range(GB):
            pool.tensor_copy(VG[g][:], V[:, :, 2 * g:2 * g + 2, :]).then_inc(vg_ready, 1)
        flat = orows.rearrange("r d -> (r d)").rearrange("(p c) -> p c", p=P)
        for b in range(EB):
            w = 2 * N // EB
            pool.dma_start(flat[:, w * b:w * (b + 1)], zeros).then_inc(y_scattered[b], 16)
        with pool.Fori(0, (NG - 1 - GB) // GB) as i:
            for u in range(GB):
                pool.wait_ge(pv_step, (i * GB + u) * STEPS + (STEPS + CREDIT))
                pool.tensor_copy(VG[u][:], V[:, :, bass.ds(2 * (i * GB + (GB + u)), 2), :]).then_inc(vg_ready, 1)
        pool.wait_ge(pv_step, (NG - GB) * STEPS + CREDIT)
        pool.tensor_copy(VG[0][:], V[:, :, 2 * (NG - 1):2 * NG, :]).then_inc(vg_ready, 1)

        pool.wait_ge(we_ready, 1)
        with pool.Fori(0, E0 // 2) as i:
            for u in range(2):
                pool.wait_ge(acc_done, i * 8 + (4 * u + 1))
                pool.tensor_copy(B1c[:, u, :], VC[:, bass.ds(8 * i + (R_B1A + 4 * u), 4)])
                pool.tensor_copy(WEc[:, u, :].unsqueeze(2),
                                 WE[:, :, bass.ds(2 * i + u, 1)]).then_inc(wec_ready, 1)

        pool.wait_ge(zeroed, 16)
        pool.wait_ge(xi_ready, 1)
        pool.wait_ge(idx_ready, 1)
        for t in range(NT):
            for k in range(2):
                pool.indirect_dma_start(
                    xslots[:, :], bass.IndirectOffsetOnAxis(ap=idx[:, t, k:k + 1].bitcast(U32), axis=0),
                    XI[:, t, k, :], None, bounds_check=SLOTS - 1, oob_is_err=False).then_inc(scattered, 16)

        with pool.Fori(0, E1 // EB) as i:
            for b in range(EB):
                pool.wait_ge(ye_taken, i * EB + (b + 3))
                pool.sem_inc(rows_weighed, 1)
                for r in range(CR):
                    pool.indirect_dma_start(
                        orows[:, :], bass.IndirectOffsetOnAxis(ap=oid[0:CP, b, r:r + 1].bitcast(U32), axis=0),
                        YE[0:CP, b, r, :], None, bounds_check=2 * N - 1, oob_is_err=False).then_inc(y_scattered[b], 16)

    @block.tensor
    def _(pe):
        pe.wait_ge(pv_zeroed, 1)
        pe.wait_ge(in_id, 16)
        for c in range(NC):
            pe.wait_ge(in_x[c], 16)
            for k in range(TPC):
                ins = pe.transpose(BK[c][:, P * k:P * (k + 1)], X[:, TPC * c + k, :], ident[:])
            ins.then_inc(xT_ready, 1)

        pe.wait_ge(w2_ready, 1)
        pe.wait_ge(xT_copied, NC)
        pe.sem_inc(pv_step, CREDIT)
        for j in range(2 * NC):
            c, w = divmod(j, 2)
            if j >= 4:
                pe.wait_ge(qk_taken, j - 3)
            for y in range(2):
                ins = pe.matmul(BK[2 * (j % 4) + y], wq2[:, 2 * w + y, :], XT[:, C * c:C * (c + 1)],
                                start=True, stop=True)
            ins.then_inc(qk_ready, 1)
        pe.wait_ge(in_wo, 32)
        for c in range(NC):
            pe.wait_ge(qk_taken, 2 * NC)
            for k in range(TPC):
                t = TPC * c + k
                ins = pe.matmul(BK[4 + c][:, P * k:P * (k + 1)], XT[:, P * t:P * (t + 1)], wqkv[:, 2, :],
                                start=True, stop=True)
            ins.then_inc(v_ready, 1)

        def max_scores(v, k, pos, g):
            qt, aa = divmod(k, 4)
            slot = (1 + pos) % 2
            pe.wait_ge(s_taken, use(g, pos) + 1)
            for h in range(2):
                ins = pe.matmul(SM[slot][:, C * h:C * (h + 1)], QG[v][:, P * qt:P * (qt + 1)],
                                KM[v][:, aa, C * h:C * (h + 1)], start=True, stop=True)
            ins.then_inc(s_ready, 1)

        def max_rows(g, pos):
            slot = (1 + pos) % 2
            pe.wait_ge(tm_ready, g + 2)
            pe.wait_ge(s_taken, use(g, pos) + 1)
            for qt in range(QT):
                ins = pe.matmul(SM[slot][:, P * qt:P * (qt + 1)], TM[:, qt, :, :].rearrange("p a r -> p (a r)"),
                                identb[:], start=True, stop=True)
            ins.then_inc(s_ready, 1)

        def turn_outputs(g, pos, phase):
            slot = (1 + pos) % 2
            pe.wait_ge(pv_evac, 2 * g + 1)
            pe.wait_ge(s_taken, use(phase, pos) + 1)
            for qt in range(QT):
                ins = pe.transpose(SM[slot][:, P * qt:P * (qt + 1)], PVs[:, P * qt:P * (qt + 1)], ident[:])
            ins.then_inc(s_ready, 1)

        def group(g, u, round_, last):
            v = (u + 1) % GB
            pos = 0
            if not last:
                pe.wait_ge(kq_loaded[v], 128 * (round_ + (1 if v else 2)))
            k = 0

            def scores(s, aa):
                half, kt = divmod(s, QT)
                pe.wait_ge(exp_done, g * (4 * STEPS) + (4 * s + aa + 1))
                if s == 0 and aa == 0:
                    pe.wait_ge(s_taken, use(g, 0) + 2)
                pe.matmul(ST[(u + s + aa) % 3][:], KM[u][:, aa, P * kt:P * (kt + 1)],
                          Q2[u][:, C * half:C * (half + 1)], start=True, stop=True).then_inc(st_ready, 1)

            def outputs(s):
                half, kt = divmod(s, QT)
                pe.wait_ge(exp_done, g * (4 * STEPS) + (4 * s + 4 + CREDIT))
                if s == 0:
                    pe.wait_ge(vg_ready, g + 1)
                if kt == 0:
                    pe.wait_ge(pv_evac, 2 * g + (1 + half))
                for aa in range(4):
                    ins = pe.matmul(PV[RH * aa:RH * aa + VD, :], VG[u][:, kt, aa // 2, :],
                                    E[(u + s) % 3][:, aa, :], start=(kt == 0), stop=(kt == QT - 1))
                ins.then_inc(pv_step, 1)

            for s in range(STEPS):
                todo = 0 if last else MAX_PER_STEP[s]
                if s == OUT_STEP:
                    turn_outputs(g, pos, g)
                    pos += 1
                scores(s, 0)
                scores(s, 1)
                if todo:
                    max_scores(v, k, pos, g)
                    k, pos, todo = k + 1, pos + 1, todo - 1
                scores(s, 2)
                if s:
                    outputs(s - 1)
                while todo:
                    max_scores(v, k, pos, g)
                    k, pos, todo = k + 1, pos + 1, todo - 1
                scores(s, 3)
            if not last:
                max_rows(g, pos)
            outputs(STEPS - 1)

        pe.wait_ge(kq_loaded[0], 128)
        for k in range(4 * QT):
            max_scores(0, k, k - 33 + 34, -1)
        max_rows(-1, 4 * QT + 1)
        pe.wait_ge(in_v, IN_V)
        pe.wait_ge(v_copied, NC)
        pe.transpose(BK[4][:, 0:R_N], VR[:], ident[0:R_N, 0:R_N]).then_inc(vec_ready, 1)
        pe.wait_ge(vec_copied, 1)
        with pe.Fori(0, (NG - 1) // GB) as i:
            for u in range(GB):
                group(i * GB + u, u, i, False)
        group(NG - 1, 0, None, True)
        turn_outputs(NG, 1, NG - 1)

        def turn(r, n, c, tile, bank):
            pe.wait_ge(tok_ready, NC * r + n + 1)
            for k in range(TPC):
                ins = pe.transpose(BK[bank][:, P * k:P * (k + 1)], tile(TPC * c + k), ident[:])
            ins.then_inc(tr_ready, 1)

        def project(n):
            pe.wait_ge(fm_ready, n + 1)
            c = SEQ_ORDER[n]
            for k in range(TPC):
                t = TPC * c + k
                ins = pe.matmul(BK[4 + c][:, P * k:P * (k + 1)], XT[:, P * t:P * (t + 1)], wo[:], start=True, stop=True)
            ins.then_inc(mo_ready, 1)

        for n, c in enumerate(SEQ_ORDER):
            turn(0, n, c, lambda t: TMP[:, P * (2 * (t % QT) + t // QT):P * (2 * (t % QT) + t // QT + 1)], c)
            if n:
                project(n - 1)
        project(NC - 1)

        def route0(n):
            pe.wait_ge(fm_ready, NC + n + 1)
            for k in range(TPC):
                t = TPC * SEQ_ORDER[n] + k
                ins = pe.matmul(BK[4][:, E0 * t:E0 * (t + 1)], XT[:, P * t:P * (t + 1)], wg0[:], start=True, stop=True)
            ins.then_inc(r0_ready, 1)

        pe.wait_ge(in_ffn, 16 * 4)
        for n, c in enumerate(SEQ_ORDER):
            turn(1, n, c, lambda t: XS[:, t, :], c)
            if n:
                route0(n - 1)
        route0(NC - 1)
        pe.wait_ge(we_ready, 1)
        for c in range(NC):
            for k in range(TPC):
                ins = pe.transpose(BK[c][0:E0, P * k:P * (k + 1)], WE[:, TPC * c + k, :], ident[:])
            ins.then_inc(wet_ready, 1)
        for c in range(NC):
            pe.wait_ge(wet_taken, c + 1)
            for k in range(TPC):
                t = TPC * c + k
                ins = pe.matmul(BK[4 + c][:, P * k:P * (k + 1)], WET[:, P * t:P * (t + 1)], b2[:], start=True, stop=True)
            ins.then_inc(mo_ready, 1)

        pe.wait_ge(mo_taken, 2 * NC)
        pe.sem_inc(y_ready, 2)
        with pe.Fori(0, E0 // 2) as i:
            def up0(u, c, f):
                j = 16 * u + 4 * c + f
                pe.wait_ge(g_done, i * 32 + (j + 1))
                for y, w in ((0, w1a), (1, w1b)):
                    ins = pe.matmul(BK[2 * (j % 2) + y], w[:, u, P * f:P * (f + 1)], XT[:, C * c:C * (c + 1)],
                                    start=True, stop=True)
                ins.then_inc(ab_ready, 1)

            def down0(n):
                u = n // 4
                pe.wait_ge(g_done, i * 32 + (4 * n + 6))
                pe.wait_ge(acc_done, i * 8 + (n + 4))
                for k in range(TPC):
                    for f in range(4):
                        ins = pe.matmul(BK[4 + n % 2][:, P * k:P * (k + 1)], G[:, n % 2, f, P * k:P * (k + 1)],
                                        w2[:, u, f, :], start=(f == 0), stop=(f == 3))
                ins.then_inc(y_ready, 1)

            for u in range(2):
                pe.wait_ge(w0_loaded[u], 48 * i + 48)
                for c in range(NC):
                    for f in range(4):
                        up0(u, c, f)
                        if f == 1 and (u or c):
                            down0(4 * u + c - 1)
            down0(7)

        pe.wait_ge(in_mix, 16 * 9)
        pe.wait_ge(cwm_ready, 1)
        for bank, src, n in ((4, cwm, 4), (5, w3, 3), (6, wb, 4), (7, wu, 4)):
            if bank < 6:
                pe.wait_ge(acc_done, 32 + 5)
            for j in range(n):
                ins = pe.transpose(BK[bank][:, P * j:P * (j + 1)], src[:, j, :], ident[:])
            ins.then_inc(tw_ready, 1)
        pe.wait_ge(tw_taken, 4)

        def conv(c):
            pe.wait_ge(fm_ready, 2 * NC + c + 1)
            for k in range(TPC):
                t = TPC * c + k
                for tap in range(4):
                    lo = P * (t % QT) + tap
                    ins = pe.matmul(BK[4 + c][:, P * k:P * (k + 1)], HT[:, t // QT, lo:lo + P], cwt[:, tap, :],
                                    start=(tap == 0), stop=(tap == 3))
            ins.then_inc(mo_ready, 1)

        for c in range(NC):
            turn(2, c, c, lambda t: XS[:, t, :], c)
            if c:
                conv(c - 1)
        conv(NC - 1)

        def qkv(c):
            pe.wait_ge(fm_ready, 3 * NC + c + 1)
            for w in range(3):
                j = 3 * c + w
                if j >= 4:
                    pe.wait_ge(qkv_taken, j - 3)
                else:
                    pe.wait_ge(mo_taken, 2 * NC + j + 1)
                pe.matmul(BK[4 + j % 4], w3t[:, w, :], XT[:, C * c:C * (c + 1)], start=True, stop=True)\
                    .then_inc(qkv_ready, 1)

        for c in range(NC):
            turn(3, c, c, lambda t: XS[:, t, :], c)
            if c:
                qkv(c - 1)
        qkv(NC - 1)
        for c in range(NC):
            pe.wait_ge(pool_done, c // 2 + 1)
            for k in range(TPC):
                t = TPC * c + k
                ins = pe.transpose(BK[c][:, P * k:P * (k + 1)], QF[:, P * t:P * (t + 1)], ident[:])
            ins.then_inc(mo_ready, 1)

        def boom_up(c, f):
            j = 4 * c + f
            pe.wait_ge(fm_ready, 4 * NC + c + 1)
            if j >= 4:
                pe.wait_ge(gelu_done, j - 3)
            else:
                pe.wait_ge(mo_taken, 3 * NC + j + 1)
            pe.matmul(BK[j % 4], wbt[:, f, :], XT[:, C * c:C * (c + 1)], start=True, stop=True).then_inc(up_ready, 1)

        def boom_down(c):
            pe.wait_ge(gelu_done, 4 * c + 4)
            for k in range(TPC):
                for f in range(4):
                    ins = pe.matmul(BK[4 + c][:, P * k:P * (k + 1)], G[:, c % 2, f, P * k:P * (k + 1)], wut[:, f, :],
                                    start=(f == 0), stop=(f == 3))
            ins.then_inc(mo_ready, 1)

        for c in range(NC):
            turn(4, c, c, lambda t: XS[:, t, :], 4 + c)
            if c >= 2:
                boom_up(0, 2 * c - 4)
                boom_up(0, 2 * c - 3)
        for c in range(1, NC):
            for f in range(4):
                boom_up(c, f)
            boom_down(c - 1)
        boom_down(NC - 1)

        def route1(c):
            pe.wait_ge(fm_ready, 5 * NC + c + 1)
            for k in range(TPC):
                t = TPC * c + k
                ins = pe.matmul(BK[4][:, E1 * t:E1 * (t + 1)], XT[:, P * t:P * (t + 1)], rw[:], start=True, stop=True)
            ins.then_inc(lg_ready, 1)

        pe.wait_ge(in_moe, 16 * 10)
        for c in range(NC):
            turn(5, c, c, lambda t: X[:, t, :], c)
            if c:
                route1(c - 1)
        route1(NC - 1)

        def up1(j, x, n, w):
            pe.wait_ge(h_done, j + 1)
            for y in range(2):
                ins = pe.matmul(BK[2 * (j_parity(j)) + y][0:FT, 0:n], w(y), x, start=True, stop=True)
            ins.then_inc(gu_ready, 1)

        def shared_down(c):
            pe.wait_ge(h_done, 2 * c + 4)
            pe.wait_ge(shared_taken, c + 1)
            for k in range(TPC):
                for f in range(2):
                    ins = pe.matmul(BK[4 + c % 2][:, P * k:P * (k + 1)], H[:, c % 2, f, P * k:P * (k + 1)],
                                    swd[:, f, :], start=(f == 0), stop=(f == 1))
            ins.then_inc(shared_ready, 1)

        def j_parity(j):
            return j % 2

        pe.wait_ge(sel_ready, 1)
        pe.matmul(BK[7][:, 0:E1 * NT], ltrib[:], selb[:].rearrange("p e t -> p (e t)"), start=True, stop=False)
        pe.matmul(BK[7][:, 0:E1 * NT], onesb[:], cumb[:].rearrange("p e t -> p (e t)"),
                  start=False, stop=True).then_inc(pos_ready, 1)
        for c in range(NC):
            for f in range(2):
                up1(2 * c + f, XT[:, C * c:C * (c + 1)], C, lambda y, f=f: swg[:, y, FT * f:FT * (f + 1)])
            if c:
                shared_down(c - 1)
        shared_down(NC - 1)

        def turn1(b, loads, e):
            pe.wait_ge(slots_loaded[b], loads)
            pe.wait_ge(xe_taken, e + 1)
            for r in range(CR):
                ins = pe.transpose(BK[6 + b % 2][:, CP * r:CP * (r + 1)], XE[0:CP, b, r, 0:P], ident[0:CP, 0:CP])
            ins.then_inc(xe_ready, 1)

        def gate_up1(b, loads, e):
            pe.wait_ge(w1_loaded[b], loads)
            pe.wait_ge(xe_taken, e + 3)
            for f in range(2):
                pe.wait_ge(h_done, e * 2 + (2 * NC + f + 1))
                for y in range(2):
                    ins = pe.matmul(BK[2 * f + y][0:FT, 0:CAPN], wg1[:, b, y, FT * f:FT * (f + 1)],
                                    XET[:, b % 2, :, :].rearrange("p r c -> p (r c)"), start=True, stop=True)
                ins.then_inc(gu_ready, 1)

        def down1(b, e):
            pe.wait_ge(h_done, e * 2 + (2 * NC + 4))
            pe.wait_ge(ye_taken, e + 1)
            for r in range(CR):
                for f in range(2):
                    ins = pe.matmul(BK[4 + b % 2][0:CP, P * r:P * (r + 1)], H[:, b % 2, f, CP * r:CP * (r + 1)],
                                    wd1[:, b, f, :], start=(f == 0), stop=(f == 1))
            ins.then_inc(ye_ready, 1)

        turn1(0, 16, 0)
        turn1(1, 16, 1)
        gate_up1(0, 48, 0)
        with pe.Fori(0, E1 // EB - 1) as i:
            for u in range(EB):
                b, e = (u + 1) % EB, i * EB + (u + 1)
                turn1((b + 1) % EB, 16 * i + (16 if u + 2 < EB else 32), e + 1)
                gate_up1(b, 48 * i + (48 if u + 1 < EB else 96), e)
                down1(u, e - 1)
        for e in range(E1 - EB + 1, E1):
            if e + 1 < E1:
                turn1((e + 1) % EB, 16 * E1 // EB, e + 1)
            gate_up1(e % EB, 48 * E1 // EB, e)
            down1((e - 1) % EB, e - 1)
        down1(EB - 1, E1 - 1)

    @block.scalar
    def _(act):
        chain = Chain(act, act_step)
        for c in range(NC):
            act.wait_ge(xT_ready, c + 1)
            act.copy(XT[:, C * c:C * (c + 1)], BK[c]).then_inc(xT_copied, 1)
        for j in range(2 * NC + 1):
            if j < 2 * NC:
                c, w = divmod(j, 2)
                act.wait_ge(rot_ready, j + 1)
                act.copy(parts[:, w, 0, C * c:C * (c + 1)], ra[:, j % 4, :]).then_inc(part0_ready, 1)
            if j:
                c, w = divmod(j - 1, 2)
                act.wait_ge(rest_ready, j)
                act.copy(parts[:, w, 1, C * c:C * (c + 1)], ra[:, (j - 1) % 4, :]).then_inc(part1_ready, 1)
        for c in range(NC):
            act.wait_ge(v_ready, c + 1)
            b, kt = c // 2, TPC * (c % 2)
            act.copy(V[:, kt:kt + TPC, NH * b:NH * (b + 1), 0:2 * HD],
                     BK[4 + c].rearrange("p (k h d) -> p k h d", k=TPC, h=NH)).then_inc(v_copied, 1)

        act.wait_ge(const_set, 2)
        act.wait_ge(lam_sum, 1)
        act.activation(lams[:, 2:4], lams[:, 0:2], ACT.Exp).then_inc(lam_exp, 1)
        act.wait_ge(vec_ready, 1)
        act.copy(VC[:], BK[4][:, 0:R_N]).then_inc(vec_copied, 1)
        act.sem_inc(exp_done, CREDIT)

        def evacuate(g, half):
            act.wait_ge(pv_step, g * STEPS + (QT * (half + 1) + CREDIT))
            act.copy(PVs[:, C * half:C * (half + 1)], PV[:]).then_inc(pv_evac, 1)

        def group(g, u, last):
            for s in range(STEPS):
                for aa in range(4):
                    act.wait_ge(st_ready, g * (4 * STEPS) + (4 * s + aa + 1))
                    if aa == 0:
                        act.wait_ge(pv_step, g * STEPS + (s + 1))
                    act.activation(E[(u + s) % 3][:, aa, :], ST[(u + s + aa) % 3][:], ACT.Exp).then_inc(exp_done, 1)
                if s == 0:
                    evacuate(g - 1, 1)
                if s == QT:
                    act.wait_ge(s_ready, g * 34 + (33 + OUT_POS + 1) if not last else use(NG - 1, 0) + 1)
                    evacuate(g, 0)

        with act.Fori(0, (NG - 1) // GB) as i:
            for u in range(GB):
                group(i * GB + u, u, False)
        group(NG - 1, 0, True)
        evacuate(NG - 1, 1)

        def turned(r, n, c, dst, scale=None, shift=None, bank0=0):
            act.wait_ge(tr_ready, NC * r + n + 1)
            if scale is None:
                ins = act.copy(dst(c), BK[bank0 + c])
            elif shift is None:
                ins = act.activation(dst(c), BK[bank0 + c], ACT.Copy, scale=scale)
            else:
                ins = act.activation(dst(c), BK[bank0 + c], ACT.Identity, scale=scale, bias=shift)
            ins.then_inc(fm_ready, 1)

        def xt(c):
            return XT[:, C * c:C * (c + 1)]

        calls = [1]

        def deviation(c, second=None):
            calls[0] += 1
            act.wait_ge(var_ready, calls[0])
            t = slice(TPC * c, TPC * (c + 1))
            if second is not None:
                e, bias = second
                act.activation(std[:, 1, t], mv[:, t, 1], ACT.Sqrt, bias=bias, scale=1.0 + e)
            act.activation(std[:, 0, t], mv[:, t, 1], ACT.Sqrt, bias=eps5[:]).then_inc(std_ready, 1)

        def norm_stage(r, order, dst, scale=None, shift=None, bank0=0, second=None, after=None):
            for n, c in enumerate(order):
                deviation(c, second)
                if n:
                    turned(r, n - 1, order[n - 1], dst, scale, shift, bank0)
                if n >= 2 and after is not None:
                    after(n - 2)
            turned(r, NC - 1, order[NC - 1], dst, scale, shift, bank0)
            if after is not None:
                after(NC - 2)
                after(NC - 1)

        act.wait_ge(var_ready, 1)
        act.activation(rden[:, 0:NT * NH], ssq[:], ACT.Sqrt, bias=eps5[:],
                       scale=1.0 / (2 * HD)).then_inc(std_ready, 1)
        for n, c in enumerate(SEQ_ORDER):
            turned(0, n, c, xt)
        norm_stage(1, SEQ_ORDER, xt, VC[:, R_LNW:R_LNW + 1], second=(EPS_FFN, epsf[:]))
        act.wait_ge(top_diff, 1)
        act.activation(top[:, 5, :], top[:, 4, :], ACT.Exp).then_inc(r0_exp, 1)
        for c in range(NC):
            act.wait_ge(wet_ready, c + 1)
            act.copy(WET[:, C * c:C * (c + 1)], BK[c][0:E0, :]).then_inc(wet_taken, 1)
        with act.Fori(0, E0 // 2) as i:
            for u in range(2):
                act.wait_ge(wec_ready, 2 * i + (u + 1))
                for c in range(NC):
                    for f in range(4):
                        j = 16 * u + 4 * c + f
                        act.wait_ge(ab_ready, i * 32 + (j + 1))
                        act.activation(gs[:, j % 2, :], BK[2 * (j % 2)], ACT.Silu,
                                       bias=B1c[:, u, f:f + 1]).then_inc(silu_done, 1)

        act.wait_ge(tw_ready, 4)
        for bank, dst, n in ((4, cwt, 4), (5, w3t, 3), (6, wbt, 4), (7, wut, 4)):
            act.copy(dst[:].rearrange("p j d -> p (j d)"), BK[bank][:, 0:P * n]).then_inc(tw_taken, 1)
        act.wait_ge(in_mix, 16 * 9)
        chunks = range(NC)
        norm_stage(2, chunks, lambda c: HT[:, c // 2, 3 + C * (c % 2):3 + C * (c % 2 + 1)],
                   VC[:, R_GB + 0:R_GB + 1], VC[:, R_GB + 1:R_GB + 2], second=(EPS, eps55[:]))
        def take_qkv(c):
            for w in range(3):
                j = 3 * c + w
                act.wait_ge(qkv_ready, j + 1)
                act.activation((QF, KF, VF)[w][:, C * c:C * (c + 1)], BK[4 + j % 4], ACT.Identity,
                               bias=VC[:, R_BQKV + w:R_BQKV + w + 1]).then_inc(qkv_taken, 1)

        norm_stage(3, chunks, xt, VC[:, R_GB + 2:R_GB + 3], VC[:, R_GB + 3:R_GB + 4], after=take_qkv)
        norm_stage(4, chunks, xt, VC[:, R_GB + 4:R_GB + 5], VC[:, R_GB + 5:R_GB + 6], 4)
        for c in range(NC):
            if c >= 2:
                act.wait_ge(mo_ready, 4 * NC + c - 1)
            for f in range(4):
                j = 4 * c + f
                act.wait_ge(up_ready, j + 1)
                act.activation(G[:, c % 2, f, :], BK[j % 4], ACT.Gelu, bias=VC[:, R_BB + f:R_BB + f + 1]).then_inc(gelu_done, 1)
        norm_stage(5, chunks, xt)
        act.sem_inc(xe_taken, 2)
        act.sem_inc(ye_taken, 2)
        act.wait_ge(prob_sub, 1)
        act.activation(Lb[:], La[:], ACT.Exp).then_inc(prob_exp, 1)
        for k in range(2):
            ins = act.copy(XI[:, :, k, 0:P], X[:])
        ins.then_inc(xi_ready, 1)
        for j in range(2 * NC):
            act.wait_ge(gu_ready, j + 1)
            act.activation(HS[:, j % 2, :], BK[2 * (j % 2)][0:FT, :], ACT.Silu).then_inc(h_silu, 1)

        def silu1(e):
            for f in range(2):
                act.wait_ge(gu_ready, e * 2 + (2 * NC + f + 1))
                act.activation(HS[:, f, 0:CAPN], BK[2 * f][0:FT, 0:CAPN], ACT.Silu).then_inc(h_silu, 1)

        def weigh1(b, uses, e):
            act.wait_ge(ye_ready, e + 1)
            act.wait_ge(y_scattered[b], uses * (16 * CR) + 16)
            for r in range(CR):
                ins = act.activation(YE[0:CP, b, r, :], BK[4 + b % 2][0:CP, P * r:P * (r + 1)], ACT.Copy,
                                     scale=slotw[0:CP, b, r:r + 1])
            ins.then_inc(ye_taken, 1)

        silu1(0)
        with act.Fori(0, E1 // EB - 1) as i:
            for u in range(EB):
                silu1(i * EB + (u + 1))
                weigh1(u, i, i * EB + u)
        for e in range(E1 - EB + 1, E1):
            silu1(e)
            weigh1((e - 1) % EB, (e - 1) // EB, e - 1)
        weigh1(EB - 1, E1 // EB - 1, E1 - 1)
        for c in range(NC):
            deviation(c)

    @block.vector
    def _(dve):
        chain = Chain(dve, dve_step)
        dve.memset(PV[:], 0.0).then_inc(pv_zeroed, 1)
        dve.wait_ge(in_w, 16 * 2)
        for w in range(2):
            scale = HD ** -0.5 if w == 0 else 1.0
            dve.tensor_scalar(wq2[:, 2 * w, :], wqkv[:, w, :], scale, None, ALU.mult)
            src = wqkv[:, w, :].rearrange("p (h t) -> p h t", t=2)
            dst = wq2[:, 2 * w + 1, :].rearrange("p (h t) -> p h t", t=2)
            for t in range(2):
                ins = dve.tensor_scalar(dst[:, :, t], src[:, :, 1 - t], scale, None, ALU.mult)
        ins.then_inc(w2_ready, 1)
        dve.wait_ge(in_id, 16)
        dve.tensor_copy(identb[:], ident[:])
        dve.memset(PVs[:], 0.0)
        chain(dve.memset(XS[:], 0.0))
        dve.memset(empty.rearrange("p (r w) -> p r w", r=CR)[:, :, P + 1], float(FAR))
        dve.memset(eps5[:], EPS)
        dve.memset(eps55[:], EPS * EPS)
        dve.memset(epsf[:], EPS_FFN * EPS).then_inc(const_set, 1)

        dve.wait_ge(in_tab, 32)
        for j in range(2 * NC + 1):
            if j < 2 * NC:
                c = j // 2
                tab = slice(C * (c % 2), C * (c % 2 + 1))
                r, q = ra[:, j % 4, :], rb[:, j % 2, :]
                dve.wait_ge(qk_ready, j + 1)
                if j >= 4:
                    dve.wait_ge(parts_ready, j - 3)
                dve.tensor_tensor(r, BK[2 * (j % 4)], cosT[:, tab], ALU.mult)
                dve.tensor_tensor(q, BK[2 * (j % 4) + 1], sinT[:, tab], ALU.mult).then_inc(qk_taken, 1)
                dve.wait_ge(qk_taken, j + 1)
                dve.tensor_tensor(r, r, q, ALU.add).then_inc(rot_ready, 1)
            if j:
                c, w = divmod(j - 1, 2)
                r = ra[:, (j - 1) % 4, :]
                dve.wait_ge(part0_ready, j)
                dve.tensor_tensor(r, r, parts[:, w, 0, C * c:C * (c + 1)], ALU.subtract).then_inc(rest_ready, 1)

        dve.sem_inc(s_taken, 2)

        def lambda_and_wo():
            dve.wait_ge(in_v, IN_V)
            for j in range(2):
                ins = dve.tensor_tensor(lamp[:, j, :], lamv[:, 2 * j, :], lamv[:, 2 * j + 1, :], ALU.mult)
            chain(ins)
            dve.reduce_sum(lams[:, 0:2], lamp[:], AX).then_inc(lam_sum, 1)
            dve.wait_ge(vec_copied, 1)
            chain(dve.tensor_scalar(gfac[:], VC[:, R_SUBLN:R_SUBLN + 1], 1.0 - LAMBDA_INIT, None, ALU.mult))
            dve.wait_ge(in_wo, 32)
            dve.tensor_scalar(wo[:], wqkv[:, 3, :], gfac[:], None, ALU.mult)
            dve.wait_ge(lam_exp, 1)
            chain(dve.scalar_tensor_tensor(lams[:, 4:5], lams[:, 3:4], -LAMBDA_INIT, lams[:, 2:3],
                                           ALU.add, ALU.subtract))

        def take_max(v, k, pos, g):
            qt, aa = divmod(k, 4)
            dve.wait_ge(s_ready, use(g, pos) + 1)
            dve.reduce_max(mx[v][:, qt, aa:aa + 1], SM[(1 + pos) % 2][:], AX).then_inc(s_taken, 1)

        def take_rows(g, v, pos):
            dve.wait_ge(s_taken, use(g, pos) + 2)
            dve.tensor_scalar(TM[:, :, :, MAXROW], mx[v][:], -1.0, None, ALU.mult).then_inc(m_hi, 1)
            dve.wait_ge(m_hi, g + 2)
            dve.scalar_tensor_tensor(TM[:, :, :, MAXROW + 1], mx[v][:], -1.0, TM[:, :, :, MAXROW],
                                     ALU.mult, ALU.subtract).then_inc(tm_ready, 1)
            dve.wait_ge(s_ready, use(g, pos) + 1)
            dve.tensor_tensor(Q2[v][:], SM[(1 + pos) % 2][:], QG[v][:], ALU.add).then_inc(s_taken, 1)

        def take_outputs(g, pos, phase):
            dve.wait_ge(s_ready, use(phase, pos) + 1)
            dve.tensor_copy(OT[:, :, bass.ds(g, 1), :, :].rearrange("p q g a v -> p q (g a) v"),
                            SM[(1 + pos) % 2][:].rearrange("p (q a r) -> p q a r", q=QT, a=4)[:, :, :, 0:VD])\
                .then_inc(s_taken, 1)

        def group(g, u):
            v, k, pos = (u + 1) % GB, 0, 0
            for s in range(STEPS):
                if s == OUT_STEP:
                    take_outputs(g, pos, g)
                    pos += 1
                for _ in range(MAX_PER_STEP[s]):
                    take_max(v, k, pos, g)
                    k, pos = k + 1, pos + 1
            take_rows(g, v, pos)

        dve.wait_ge(kq_loaded[0], 128)
        for k in range(4 * QT):
            take_max(0, k, k + 1, -1)
        take_rows(-1, 0, 4 * QT + 1)
        lambda_and_wo()
        with dve.Fori(0, (NG - 1) // GB) as i:
            for u in range(GB):
                dve.wait_ge(kq_loaded[(u + 1) % GB], 128 * (i + (1 if (u + 1) % GB else 2)))
                group(i * GB + u, u)
        take_outputs(NG - 1, 0, NG - 1)

        def weigh_heads(lo, hi):
            o = OT[:, :, 1 + lo:1 + hi, :, :].rearrange("p q g a v -> p q (g a) v")
            rv = rden[:].rearrange("p (q m) -> p q m", q=QT)[:, :, 4 * lo:4 * hi]
            chain(dve.reciprocal(rv, o[:, :, :, 2 * HD]))
            r2 = rv.rearrange("p q (m s) -> p q m s", s=2)[:, :, :, 1]
            chain(dve.tensor_scalar(r2, r2, lams[:, 4:5], None, ALU.mult))
            nr = NRM.rearrange("p (q m d) -> p q m d", q=QT, d=8)[:, :, 4 * lo:4 * hi, :]
            chain(dve.tensor_tensor(nr, o[:, :, :, 0:2 * HD],
                                    rv.unsqueeze(3).to_broadcast([P, QT, 4 * (hi - lo), 8]), ALU.mult))
            n2 = nr.rearrange("p q (m s) d -> p q m s d", s=2)
            A = TMP[:].rearrange("p (q m d) -> p q m d", q=QT, d=8)[:, :, 2 * lo:2 * hi, :]
            chain(dve.tensor_tensor(A, n2[:, :, :, 0, :], n2[:, :, :, 1, :], ALU.add))
            chain(dve.tensor_tensor(n2[:, :, :, 0, :], A, A, ALU.mult))
            return dve.reduce_sum(ssq[:].rearrange("p (q m) -> p q m", q=QT)[:, :, 2 * lo:2 * hi],
                                  n2[:, :, :, 0, :], AX)

        dve.wait_ge(s_taken, use(NG - 1, 0) + 3)
        weigh_heads(0, NG - 1)
        take_outputs(NG, 1, NG - 1)
        dve.wait_ge(s_taken, use(NG - 1, 1) + 3)
        weigh_heads(NG - 1, NG).then_inc(var_ready, 1)
        dve.wait_ge(std_ready, 1)
        rms = rden[:, NT * NH:2 * NT * NH]
        chain(dve.reciprocal(rms, rden[:, 0:NT * NH]))
        for h in range(2):
            m = slice(NT * NH // 2 * h, NT * NH // 2 * (h + 1))
            A = TMP[:].rearrange("p (m d) -> p m d", d=8)[:, m, :]
            chain(dve.tensor_tensor(A, A, rms[:, m].unsqueeze(2).to_broadcast([P, NT * NH // 2, 8]), ALU.mult))
            dve.sem_inc(tok_ready, 2)

        norms = [1]

        def tiles(c):
            return range(TPC * c, TPC * (c + 1))

        def norm(src, outs, order, prepare=None, double=False):
            def begin(c):
                if prepare is not None:
                    prepare(c)
                for t in tiles(c):
                    ins = dve.bn_stats(stats[:, t, :], src[:, t, :])
                chain(ins)
                for t in tiles(c):
                    ins = dve.bn_aggr(mv[:, t, :], stats[:, t, :])
                ins.then_inc(var_ready, 1)

            def finish(c):
                norms[0] += 1
                dve.wait_ge(std_ready, norms[0])
                ts = slice(TPC * c, TPC * (c + 1))
                w = 2 if double else 1
                chain(dve.reciprocal(rstd[:, 0:w, ts], std[:, 0:w, ts]))
                for dst, which, signal in outs:
                    for t in tiles(c):
                        ins = dve.tensor_scalar(dst[:, t, :], src[:, t, :], mv[:, t, 0:1], rstd[:, which, t:t + 1],
                                                ALU.subtract, ALU.mult)
                    if signal is None:
                        chain(ins)
                    else:
                        ins.then_inc(signal, 1)

            for n, c in enumerate(order):
                begin(c)
                if n:
                    finish(order[n - 1])
            finish(order[NC - 1])

        def add_chunk(dst, src, n, c, bank):
            dve.wait_ge(mo_ready, n + 1)
            dve.tensor_tensor(dst[:, TPC * c:TPC * (c + 1), :], BK[bank].rearrange("p (k d) -> p k d", d=P),
                              src[:, TPC * c:TPC * (c + 1), :], ALU.add).then_inc(mo_taken, 1)
            dve.wait_ge(mo_taken, n + 1)

        def row(v_, n=NT):
            return v_.unsqueeze(1).to_broadcast([P, n, v_.shape[-1]])

        def each(v_, e):
            return v_.unsqueeze(2).to_broadcast([P, NT, e])

        def top2(L, rev, sa_, sb_, e):
            src = L
            for k in range(2):
                chain(dve.tensor_reduce(top[:, 2 * k, :], src, AX, ALU.max))
                chain(dve.tensor_tensor(sa_, src, each(top[:, 2 * k, :], e), ALU.is_equal))
                chain(dve.tensor_tensor(sa_, sa_, row(rev), ALU.mult))
                chain(dve.tensor_reduce(top[:, 2 * k + 1, :], sa_, AX, ALU.max))
                chain(dve.tensor_tensor(oh[:, k, :, 0:e], sa_, each(top[:, 2 * k + 1, :], e), ALU.is_equal))
                if k == 0:
                    chain(dve.scalar_tensor_tensor(sb_, oh[:, 0, :, 0:e], -3.0e38, L, ALU.mult, ALU.add))
                    src = sb_

        dve.wait_ge(zeroed, 16)
        for b in range(EB):
            dve.wait_ge(y_scattered[b], 16)
        norm(X, [(XS, 1, tok_ready), (X, 0, None)], SEQ_ORDER,
             lambda c: add_chunk(X, X, SEQ_ORDER.index(c), c, 4 + c), True)

        dve.wait_ge(r0_ready, NC)
        chain(dve.tensor_tensor(L0[:], BK[4][:, 0:NT * E0].rearrange("p (t e) -> p t e", e=E0), row(bg0[:]), ALU.add))
        top2(L0[:], rev0[:], La[:, :, 0:E0], Lb[:, :, 0:E0], E0)
        dve.tensor_tensor(top[:, 4, :], top[:, 2, :], top[:, 0, :], ALU.subtract).then_inc(top_diff, 1)
        dve.wait_ge(r0_exp, 1)
        chain(dve.tensor_scalar(top[:, 6, :], top[:, 5, :], 1.0, None, ALU.add))
        chain(dve.reciprocal(top[:, 7, :], top[:, 6, :]))
        chain(dve.tensor_tensor(top[:, 6, :], top[:, 7, :], top[:, 5, :], ALU.mult))
        dve.tensor_tensor(La[:, :, 0:E0], oh[:, 0, :, 0:E0], each(top[:, 7, :], E0), ALU.mult)
        chain(dve.tensor_tensor(Lb[:, :, 0:E0], oh[:, 1, :, 0:E0], each(top[:, 6, :], E0), ALU.mult))
        dve.tensor_tensor(WE[:], La[:, :, 0:E0], Lb[:, :, 0:E0], ALU.add).then_inc(we_ready, 1)
        for c in range(NC):
            add_chunk(X, X, NC + c, c, 4 + c)
        dve.sem_inc(g_done, 2)
        dve.sem_inc(acc_done, 5)

        with dve.Fori(0, E0 // 2) as i:
            def gate0(u, c, f):
                j = 16 * u + 4 * c + f
                dve.wait_ge(silu_done, i * 32 + (j + 1))
                if f == 0:
                    dve.wait_ge(y_ready, i * 8 + (4 * u + c + 1))
                dve.scalar_tensor_tensor(G[:, c % 2, f, :], BK[2 * (j % 2) + 1], VC[:, bass.ds(8 * i + (R_B1B + 4 * u + f), 1)],
                                         gs[:, j % 2, :], ALU.add, ALU.mult).then_inc(g_done, 1)

            def sum0(n):
                u, c = divmod(n, 4)
                dve.wait_ge(y_ready, i * 8 + (n + 3))
                dve.wait_ge(acc_done, i * 8 + (n + 2))
                dve.wait_ge(wec_ready, 2 * i + (u + 1))
                for k in range(TPC):
                    t = TPC * c + k
                    ins = dve.scalar_tensor_tensor(X[:, t, :], BK[4 + n % 2][:, P * k:P * (k + 1)],
                                                   WEc[:, u, t:t + 1], X[:, t, :], ALU.mult, ALU.add)
                ins.then_inc(acc_done, 1)

            for u in range(2):
                for c in range(NC):
                    for f in range(4):
                        gate0(u, c, f)
                    if u or c:
                        sum0(4 * u + c - 1)
            sum0(7)

        dve.wait_ge(acc_done, 32 + 5)
        dve.memset(HT[:, :, 0:3], 0.0)
        dve.memset(onesS[:], 1.0)
        dve.memset(onesb[:], 1.0)
        chain(dve.memset(cwm[:], 0.0))
        dve.wait_ge(in_mix, 16 * 9)
        for q in range(4):
            r = slice(32 * q, 32 * (q + 1))
            ins = dve.tensor_copy(cwm[r, :, r], cw[r, :, :].rearrange("p i t -> p t i"))
        ins.then_inc(cwm_ready, 1)
        norm(X, [(XS, 1, tok_ready), (X, 0, None)], range(NC), None, True)
        chain(dve.tensor_tensor(X0[:], X[:], row(rows[:, 0, :]), ALU.add))
        norm(X0, [(XS, 0, tok_ready)], range(NC), lambda c: add_chunk(X0, X0, 2 * NC + c, c, 4 + c))
        for b in range(NB):
            r = slice(S * b, S * (b + 1))
            dve.wait_ge(qkv_taken, 6 * (b + 1))
            chain(dve.tensor_tensor_scan(TMP[:, r], onesS[:], QF[:, r], 0.0, ALU.mult, ALU.add))
            chain(dve.tensor_tensor(TMP[:, r], TMP[:, r], invp[:], ALU.mult))
            chain(dve.tensor_tensor(TMP[:, r], TMP[:, r], KF[:, r], ALU.mult))
            chain(dve.tensor_tensor_scan(QF[:, r], onesS[:], TMP[:, r], 0.0, ALU.mult, ALU.add))
            chain(dve.tensor_tensor(QF[:, r], QF[:, r], invp[:], ALU.mult))
            dve.tensor_tensor(QF[:, r], QF[:, r], VF[:, r], ALU.mult).then_inc(pool_done, 1)
        norm(X0, [(XS, 0, tok_ready)], range(NC), lambda c: add_chunk(X0, X0, 3 * NC + c, c, c))
        chain(dve.tensor_tensor(X[:], X[:], X0[:], ALU.add))
        chain(dve.tensor_tensor(X[:], X[:], row(rows[:, 1, :]), ALU.add))
        norm(X, [(X, 0, tok_ready)], range(NC), lambda c: add_chunk(X, X, 4 * NC + c, c, 4 + c))

        dve.wait_ge(in_moe, 16 * 10)
        dve.wait_ge(lg_ready, NC)
        chain(dve.tensor_tensor(La[:], BK[4][:, 0:NT * E1].rearrange("p (t e) -> p t e", e=E1), row(rbb[:]), ALU.add))
        chain(dve.tensor_reduce(top[:, 0, :], La[:], AX, ALU.max))
        dve.tensor_tensor(La[:], La[:], each(top[:, 0, :], E1), ALU.subtract).then_inc(prob_sub, 1)
        dve.wait_ge(prob_exp, 1)
        chain(dve.reduce_sum(top[:, 1, :], Lb[:], AX))
        chain(dve.reciprocal(top[:, 2, :], top[:, 1, :]))
        chain(dve.tensor_tensor(La[:], Lb[:], each(top[:, 2, :], E1), ALU.mult))
        top2(La[:], rev1[:], prod[:], Lb[:], E1)
        chain(dve.tensor_tensor(self_[:].rearrange("p e t -> p t e"), oh[:, 0], oh[:, 1], ALU.add))
        chain(dve.tensor_tensor_scan(cumf[:].rearrange("p e t -> p (e t)"), seg[:],
                                     self_[:].rearrange("p e t -> p (e t)"), 0.0, ALU.mult, ALU.add))
        dve.tensor_copy(selb[:], self_[:])
        dve.tensor_copy(ltrib[:], ltri[:])
        dve.tensor_tensor(cumb[:], cumf[:], self_[:], ALU.subtract).then_inc(sel_ready, 1)
        chain(dve.tensor_tensor(top[:, 4, :], top[:, 0, :], top[:, 2, :], ALU.add))
        chain(dve.tensor_scalar(top[:, 4, :], top[:, 4, :], 1e-9, None, ALU.add))
        chain(dve.reciprocal(top[:, 5, :], top[:, 4, :]))
        dve.tensor_tensor(XI[:, :, 0, P], top[:, 0, :], top[:, 5, :], ALU.mult)
        dve.tensor_tensor(XI[:, :, 1, P], top[:, 2, :], top[:, 5, :], ALU.mult)
        dve.tensor_copy(XI[:, :, :, P + 1], rowid[:])

        dve.sem_inc(h_done, 2)

        dve.wait_ge(pos_ready, 1)
        pos = BK[7][:, 0:E1 * NT].rearrange("p (e t) -> p t e", e=E1)
        dve.tensor_scalar(posx[:, 1], pos, float(CAP), None, ALU.is_ge)
        chain(dve.tensor_tensor(posx[:, 0], pos, row(base1[:]), ALU.add))
        chain(dve.scalar_tensor_tensor(posx[:, 0], posx[:, 1], float(FAR), posx[:, 0], ALU.mult, ALU.add))
        for k in range(2):
            chain(dve.tensor_tensor(prod[:], posx[:, 0], oh[:, k], ALU.mult))
            chain(dve.reduce_sum(fidx[:, k, :], prod[:], AX))
        dve.tensor_copy(idx[:].rearrange("p t k -> p k t"), fidx[:]).then_inc(idx_ready, 1)

        def gate_shared(c, f):
            j = 2 * c + f
            dve.wait_ge(h_silu, j + 1)
            if c >= 2 and f == 0:
                dve.wait_ge(shared_ready, c - 1)
            dve.tensor_tensor(H[:, c % 2, f, :], HS[:, f, :], BK[2 * f + 1][0:FT, :], ALU.mult).then_inc(h_done, 1)

        def shared_out(c):
            dve.wait_ge(shared_ready, c + 1)
            dve.tensor_tensor(XS[:, TPC * c:TPC * (c + 1), :], BK[4 + c % 2].rearrange("p (k d) -> p k d", d=P),
                              XS[:, TPC * c:TPC * (c + 1), :], ALU.add).then_inc(shared_taken, 1)

        dve.sem_inc(shared_taken, 2)
        chain(dve.tensor_scalar(XS[:], X[:], 2.0, None, ALU.mult))
        for c in range(NC):
            for f in range(2):
                gate_shared(c, f)
            if c:
                shared_out(c - 1)
        shared_out(NC - 1)

        def take_tokens1(b, e):
            dve.wait_ge(xe_ready, e + 1)
            dve.tensor_copy(XET[:, b % 2, :, :].rearrange("p r c -> p (r c)"), BK[6 + b % 2][:, 0:CAPN]).then_inc(xe_taken, 1)

        def gate1(b, uses, e):
            dve.wait_ge(y_scattered[b], uses * (16 * CR) + 16)
            dve.tensor_copy(oid[0:CP, b, :], XE[0:CP, b, :, P + 1])
            dve.tensor_copy(slotw[0:CP, b, :], XE[0:CP, b, :, P])
            for f in range(2):
                dve.wait_ge(h_silu, e * 2 + (2 * NC + f + 1))
                if f == 0:
                    dve.wait_ge(ye_taken, e + 1)
                dve.tensor_tensor(H[:, b % 2, f, 0:CAPN], HS[:, f, 0:CAPN], BK[2 * f + 1][0:FT, 0:CAPN],
                                  ALU.mult).then_inc(h_done, 1)

        take_tokens1(0, 0)
        take_tokens1(1, 1)
        gate1(0, 0, 0)
        with dve.Fori(0, E1 // EB - 1) as i:
            for u in range(EB):
                b, e = (u + 1) % EB, i * EB + (u + 1)
                take_tokens1((b + 1) % EB, e + 1)
                gate1(b, i if u + 1 < EB else i + 1, e)
        for e in range(E1 - EB + 1, E1):
            if e + 1 < E1:
                take_tokens1((e + 1) % EB, e + 1)
            gate1(e % EB, e // EB, e)

        def add_rows(c):
            dve.wait_ge(yg_loaded[c], 16)
            t = slice(TPC * c, TPC * (c + 1))
            for k in range(2):
                chain(dve.tensor_tensor(XS[:, t, :], YG[:, t, k, :], XS[:, t, :], ALU.add))

        norm(XS, [(XS, 0, result_ready)], range(NC), add_rows)


_NAMES = {
    "x": "L0_attn_x", "Wq": "L0_attn_Wq", "Wk": "L0_attn_Wk", "Wv": "L0_attn_Wv", "Wo": "L0_attn_Wo",
    "lq1": "L0_attn_lambda_q1", "lk1": "L0_attn_lambda_k1", "lq2": "L0_attn_lambda_q2", "lk2": "L0_attn_lambda_k2",
    "subln_g": "L0_attn_subln_g", "ln_w": "L0_ffn_ln_w", "Wg": "L0_ffn_Wg", "bg": "L0_ffn_bg",
    "W1a": "L0_ffn_W1a", "b1a": "L0_ffn_b1a", "W1b": "L0_ffn_W1b", "b1b": "L0_ffn_b1b", "W2": "L0_ffn_W2",
    "b2": "L0_ffn_b2", "ln_attn_g": "L1_attn_ln_attn_g", "ln_attn_b": "L1_attn_ln_attn_b", "mWq": "L1_attn_Wq",
    "bq": "L1_attn_bq", "mWk": "L1_attn_Wk", "bk": "L1_attn_bk", "mWv": "L1_attn_Wv", "bv": "L1_attn_bv",
    "ln_conv_g": "L1_attn_ln_conv_g", "ln_conv_b": "L1_attn_ln_conv_b", "conv_w": "L1_attn_conv_w",
    "conv_b": "L1_attn_conv_b", "ln_boom_g": "L1_attn_ln_boom_g", "ln_boom_b": "L1_attn_ln_boom_b",
    "Wb": "L1_attn_Wb", "bb": "L1_attn_bb", "Wu": "L1_attn_Wu", "bu": "L1_attn_bu",
    "router_w": "L1_ffn_router_w", "router_b": "L1_ffn_router_b", "w_gate": "L1_ffn_w_gate",
    "w_up": "L1_ffn_w_up", "w_down": "L1_ffn_w_down", "sw_gate": "L1_ffn_sw_gate", "sw_up": "L1_ffn_sw_up",
    "sw_down": "L1_ffn_sw_down",
}


def _constants(np):
    f = np.float32
    d = np.arange(P) % HD
    freq = f(1.0) / f(0.0001) ** (f(2.0) * np.arange(HD // 2, dtype=f) / f(HD))
    angle = np.arange(S, dtype=f)[None, :] * freq[d // 2][:, None]
    sign = np.where(d % 2 == 0, f(-1.0), f(1.0))[:, None]
    return {
        "ident": np.eye(P, dtype=f),
        "cos": np.cos(angle.astype(np.float64)).astype(f),
        "sin": np.sin(angle.astype(np.float64)).astype(f) * sign,
        "rev0": np.arange(E0, 0, -1).astype(f),
        "rev1": np.arange(E1, 0, -1).astype(f),
        "base1": (np.arange(E1) * CAPS).astype(f),
        "rowid": (2 * (np.arange(P)[:, None, None] + P * np.arange(NT)[None, :, None])
                  + np.arange(2)[None, None, :]).astype(f),
        "seg": np.tile((np.arange(NT) > 0).astype(f), E1),
        "ltri": np.triu(np.ones((P, P), f), 1),
        "invp": f(1.0) / np.arange(1, S + 1, dtype=f),
    }


def kernel(**inputs):
    import numpy as _np
    import concourse.bacc as _bacc
    from concourse import mybir as _mybir
    from concourse.bass_utils import run_bass_kernel_spmd as _run

    nc = _bacc.Bacc("TRN2", target_bir_lowering=False, num_devices=1)
    arrays, aps = {}, {}
    given = {short: _np.ascontiguousarray(inputs[name]) for short, name in _NAMES.items()}
    for name, v in {**given, **_constants(_np)}.items():
        arrays[f"in_{name}"] = v
        aps[name] = nc.dram_tensor(f"in_{name}", v.shape, _mybir.dt.from_np(v.dtype), kind="ExternalInput").ap()
    out = nc.dram_tensor("out", (NB, S, P), F32, kind="ExternalOutput").ap()
    build(nc, aps, out)
    r = _run(nc, [arrays], core_ids=[0])
    return r.results[0]["out"]
```

```python
import math
from contextlib import ExitStack

import concourse.bass as bass
from concourse import mybir

F32 = mybir.dt.float32
BF16 = mybir.dt.bfloat16
I32 = mybir.dt.int32
U32 = mybir.dt.uint32
ALU = mybir.AluOpType
ACT = mybir.ActivationFunctionType
AX = mybir.AxisListType.X

P = 128
NB, S = 2, 1024
N = NB * S
NT = N // P
QT = S // P
C = 512
NC = N // C
TPC = C // P

NH, HD = 16, 4
VD = 2 * HD + 1
NG = NB * 8
GB = 3
RH = 32
NBLK = 6
BLOCKS = ((slice(2, 5), slice(1, 6, 4), slice(0, 1)),
          (slice(0, 3), slice(3, 6, 2), slice(4, 5)))
MAXROW = HD * NBLK
EPS = 1e-5
LAMBDA_INIT = 0.8 - 0.6 * math.exp(-0.3 * 12)
FAR = 1 << 20
EPS_FFN = 1.1920928955078125e-07
CREDIT = 3
STEPS = 16
OUT_STEP = 2
EARLY = 4
PLAN = [[("next", EARLY + 2 * s + j) for j in range(2)] for s in range(STEPS - 2)] + [
    [("after", 0), ("after", 1)], [("rows", None), ("after", 2), ("after", 3)]]
OUT_POS = sum(len(PLAN[s]) for s in range(OUT_STEP))
USES = 4 * 8 + 2
FIRST = USES - 1 + EARLY

E0, F0 = 8, 512
T0 = (2 * N + E0 * (P - 1)) // P
XB = 4
R0 = E0 * N // P
PEEL = 2
PASSES = (T0 - PEEL - 1) // 4
assert T0 == PEEL + 4 * PASSES + 1
E1, F1 = 16, 176
FT = F1 // 2
CAP = 320
CR = 3
CP = -(-CAP // CR)
CAPN = CP * CR
CAPS = CR * P
SLOTS = E1 * CAPS
RW = P + 1
EB = 4

R_B1A, R_B1B, R_BB, R_BQKV = 0, 4 * E0, 8 * E0, 8 * E0 + 4
R_GB = R_BQKV + 3
R_LNW, R_SUBLN = R_GB + 6, R_GB + 7
R_N = R_SUBLN + 1
IN_V = 16 * (4 + 1 + 2 + 1 + 10)


def build(nc, a, out):
    with ExitStack() as ctx:
        program(nc, ctx, a, out)


def program(nc, ctx, a, out):
    def sb(name, shape, dt=F32):
        return ctx.enter_context(nc.sbuf_tensor(name, shape, dt))

    def sem(name):
        return ctx.enter_context(nc.semaphore(name))

    ident = sb("ident", [P, P])
    identb = sb("identb", [P, P], BF16)
    eps5 = sb("eps5", [P, 1])
    epsf = sb("epsf", [P, 1])
    eps55 = sb("eps55", [P, 1])
    X = sb("X", [P, NT, P])
    XS = sb("XS", [P, NT, P])
    empty = XS[:].rearrange("p t d -> p (t d)")[:, 0:CR * RW]
    zeros = XS[:].rearrange("p t d -> p (t d)")[:, N - 2 * N // 4:N]
    XT = sb("XT", [P, N])
    TMP = sb("TMP", [P, N])
    stats = sb("stats", [P, NT, 6])
    mv = sb("mv", [P, NT, 2])
    std = sb("std", [P, 2, NT])
    rstd = sb("rstd", [P, 2, NT])
    shift = sb("shift", [P, NT])
    wqkv = sb("wqkv", [P, 4, P])
    lamv = sb("lamv", [P, 4, HD])
    lamp = sb("lamp", [P, 2, HD])
    lams = sb("lams", [P, 8])
    gfac = sb("gfac", [P, 1])
    VR = sb("VR", [R_N, P])
    VC = sb("VC", [P, R_N])
    wo = sb("wo", [P, P])

    wg0 = sb("wg0", [P, E0])
    bg0 = sb("bg0", [P, E0])
    b2 = sb("b2", [E0, P])
    rev0 = sb("rev0", [P, E0])
    cw = sb("cw", [P, 32, 4])
    w3 = sb("w3", [P, 3, P])
    wb = sb("wb", [P, 4, P])
    wu = sb("wu", [P, 4, P])
    rows = sb("rows", [P, 2, P])
    rw = sb("rw", [P, E1])
    rbb = sb("rbb", [P, E1])
    rev1 = sb("rev1", [P, E1])
    base1 = sb("base1", [P, E1])
    base0 = sb("base0", [P, E0])
    seg = sb("seg", [P, E1 * (QT + 1)])
    ltri = sb("ltri", [P, P])
    steps0 = sb("steps0", [P, T0])
    rowid = sb("rowid", [P, NT, 2])
    ltrib = sb("ltrib", [P, P], BF16)
    swg = sb("swg", [P, 2, F1])
    swd = sb("swd", [FT, 2, P])

    with ExitStack() as first:
        def sa(name, shape, dt=F32):
            return first.enter_context(nc.sbuf_tensor(name, shape, dt))

        wq2 = sa("wq2", [P, 4, P])
        cosT = sa("cosT", [P, S])
        sinT = sa("sinT", [P, S])
        ra = sa("ra", [P, 4, C])
        rb = sa("rb", [P, 2, C])
        parts = sa("parts", [P, 2, 3, N], BF16)
        KM = [sa(f"KM{u}", [P, 4, S], BF16) for u in range(GB)]
        QG = [sa(f"QG{u}", [P, S], BF16) for u in range(GB)]
        Q2 = [sa(f"Q2{u}", [P, S], BF16) for u in range(GB)]
        VG = [sa(f"VG{u}", [P, QT, 2, VD]) for u in range(GB)]
        V = sa("V", [P, QT, NB * NH, VD])
        E = [sa(f"E{u}", [P, 4, C]) for u in range(3)]
        mx = [sa(f"mx{u}", [P, QT, 4]) for u in range(GB)]
        TM = sa("TM", [P, QT, 4, RH], BF16)
        PVs = sa("PVs", [P, S])
        OT = sa("OT", [P, QT, NG + 1, 4, VD])
        rden = sa("rden", [P, QT * NG * 4])
        ssq = sa("ssq", [P, QT * NG * 2])
        NRM = parts[:].rearrange("p w t n -> p (w t n)").bitcast(F32)[:, 0:QT * NG * 4 * 2 * HD]

    L0 = sb("L0", [P, NT, E0])
    La = sb("La", [P, NT, E1])
    Lb = sb("Lb", [P, NT, E1])
    oh = sb("oh", [P, 2, NT, E1])
    top = sb("top", [P, 8, NT])
    WE = sb("WE", [P, NT, E0])
    onesb = sb("onesb", [P, P], BF16)
    selx = sb("selx", [P, E1, QT + 1])
    inclx = sb("inclx", [P, E1, QT + 1])
    selb = sb("selb", [P, NB, E1, QT], BF16)
    cumb = sb("cumb", [P, NB, E1, QT], BF16)
    totb = sb("totb", [P, E0], BF16)
    posx = sb("posx", [P, 2, QT, E1])
    prod = sb("prod", [P, 2, QT, E1])
    idx = sb("idx", [P, NT, 2], I32)
    fidx = sb("fidx", [P, 2, QT])
    wts = sb("wts", [P, 2, NT])
    XI = sb("XI", [P, NT, 2, RW])
    over = sb("over", [P, E0, NT])
    ends = sb("ends", [P, 3, E0])
    passed = sb("passed", [P, T0, E0])
    skipped = sb("skipped", [P, T0, E0])
    tile_f = sb("tile_f", [P, 2, T0])
    tile_e = sb("tile_e", [P, T0], I32)
    tile_s = sb("tile_s", [P, T0], I32)
    HT = sb("HT", [P, NB, S + 3])
    cwm = sb("cwm", [P, 4, P])
    cwt = sb("cwt", [P, 4, P])
    w3t = sb("w3t", [P, 3, P])
    wbt = sb("wbt", [P, 4, P])
    wut = sb("wut", [P, 4, P])
    invp = sb("invp", [P, S])
    onesS = sb("onesS", [P, S])

    with ExitStack() as second:
        def sc(name, shape, dt=F32):
            return second.enter_context(nc.sbuf_tensor(name, shape, dt))

        WET = TMP[0:E0, :]
        W1A = sc("W1A", [P, E0, F0])
        W1B = sc("W1B", [P, E0, F0])
        W2 = sc("W2", [P, E0, 4, P])
        B1 = sc("B1", [P, E0, 2, F0])
        XE0 = sc("XE0", [P, XB, RW])
        XT0 = sc("XT0", [P, 2, P])
        A0 = sc("A0", [P, 2, F0])
        U0 = sc("U0", [P, 2, F0])
        SA0, G0 = A0, U0
        GT0 = sc("GT0", [P, 2, 4, P])
        YE0 = sc("YE0", [P, XB, P])
        YG0 = W1A[:].rearrange("p e f -> p (e f)").rearrange("p (t k d) -> p t k d", k=2, d=P)
        oid0 = sc("oid0", [P, XB], I32)

    QF = sb("QF", [P, N])
    KF = sb("KF", [P, N])
    VF = sb("VF", [P, N])
    X0 = sb("X0", [P, NT, P])
    G = sb("G", [P, 2, 4, C])
    wg1 = sb("wg1", [P, EB, 2, F1])
    wd1 = sb("wd1", [FT, EB, 2, P])
    XE = VF[:, 0:EB * CR * RW].rearrange("p (b r w) -> p b r w", b=EB, r=CR)
    XET = sb("XET", [P, 2, CR, CP])
    oid = sb("oid", [P, EB, CR], I32)
    HS = sb("HS", [FT, 2, C])
    H = sb("H", [FT, 2, 2, C])
    YE = KF[:, 0:EB * CR * P].rearrange("p (b r d) -> p b r d", b=EB, r=CR)
    YG = G[:].rearrange("p u f c -> p (u f c)").rearrange("p (t k d) -> p t k d", k=2, d=P)

    SM = [ctx.enter_context(nc.psum_tensor(f"SM{i}", [P, 2 * C], F32)) for i in range(2)]
    ST = [ctx.enter_context(nc.psum_tensor(f"ST{i}", [P, C], F32)) for i in range(3)]
    PV = ctx.enter_context(nc.psum_tensor("PVp", [P, C], F32))
    BK = [SM[0][:, 0:C], SM[0][:, C:2 * C], SM[1][:, 0:C], SM[1][:, C:2 * C],
          ST[0][:, :], ST[1][:, :], ST[2][:, :], PV[:, :]]

    qrows = nc.dram_tensor("qrows", [NBLK, NB * P, S], BF16, kind="Internal").ap()
    krows = nc.dram_tensor("krows", [NBLK, NB * P, S], BF16, kind="Internal").ap()
    xslots = nc.dram_tensor("xslots", [SLOTS, RW], F32, kind="Internal").ap()
    xslots0 = nc.dram_tensor("xslots0", [(R0 + T0) * P, RW], F32, kind="Internal").ap()
    orows0 = nc.dram_tensor("orows0", [2 * N, P], F32, kind="Internal").ap()
    orows = nc.dram_tensor("orows", [2 * N, P], F32, kind="Internal").ap()

    in_id, in_x, in_wo = sem("in_id"), [sem(f"in_x{c}") for c in range(NC)], sem("in_wo")
    in_w, in_tab, in_v, in_ffn, in_mix, in_moe = (sem(n) for n in (
        "in_w", "in_tab", "in_v", "in_ffn", "in_mix", "in_moe"))
    in_invp = sem("in_invp")
    km_zeroed, pv_zeroed = sem("km_zeroed"), sem("pv_zeroed")
    const_set = sem("const_set")
    dve_step = sem("dve_step")
    act_step = sem("act_step")
    vec_ready, vec_copied = sem("vec_ready"), sem("vec_copied")
    xT_ready, xT_copied = sem("xT_ready"), sem("xT_copied")
    w2_ready = sem("w2_ready")
    qk_ready, qk_taken = sem("qk_ready"), sem("qk_taken")
    v_ready, v_copied = sem("v_ready"), sem("v_copied")
    rot_ready, part0_ready, rest_ready, part1_ready, parts_ready = (sem(n) for n in (
        "rot_ready", "part0_ready", "rest_ready", "part1_ready", "parts_ready"))
    rows_stored = sem("rows_stored")
    kq_loaded = [sem(f"kq_loaded{u}") for u in range(GB)]
    vg_ready = sem("vg_ready")
    s_ready, s_taken = sem("s_ready"), sem("s_taken")
    m_hi, tm_ready = sem("m_hi"), sem("tm_ready")
    st_ready, exp_done = sem("st_ready"), sem("exp_done")
    pv_step, pv_evac = sem("pv_step"), sem("pv_evac")
    lam_sum, lam_exp = sem("lam_sum"), sem("lam_exp")
    x_normed, x0_ready = sem("x_normed"), sem("x0_ready")
    var_ready, std_ready = sem("var_ready"), sem("std_ready")
    rows_ready, rows_added, kv_scaled = sem("rows_ready"), sem("rows_added"), sem("kv_scaled")
    tok_ready = sem("tok_ready")
    tr_ready = sem("tr_ready")
    mo_ready, mo_taken = sem("mo_ready"), sem("mo_taken")
    fm_ready = sem("fm_ready")
    r0_exp, we_ready = sem("r0_exp"), sem("we_ready")
    top_diff = sem("top_diff")
    wet_ready, wet_taken = sem("wet_ready"), sem("wet_taken")
    w0_loaded = sem("w0_loaded")
    tot_ready, pos0_ready, tiles_ready = sem("tot_ready"), sem("pos0_ready"), sem("tiles_ready")
    s0_loaded = [sem(f"s0_loaded{b}") for b in range(XB)]
    y0_scattered = [sem(f"y0_scattered{b}") for b in range(XB)]
    yg0_loaded = [sem(f"yg0_loaded{c}") for c in range(NC)]
    xe0_ready, xt0_taken, ab0_ready, sum0_ready, ab0_taken = (sem(n) for n in (
        "xe0_ready", "xt0_taken", "ab0_ready", "sum0_ready", "ab0_taken"))
    silu0_done, g0_done, gt0_ready, gt0_taken = (sem(n) for n in (
        "silu0_done", "g0_done", "gt0_ready", "gt0_taken"))
    y0_ready, y0_taken = sem("y0_ready"), sem("y0_taken")
    y0_seen = sem("y0_seen")
    tw_ready, tw_taken = sem("tw_ready"), sem("tw_taken")
    cwm_ready = sem("cwm_ready")
    up_ready, gelu_done = sem("up_ready"), sem("gelu_done")
    lg_ready, prob_exp, prob_sub = sem("lg_ready"), sem("prob_exp"), sem("prob_sub")
    sel_ready, pos_ready = sem("sel_ready"), sem("pos_ready")
    idx_ready, scattered, zeroed = sem("idx_ready"), sem("scattered"), sem("zeroed")
    w1_loaded = [sem(f"w1_loaded{u}") for u in range(EB)]
    slots_loaded = [sem(f"slots_loaded{u}") for u in range(EB)]
    y_scattered = [sem(f"y_scattered{u}") for u in range(EB)]
    xi_ready, y_seen = sem("xi_ready"), sem("y_seen")
    yg_loaded = [sem(f"yg_loaded{c}") for c in range(NC)]
    xe_ready, xe_taken = sem("xe_ready"), sem("xe_taken")
    qkv_ready, qkv_taken, pool_done = sem("qkv_ready"), sem("qkv_taken"), sem("pool_done")
    gu_ready, h_silu, h_done = sem("gu_ready"), sem("h_silu"), sem("h_done")
    ye_ready, ye_taken = sem("ye_ready"), sem("ye_taken")
    shared_ready, shared_taken = sem("shared_ready"), sem("shared_taken")
    result_ready, stored = sem("result_ready"), sem("stored")

    block = ctx.enter_context(nc.Block())

    class Chain:

        def __init__(self, eng, s):
            self.eng, self.s, self.n = eng, s, 0

        def __call__(self, ins):
            self.n += 1
            ins.then_inc(self.s, 1)
            self.eng.wait_ge(self.s, self.n)

    def use(g, pos):
        return FIRST + USES * g + pos

    @block.sync
    def _(sp):
        def load_x(c):
            sp.dma_start(X[:, TPC * c:TPC * (c + 1), :],
                         a["x"].rearrange("b (t p) d -> p (b t) d", p=P)[:, TPC * c:TPC * (c + 1), :]).then_inc(in_x[c], 16)

        sp.dma_start(ident[:], a["ident"]).then_inc(in_id, 16)
        load_x(0)
        for j, n in enumerate(("Wq", "Wk")):
            sp.dma_start(wqkv[:, j, :], a[n]).then_inc(in_w, 16)
        sp.dma_start(cosT[:], a["cos"]).then_inc(in_tab, 16)
        sp.dma_start(sinT[:], a["sin"]).then_inc(in_tab, 16)
        for c in range(1, NC):
            load_x(c)
        for j, n in ((2, "Wv"), (3, "Wo")):
            sp.dma_start(wqkv[:, j, :], a[n]).then_inc(in_wo, 16)
        def store_rows(j):
            c, w = divmod(j, 2)
            b, h = divmod(c, 2)
            sp.wait_ge(parts_ready, j + 1)
            for part in range(3):
                blocks = BLOCKS[w][part]
                n = len(range(NBLK)[blocks])
                sp.dma_start((qrows, krows)[w][blocks, P * b:P * (b + 1), C * h:C * (h + 1)].rearrange("k r t -> r k t"),
                             parts[:, w, part, C * c:C * (c + 1)].unsqueeze(1).to_broadcast([P, n, C]))\
                    .then_inc(rows_stored, 16)

        def load_group(u, g):
            for aa in range(4):
                for src, dst in ((qrows, QG[u][RH * aa:RH * aa + MAXROW, :]),
                                 (krows, KM[u][RH * aa:RH * aa + MAXROW, aa, :])):
                    sp.dma_start(dst, src.rearrange("k (g a d) t -> k g a d t", a=4, d=HD)[:, bass.ds(g, 1), aa]
                                 .rearrange("k g d t -> k (g d) t")).then_inc(kq_loaded[u], 16)

        for j in range(NC):
            store_rows(j)
        sp.wait_ge(const_set, 2)
        sp.wait_ge(rows_stored, 12 * 16)
        for g in range(GB):
            load_group(g, g)
        for j, n in enumerate(("lq1", "lk1", "lq2", "lk2")):
            sp.dma_start(lamv[:, j, :], a[n].partition_broadcast(P)).then_inc(in_v, 16)
        sp.dma_start(VR[R_SUBLN:R_SUBLN + 1, :].rearrange("o (h d) -> o h d", h=NH),
                     a["subln_g"].partition_broadcast(NH).unsqueeze(0)).then_inc(in_v, 16)
        for r, n in ((R_B1A, "b1a"), (R_B1B, "b1b")):
            sp.dma_start(VR[r:r + 4 * E0, :], a[n].rearrange("e (f p) -> (e f) p", p=P)).then_inc(in_v, 16)
        sp.dma_start(VR[R_BB:R_BB + 4, :], a["bb"].rearrange("(f p) -> f p", p=P)).then_inc(in_v, 16)
        for r, n in ((R_BQKV, "bq"), (R_BQKV + 1, "bk"), (R_BQKV + 2, "bv"), (R_GB, "ln_conv_g"),
                     (R_GB + 1, "ln_conv_b"), (R_GB + 2, "ln_attn_g"), (R_GB + 3, "ln_attn_b"),
                     (R_GB + 4, "ln_boom_g"), (R_GB + 5, "ln_boom_b"), (R_LNW, "ln_w")):
            sp.dma_start(VR[r:r + 1, :], a[n].unsqueeze(0)).then_inc(in_v, 16)

        for j in range(NC, 2 * NC):
            store_rows(j)
        sp.wait_ge(rows_stored, 24 * 16)

        sp.dma_start(wg0[:], a["Wg"]).then_inc(in_ffn, 16)
        sp.dma_start(bg0[:], a["bg"].partition_broadcast(P)).then_inc(in_ffn, 16)
        sp.dma_start(rev0[:], a["rev0"].partition_broadcast(P)).then_inc(in_ffn, 16)
        sp.dma_start(b2[:], a["b2"]).then_inc(in_ffn, 16)
        sp.dma_start(cw[:], a["conv_w"]).then_inc(in_mix, 16)
        for j, n in enumerate(("mWq", "mWk", "mWv")):
            sp.dma_start(w3[:, j, :], a[n]).then_inc(in_mix, 16)
        sp.dma_start(wb[:], a["Wb"].rearrange("(f p) d -> p f d", p=P)).then_inc(in_mix, 16)
        sp.dma_start(wu[:], a["Wu"].rearrange("d (f p) -> d f p", p=P)).then_inc(in_mix, 16)
        sp.dma_start(rows[:, 0, :], a["conv_b"].partition_broadcast(P)).then_inc(in_mix, 16)
        sp.dma_start(rows[:, 1, :], a["bu"].partition_broadcast(P)).then_inc(in_mix, 16)
        sp.dma_start(rw[:], a["router_w"]).then_inc(in_moe, 16)
        sp.dma_start(rowid[:], a["rowid"]).then_inc(in_moe, 16)
        sp.dma_start(steps0[:], a["steps0"].partition_broadcast(P)).then_inc(in_moe, 16)
        for dst, n in ((rbb[:], "router_b"), (rev1[:], "rev1"), (base0[:], "base0"), (base1[:], "base1"), (seg[:], "seg")):
            sp.dma_start(dst, a[n].partition_broadcast(P)).then_inc(in_moe, 16)
        sp.dma_start(ltri[:], a["ltri"]).then_inc(in_moe, 16)
        sp.dma_start(swg[:, 0, :], a["sw_gate"]).then_inc(in_moe, 16)
        sp.dma_start(swg[:, 1, :], a["sw_up"]).then_inc(in_moe, 16)
        sp.dma_start(swd[:], a["sw_down"].rearrange("(f p) d -> p f d", p=FT)).then_inc(in_moe, 16)
        sp.dma_start(xslots.rearrange("(e p r) d -> p e (r d)", e=E1, p=P),
                     empty.unsqueeze(1).to_broadcast([P, E1, CR * RW])).then_inc(zeroed, 16)

        n = R0 // 4
        for j in range(4):
            sp.dma_start(xslots0.rearrange("(t p) w -> p t w", p=P)[:, n * j:n * (j + 1), :],
                         empty[:, 0:RW].unsqueeze(1).to_broadcast([P, n, RW])).then_inc(zeroed, 16)

        with sp.Fori(0, (NG - 1 - GB) // GB) as i:
            for u in range(GB):
                sp.wait_ge(pv_step, (i * GB + u) * STEPS + (STEPS + CREDIT))
                load_group(u, i * GB + (GB + u))
        sp.wait_ge(pv_step, (NG - GB) * STEPS + CREDIT)
        load_group(0, NG - 1)
        sp.wait_ge(pv_step, (NG - 2) * STEPS + CREDIT)
        load_group(1, 0)

        sp.wait_ge(tok_ready, NC)
        sp.dma_start(invp[:], a["invp"].partition_broadcast(P)).then_inc(in_invp, 16)

        for e in range(E0):
            sp.dma_start(W1A[:, e, :], a["W1a"][e]).then_inc(w0_loaded, 16)
            sp.dma_start(W1B[:, e, :], a["W1b"][e]).then_inc(w0_loaded, 16)
            sp.dma_start(B1[:, e, 0, :], a["b1a"][e].partition_broadcast(P)).then_inc(w0_loaded, 16)
            sp.dma_start(B1[:, e, 1, :], a["b1b"][e].partition_broadcast(P)).then_inc(w0_loaded, 16)
            sp.dma_start(W2[:, e, :, :], a["W2"][e].rearrange("(f p) d -> p f d", p=P)).then_inc(w0_loaded, 16)

        def load_tile0(b, t):
            s = sp.value_load(tile_s[0:1, bass.ds(t, 1)], min_val=0, max_val=R0 + T0 - 1)
            sp.dma_start(XE0[:, b, :], xslots0.rearrange("(t p) w -> t p w", p=P)[bass.ds(s, 1)]
                         .rearrange("t p w -> (t p) w")).then_inc(s0_loaded[b], 16)

        sp.wait_ge(tiles_ready, 1)
        sp.wait_ge(scattered, 16 * 2 * NT)
        for b in range(XB):
            load_tile0(b, b)
        with sp.Fori(0, T0 // XB - 1) as i:
            for b in range(XB):
                sp.wait_ge(g0_done, i * XB + (b + 1))
                load_tile0(b, i * XB + (XB + b))
        for t in range(T0 - T0 % XB, T0):
            sp.wait_ge(g0_done, t - XB + 1)
            load_tile0(t % XB, t)

        def load_rows(dst, src, signal):
            for c in range(NC):
                sp.dma_start(dst[:, TPC * c:TPC * (c + 1), :, :].rearrange("p t k d -> p t (k d)"),
                             src.rearrange("(t p k) d -> p t (k d)", p=P, k=2)[:, TPC * c:TPC * (c + 1), :])\
                    .then_inc(signal[c], 16)

        for b in range(XB):
            sp.wait_ge(y0_scattered[b], 16 * len(range(b, T0, XB)) + 16)
        load_rows(YG0, orows0, yg0_loaded)

        sp.wait_ge(tok_ready, 3 * NC)
        def load_weights1(b, e):
            sp.dma_start(wg1[:, b, 0, :], a["w_gate"][bass.ds(e, 1)].rearrange("e d f -> (e d) f")).then_inc(w1_loaded[b], 16)
            sp.dma_start(wg1[:, b, 1, :], a["w_up"][bass.ds(e, 1)].rearrange("e d f -> (e d) f")).then_inc(w1_loaded[b], 16)
            sp.dma_start(wd1[:, b, :, :],
                         a["w_down"][bass.ds(e, 1)].rearrange("e (f p) d -> p (e f) d", p=FT)).then_inc(w1_loaded[b], 16)

        def load_slots1(b, e):
            xr = xslots.rearrange("(e p r) d -> e p (r d)", e=E1, p=P)[bass.ds(e, 1), 0:CP]
            sp.dma_start(XE[0:CP, b, :, :].rearrange("p r d -> p (r d)"),
                         xr.rearrange("e p c -> (e p) c")).then_inc(slots_loaded[b], 16)

        for b in range(EB):
            load_weights1(b, b)
        sp.wait_ge(scattered, 2 * 16 * 2 * NT)
        for b in range(EB):
            load_slots1(b, b)
        with sp.Fori(0, E1 // EB - 1) as i:
            for b in range(EB):
                sp.wait_ge(h_done, i * (2 * EB) + (2 * NC + 2 * b + 4))
                load_slots1(b, i * EB + (EB + b))
                sp.wait_ge(ye_ready, i * EB + (b + 1))
                load_weights1(b, i * EB + (EB + b))

        for b in range(EB):
            sp.wait_ge(y_scattered[b], 16 * CR * (E1 // EB) + 16)
        load_rows(YG, orows, yg_loaded)
        ov = out.rearrange("b (t p) d -> p (b t) d", p=P)
        for t in range(0, NT, 4):
            sp.wait_ge(result_ready, t // 4 + 1)
            sp.dma_start(ov[:, t:t + 4, :], XS[:, t:t + 4, :]).then_inc(stored, 16)
        sp.wait_ge(stored, 16 * NT // 4)

    @block.gpsimd
    def _(pool):
        for u in range(GB):
            pool.memset(QG[u][:], 0.0)
            pool.memset(KM[u][:], 0.0)
        pool.memset(TM[:], 0.0)
        pool.memset(V[:, :, :, 2 * HD:VD], 1.0).then_inc(km_zeroed, 1)
        pool.wait_ge(km_zeroed, 1)
        for u in range(GB):
            for aa in range(4):
                ins = pool.memset(KM[u][RH * aa:RH * aa + MAXROW + 2, aa, :], 1.0)
        ins.then_inc(const_set, 1)
        pool.wait_ge(const_set, 2)
        for j in range(2 * NC):
            c, w = divmod(j, 2)
            pool.wait_ge(part1_ready, j + 1)
            pool.tensor_tensor(parts[:, w, 2, C * c:C * (c + 1)], ra[:, j % 4, :], parts[:, w, 1, C * c:C * (c + 1)],
                               ALU.subtract).then_inc(parts_ready, 1)
        pool.wait_ge(const_set, 2)
        pool.wait_ge(v_copied, NC)
        for g in range(GB):
            pool.tensor_copy(VG[g][:], V[:, :, 2 * g:2 * g + 2, :]).then_inc(vg_ready, 1)
        flat = orows.rearrange("r d -> (r d)").rearrange("(p c) -> p c", p=P)
        for b in range(EB):
            w = 2 * N // EB
            pool.dma_start(flat[:, w * b:w * (b + 1)], zeros).then_inc(y_scattered[b], 16)
        for b in range(XB):
            lo, hi = R0 + T0 * b // XB, R0 + T0 * (b + 1) // XB
            n = hi - lo
            pool.dma_start(xslots0.rearrange("(t p) w -> p t w", p=P)[:, lo:hi, :],
                           empty[:, 0:RW].unsqueeze(1).to_broadcast([P, n, RW])).then_inc(y0_scattered[b], 16)
        with pool.Fori(0, (NG - 1 - GB) // GB) as i:
            for u in range(GB):
                pool.wait_ge(pv_step, (i * GB + u) * STEPS + (STEPS + CREDIT))
                pool.tensor_copy(VG[u][:], V[:, :, bass.ds(2 * (i * GB + (GB + u)), 2), :]).then_inc(vg_ready, 1)
        pool.wait_ge(pv_step, (NG - GB) * STEPS + CREDIT)
        pool.tensor_copy(VG[0][:], V[:, :, 2 * (NG - 1):2 * NG, :]).then_inc(vg_ready, 1)

        def scatter_pairs(dst, n, slots):
            for c in range(NC):
                pool.wait_ge(xi_ready, n * NC + c + 1)
                pool.wait_ge(idx_ready, n * NB + c // 2 + 1)
                for t in range(TPC * c, TPC * (c + 1)):
                    for k in range(2):
                        pool.indirect_dma_start(
                            dst[:, :], bass.IndirectOffsetOnAxis(ap=idx[:, t, k:k + 1].bitcast(U32), axis=0),
                            XI[:, t, k, :], None, bounds_check=slots - 1, oob_is_err=False).then_inc(scattered, 16)

        for b in range(XB):
            pool.wait_ge(y0_scattered[b], 16)
        pool.wait_ge(zeroed, 16 * 5)
        scatter_pairs(xslots0, 0, (R0 + T0) * P)
        def scatter_tile0(b, t):
            pool.wait_ge(y0_taken, t + 2)
            pool.sem_inc(y0_seen, 1)
            pool.indirect_dma_start(
                orows0[:, :], bass.IndirectOffsetOnAxis(ap=oid0[:, b:b + 1].bitcast(U32), axis=0),
                YE0[:, b, :], None, bounds_check=2 * N - 1, oob_is_err=False).then_inc(y0_scattered[b], 16)

        with pool.Fori(0, T0 // XB) as i:
            for b in range(XB):
                scatter_tile0(b, i * XB + b)
        for t in range(T0 - T0 % XB, T0):
            scatter_tile0(t % XB, t)

        def add_pairs(n, rows2):
            for c in range(1, NC):
                pool.wait_ge(rows_ready, (NC - 1) * n + c)
                t = slice(TPC * c, TPC * (c + 1))
                pool.tensor_tensor(rows2[:, t, 0, :], rows2[:, t, 0, :], rows2[:, t, 1, :], ALU.add).then_inc(rows_added, 1)

        add_pairs(0, YG0)

        for c in range(NC):
            pool.wait_ge(x_normed, c + 1)
            t = slice(TPC * c, TPC * (c + 1))
            pool.tensor_tensor(X0[:, t, :], X[:, t, :], rows[:, 0, :].unsqueeze(1).to_broadcast([P, TPC, P]), ALU.add)\
                .then_inc(x0_ready, 1)

        pool.wait_ge(in_invp, 16)
        for b in range(NB):
            pool.wait_ge(qkv_taken, 6 * (b + 1))
            for m in (KF, VF):
                r = m[:, S * b:S * (b + 1)]
                pool.tensor_tensor(r, r, invp[:], ALU.mult).then_inc(kv_scaled, 1)

        scatter_pairs(xslots, 1, SLOTS)
        with pool.Fori(0, E1 // EB) as i:
            for b in range(EB):
                pool.wait_ge(ye_taken, i * EB + (b + 3))
                pool.sem_inc(y_seen, 1)
                for r in range(CR):
                    pool.indirect_dma_start(
                        orows[:, :], bass.IndirectOffsetOnAxis(ap=oid[0:CP, b, r:r + 1].bitcast(U32), axis=0),
                        YE[0:CP, b, r, :], None, bounds_check=2 * N - 1, oob_is_err=False).then_inc(y_scattered[b], 16)

        add_pairs(1, YG)

    @block.tensor
    def _(pe):
        pe.wait_ge(pv_zeroed, 1)
        pe.wait_ge(in_id, 16)
        for c in range(NC):
            pe.wait_ge(in_x[c], 16)
            for k in range(TPC):
                ins = pe.transpose(BK[c][:, P * k:P * (k + 1)], X[:, TPC * c + k, :], ident[:])
            ins.then_inc(xT_ready, 1)

        pe.wait_ge(w2_ready, 1)
        pe.wait_ge(xT_copied, NC)
        pe.sem_inc(pv_step, CREDIT)
        for j in range(2 * NC):
            c, w = divmod(j, 2)
            if j >= 4:
                pe.wait_ge(qk_taken, j - 3)
            for y in range(2):
                ins = pe.matmul(BK[2 * (j % 4) + y], wq2[:, 2 * w + y, :], XT[:, C * c:C * (c + 1)],
                                start=True, stop=True)
            ins.then_inc(qk_ready, 1)
        pe.wait_ge(in_wo, 32)
        for c in range(NC):
            pe.wait_ge(qk_taken, 2 * NC)
            for k in range(TPC):
                t = TPC * c + k
                ins = pe.matmul(BK[4 + c][:, P * k:P * (k + 1)], XT[:, P * t:P * (t + 1)], wqkv[:, 2, :],
                                start=True, stop=True)
            ins.then_inc(v_ready, 1)

        def max_scores(v, k, pos, g):
            qt, aa = divmod(k, 4)
            slot = (1 + pos) % 2
            pe.wait_ge(s_taken, use(g, pos) + 1)
            for h in range(2):
                ins = pe.matmul(SM[slot][:, C * h:C * (h + 1)], QG[v][:, P * qt:P * (qt + 1)],
                                KM[v][:, aa, C * h:C * (h + 1)], start=True, stop=True)
            ins.then_inc(s_ready, 1)

        def max_rows(g, pos):
            slot = (1 + pos) % 2
            pe.wait_ge(tm_ready, g + 2)
            pe.wait_ge(s_taken, use(g, pos) + 1)
            for qt in range(QT):
                ins = pe.matmul(SM[slot][:, P * qt:P * (qt + 1)], TM[:, qt, :, :].rearrange("p a r -> p (a r)"),
                                identb[:], start=True, stop=True)
            ins.then_inc(s_ready, 1)

        def turn_outputs(g, pos, phase):
            slot = (1 + pos) % 2
            pe.wait_ge(pv_evac, 2 * g + 1)
            pe.wait_ge(s_taken, use(phase, pos) + 1)
            for qt in range(QT):
                ins = pe.transpose(SM[slot][:, P * qt:P * (qt + 1)], PVs[:, P * qt:P * (qt + 1)], ident[:])
            ins.then_inc(s_ready, 1)

        def group(g, u, round_, last):
            v = (u + 1) % GB
            w = (u + 2) % GB
            pos = 0

            def scores(s, aa):
                half, kt = divmod(s, QT)
                pe.wait_ge(exp_done, g * (4 * STEPS) + (4 * s + aa + 1))
                if s == 0 and aa == 0:
                    pe.wait_ge(s_taken, use(g, 0) + (2 - EARLY))
                pe.matmul(ST[(u + s + aa) % 3][:], KM[u][:, aa, P * kt:P * (kt + 1)],
                          Q2[u][:, C * half:C * (half + 1)], start=True, stop=True).then_inc(st_ready, 1)

            def outputs(s):
                half, kt = divmod(s, QT)
                pe.wait_ge(exp_done, g * (4 * STEPS) + (4 * s + 4 + CREDIT))
                if s == 0:
                    pe.wait_ge(vg_ready, g + 1)
                if kt == 0:
                    pe.wait_ge(pv_evac, 2 * g + (1 + half))
                for aa in range(4):
                    ins = pe.matmul(PV[RH * aa:RH * aa + VD, :], VG[u][:, kt, aa // 2, :],
                                    E[(u + s) % 3][:, aa, :], start=(kt == 0), stop=(kt == QT - 1))
                ins.then_inc(pv_step, 1)

            def maximum(pos, item):
                what, k = item
                if what == "rows":
                    max_rows(g, pos)
                else:
                    if item == ("after", 0):
                        pe.wait_ge(kq_loaded[w], 128 * (round_ + (1 if u == 0 else 2)))
                    max_scores(v if what == "next" else w, k, pos, g)

            for s in range(STEPS):
                work = [] if last else list(PLAN[s])
                if s == OUT_STEP:
                    turn_outputs(g, pos, g)
                    pos += 1
                scores(s, 0)
                scores(s, 1)
                if work:
                    maximum(pos, work.pop(0))
                    pos += 1
                scores(s, 2)
                if s:
                    outputs(s - 1)
                for item in work:
                    maximum(pos, item)
                    pos += 1
                scores(s, 3)
            outputs(STEPS - 1)

        pe.wait_ge(kq_loaded[0], 128)
        for k in range(4 * QT):
            max_scores(0, k, k - use(-1, 0), -1)
            if k == 2 * QT:
                pe.wait_ge(in_v, IN_V)
                pe.wait_ge(v_copied, NC)
                pe.transpose(BK[4][:, 0:R_N], VR[:], ident[0:R_N, 0:R_N]).then_inc(vec_ready, 1)
        max_rows(-1, 4 * QT - use(-1, 0))
        pe.wait_ge(kq_loaded[1], 128)
        for k in range(EARLY):
            max_scores(1, k, 4 * QT + 1 + k - use(-1, 0), -1)
        pe.wait_ge(vec_copied, 1)
        with pe.Fori(0, (NG - 1) // GB) as i:
            for u in range(GB):
                group(i * GB + u, u, i, False)
        group(NG - 1, 0, None, True)
        turn_outputs(NG, 1, NG - 1)

        def turn(r, n, c, tile, bank):
            pe.wait_ge(tok_ready, NC * r + n + 1)
            for k in range(TPC):
                ins = pe.transpose(BK[bank][:, P * k:P * (k + 1)], tile(TPC * c + k), ident[:])
            ins.then_inc(tr_ready, 1)

        def project(n):
            pe.wait_ge(fm_ready, n + 1)
            c = n
            for k in range(TPC):
                t = TPC * c + k
                ins = pe.matmul(BK[4 + c][:, P * k:P * (k + 1)], XT[:, P * t:P * (t + 1)], wo[:], start=True, stop=True)
            ins.then_inc(mo_ready, 1)

        for n, c in enumerate(range(NC)):
            turn(0, n, c, lambda t: TMP[:, P * (2 * (t % QT) + t // QT):P * (2 * (t % QT) + t // QT + 1)], c)
            if n:
                project(n - 1)
        project(NC - 1)

        def logits(r, n, c, w, e):
            pe.wait_ge(fm_ready, NC * r + n + 1)
            for k in range(TPC):
                t = TPC * c + k
                ins = pe.matmul(BK[4 + c][:, e * k:e * (k + 1)], XT[:, P * t:P * (t + 1)], w, start=True, stop=True)
            ins.then_inc(lg_ready, 1)

        def positions(r, b, e):
            pe.wait_ge(sel_ready, NB * r + b + 1)
            dst = BK[5 + 2 * b][:, 2 * P:2 * P + e * QT]
            pe.matmul(dst, ltrib[:], selb[:, b, 0:e, :].rearrange("p e t -> p (e t)"), start=True, stop=False)
            pe.matmul(dst, onesb[:], cumb[:, b, 0:e, :].rearrange("p e t -> p (e t)"),
                      start=False, stop=True).then_inc(pos_ready, 1)

        pe.wait_ge(in_ffn, 16 * 4)
        for b in range(NB):
            for c in (2 * b, 2 * b + 1):
                turn(1, c, c, lambda t: XS[:, t, :], c)
            for c in (2 * b, 2 * b + 1):
                logits(1, c, c, wg0[:], E0)
            positions(0, b, E0)
        pe.wait_ge(tot_ready, 1)
        pe.matmul(BK[7][:, 3 * P:3 * P + E0], onesb[:], totb[:], start=True, stop=True).then_inc(pos0_ready, 1)

        pe.wait_ge(we_ready, 1)
        for c in range(NC):
            for k in range(TPC):
                ins = pe.transpose(BK[c][0:E0, P * k:P * (k + 1)], WE[:, TPC * c + k, :], ident[:])
            ins.then_inc(wet_ready, 1)
        pe.wait_ge(tiles_ready, 1)
        for c in range(NC):
            pe.wait_ge(wet_taken, c + 1)
            for k in range(TPC):
                t = TPC * c + k
                ins = pe.matmul(BK[4 + c][:, P * k:P * (k + 1)], WET[:, P * t:P * (t + 1)], b2[:], start=True, stop=True)
            ins.then_inc(mo_ready, 1)

        pe.wait_ge(in_mix, 16 * 8)
        pe.wait_ge(cwm_ready, 1)
        for bank, src, n in ((0, cwm, 4), (1, w3, 3), (2, wb, 4), (3, wu, 4)):
            for j in range(n):
                ins = pe.transpose(BK[bank][:, P * j:P * (j + 1)], src[:, j, :], ident[:])
            ins.then_inc(tw_ready, 1)

        def turn_x0(b, loads, t):
            pe.wait_ge(s0_loaded[b], loads * 16)
            pe.wait_ge(xt0_taken, t)
            pe.transpose(BK[6][:, 0:P], XE0[:, b, 0:P], ident[:]).then_inc(xe0_ready, 1)

        def up0(h, t, free):
            e = pe.value_load(tile_e[0:1, bass.ds(t, 1)], min_val=0, max_val=E0 - 1)
            pe.wait_ge(xt0_taken, t + 1)
            if free is not None:
                pe.wait_ge(ab0_taken, free)
            for y, w in ((0, W1A), (1, W1B)):
                ins = pe.matmul(BK[2 * h + y], XT0[:, h, :], w[:, bass.ds(e, 1), :].rearrange("p e f -> p (e f)"),
                                start=True, stop=True)
            ins.then_inc(ab0_ready, 1)

        def turn_g0(h, t, free):
            pe.wait_ge(g0_done, t + 1)
            if free is not None:
                pe.wait_ge(gt0_taken, free)
            for f in range(4):
                ins = pe.transpose(BK[4][:, P * f:P * (f + 1)], G0[:, h, P * f:P * (f + 1)], ident[:])
            ins.then_inc(gt0_ready, 1)

        def down0(h, t, free):
            e = pe.value_load(tile_e[0:1, bass.ds(t, 1)], min_val=0, max_val=E0 - 1)
            pe.wait_ge(gt0_taken, t + 1)
            pe.wait_ge(y0_taken, free)
            for f in range(4):
                ins = pe.matmul(BK[7][:, 0:P], GT0[:, h, f, :], W2[:, bass.ds(e, 1), f, :].rearrange("p e d -> p (e d)"),
                                start=(f == 0), stop=(f == 3))
            ins.then_inc(y0_ready, 1)

        pe.wait_ge(mo_taken, 2 * NC)
        pe.wait_ge(tw_taken, 4)
        pe.wait_ge(w0_loaded, 16 * 5 * E0)
        pe.wait_ge(s0_loaded[0], 16)
        pe.transpose(BK[6][:, 0:P], XE0[:, 0, 0:P], ident[:]).then_inc(xe0_ready, 1)
        for t in range(PEEL):
            turn_x0(t + 1, 1, t + 1)
            up0(t % 2, t, None)
            if t >= 1:
                turn_g0((t - 1) % 2, t - 1, None)
        with pe.Fori(0, PASSES) as i:
            for u in range(4):
                t, h = i * 4 + (PEEL + u), (PEEL + u) % 2
                turn_x0((PEEL + u + 1) % XB, i + (1 + (PEEL + u + 1) // XB), i * 4 + (PEEL + u + 1))
                up0(h, t, i * 4 + (PEEL + u - 1))
                turn_g0(1 - h, i * 4 + (PEEL + u - 1), i * 4 + (PEEL + u - 1))
                down0(h, i * 4 + (PEEL + u - 2), i * 4 + (PEEL + u - 1))
        t = T0 - 1
        up0(t % 2, t, t - 1)
        turn_g0((t - 1) % 2, t - 1, t - 1)
        down0(t % 2, t - 2, t - 1)
        turn_g0(t % 2, t, t)
        down0((t - 1) % 2, t - 1, t)
        down0(t % 2, t, t + 1)

        def conv(c):
            pe.wait_ge(fm_ready, 2 * NC + c + 1)
            for k in range(TPC):
                t = TPC * c + k
                for tap in range(4):
                    lo = P * (t % QT) + tap
                    ins = pe.matmul(BK[4 + c][:, P * k:P * (k + 1)], HT[:, t // QT, lo:lo + P], cwt[:, tap, :],
                                    start=(tap == 0), stop=(tap == 3))
            ins.then_inc(mo_ready, 1)

        for c in range(NC):
            turn(2, c, c, lambda t: XS[:, t, :], c)
            if c:
                conv(c - 1)
        conv(NC - 1)

        def qkv(c):
            pe.wait_ge(fm_ready, 3 * NC + c + 1)
            for w in range(3):
                j = 3 * c + w
                if j >= 4:
                    pe.wait_ge(qkv_taken, j - 3)
                else:
                    pe.wait_ge(mo_taken, 2 * NC + j + 1)
                pe.matmul(BK[4 + j % 4], w3t[:, w, :], XT[:, C * c:C * (c + 1)], start=True, stop=True)\
                    .then_inc(qkv_ready, 1)

        for c in range(NC):
            turn(3, c, c, lambda t: XS[:, t, :], c)
            if c:
                qkv(c - 1)
        qkv(NC - 1)
        for c in range(NC):
            pe.wait_ge(pool_done, c // 2 + 1)
            for k in range(TPC):
                t = TPC * c + k
                ins = pe.transpose(BK[c][:, P * k:P * (k + 1)], QF[:, P * t:P * (t + 1)], ident[:])
            ins.then_inc(mo_ready, 1)

        def boom_up(c, f):
            j = 4 * c + f
            pe.wait_ge(fm_ready, 4 * NC + c + 1)
            if j >= 4:
                pe.wait_ge(gelu_done, j - 3)
            else:
                pe.wait_ge(mo_taken, 3 * NC + j + 1)
            pe.matmul(BK[j % 4], wbt[:, f, :], XT[:, C * c:C * (c + 1)], start=True, stop=True).then_inc(up_ready, 1)

        def boom_down(c):
            pe.wait_ge(gelu_done, 4 * c + 4)
            for k in range(TPC):
                for f in range(4):
                    ins = pe.matmul(BK[4 + c][:, P * k:P * (k + 1)], G[:, c % 2, f, P * k:P * (k + 1)], wut[:, f, :],
                                    start=(f == 0), stop=(f == 3))
            ins.then_inc(mo_ready, 1)

        for c in range(NC):
            turn(4, c, c, lambda t: XS[:, t, :], 4 + c)
            if c >= 2:
                boom_up(0, 2 * c - 4)
                boom_up(0, 2 * c - 3)
        def route1(b):
            for c in (2 * b, 2 * b + 1):
                turn(5, c, c, lambda t: X[:, t, :], 4 + c)
            for c in (2 * b, 2 * b + 1):
                logits(5, c, c, rw[:], E1)

        pe.wait_ge(in_moe, 16 * 12)
        for c in range(1, NC):
            for f in range(4):
                boom_up(c, f)
            if c < NC - 1:
                boom_down(c - 1)
        route1(0)
        boom_down(NC - 2)
        positions(1, 0, E1)
        boom_down(NC - 1)
        route1(1)

        def up1(j, x, n, w):
            pe.wait_ge(h_done, j + 1)
            for y in range(2):
                ins = pe.matmul(BK[2 * (j_parity(j)) + y][0:FT, 0:n], w(y), x, start=True, stop=True)
            ins.then_inc(gu_ready, 1)

        def shared_down(c):
            pe.wait_ge(h_done, 2 * c + 4)
            pe.wait_ge(shared_taken, c + 1)
            for k in range(TPC):
                for f in range(2):
                    ins = pe.matmul(BK[4 + c % 2][:, P * k:P * (k + 1)], H[:, c % 2, f, P * k:P * (k + 1)],
                                    swd[:, f, :], start=(f == 0), stop=(f == 1))
            ins.then_inc(shared_ready, 1)

        def j_parity(j):
            return j % 2

        for c in range(NC):
            for f in range(2):
                up1(2 * c + f, XT[:, C * c:C * (c + 1)], C, lambda y, f=f: swg[:, y, FT * f:FT * (f + 1)])
            if c == 0:
                positions(1, 1, E1)
                pe.wait_ge(idx_ready, 2 * NB)
            if c:
                shared_down(c - 1)
        shared_down(NC - 1)

        def turn1(b, loads, e):
            pe.wait_ge(slots_loaded[b], loads)
            pe.wait_ge(xe_taken, e + 1)
            for r in range(CR):
                ins = pe.transpose(BK[6 + b % 2][:, CP * r:CP * (r + 1)], XE[0:CP, b, r, 0:P], ident[0:CP, 0:CP])
            ins.then_inc(xe_ready, 1)

        def gate_up1(b, loads, e):
            pe.wait_ge(w1_loaded[b], loads)
            pe.wait_ge(xe_taken, e + 3)
            for f in range(2):
                pe.wait_ge(h_done, e * 2 + (2 * NC + f + 1))
                for y in range(2):
                    ins = pe.matmul(BK[2 * f + y][0:FT, 0:CAPN], wg1[:, b, y, FT * f:FT * (f + 1)],
                                    XET[:, b % 2, :, :].rearrange("p r c -> p (r c)"), start=True, stop=True)
                ins.then_inc(gu_ready, 1)

        def down1(b, e):
            pe.wait_ge(h_done, e * 2 + (2 * NC + 4))
            pe.wait_ge(ye_taken, e + 1)
            for r in range(CR):
                for f in range(2):
                    ins = pe.matmul(BK[4 + b % 2][0:CP, P * r:P * (r + 1)], H[:, b % 2, f, CP * r:CP * (r + 1)],
                                    wd1[:, b, f, :], start=(f == 0), stop=(f == 1))
            ins.then_inc(ye_ready, 1)

        turn1(0, 16, 0)
        turn1(1, 16, 1)
        gate_up1(0, 48, 0)
        with pe.Fori(0, E1 // EB - 1) as i:
            for u in range(EB):
                b, e = (u + 1) % EB, i * EB + (u + 1)
                turn1((b + 1) % EB, 16 * i + (16 if u + 2 < EB else 32), e + 1)
                gate_up1(b, 48 * i + (48 if u + 1 < EB else 96), e)
                down1(u, e - 1)
        for e in range(E1 - EB + 1, E1):
            if e + 1 < E1:
                turn1((e + 1) % EB, 16 * E1 // EB, e + 1)
            gate_up1(e % EB, 48 * E1 // EB, e)
            down1((e - 1) % EB, e - 1)
        down1(EB - 1, E1 - 1)

    @block.scalar
    def _(act):
        chain = Chain(act, act_step)
        for c in range(NC):
            act.wait_ge(xT_ready, c + 1)
            act.copy(XT[:, C * c:C * (c + 1)], BK[c]).then_inc(xT_copied, 1)
        for j in range(2 * NC + 1):
            if j < 2 * NC:
                c, w = divmod(j, 2)
                act.wait_ge(rot_ready, j + 1)
                act.copy(parts[:, w, 0, C * c:C * (c + 1)], ra[:, j % 4, :]).then_inc(part0_ready, 1)
            if j:
                c, w = divmod(j - 1, 2)
                act.wait_ge(rest_ready, j)
                act.copy(parts[:, w, 1, C * c:C * (c + 1)], ra[:, (j - 1) % 4, :]).then_inc(part1_ready, 1)
        for c in range(NC):
            act.wait_ge(v_ready, c + 1)
            b, kt = c // 2, TPC * (c % 2)
            act.copy(V[:, kt:kt + TPC, NH * b:NH * (b + 1), 0:2 * HD],
                     BK[4 + c].rearrange("p (k h d) -> p k h d", k=TPC, h=NH)).then_inc(v_copied, 1)

        act.wait_ge(vec_ready, 1)
        act.copy(VC[:], BK[4][:, 0:R_N]).then_inc(vec_copied, 1)
        act.wait_ge(const_set, 2)
        act.wait_ge(lam_sum, 1)
        act.activation(lams[:, 2:4], lams[:, 0:2], ACT.Exp).then_inc(lam_exp, 1)
        act.sem_inc(exp_done, CREDIT)

        def evacuate(g, half):
            act.wait_ge(pv_step, g * STEPS + (QT * (half + 1) + CREDIT))
            act.copy(PVs[:, C * half:C * (half + 1)], PV[:]).then_inc(pv_evac, 1)

        def group(g, u, last):
            for s in range(STEPS):
                for aa in range(4):
                    act.wait_ge(st_ready, g * (4 * STEPS) + (4 * s + aa + 1))
                    if aa == 0:
                        act.wait_ge(pv_step, g * STEPS + (s + 1))
                    act.activation(E[(u + s) % 3][:, aa, :], ST[(u + s + aa) % 3][:], ACT.Exp).then_inc(exp_done, 1)
                if s == 0:
                    evacuate(g - 1, 1)
                if s == QT:
                    act.wait_ge(s_ready, g * USES + (FIRST + OUT_POS + 1) if not last else use(NG - 1, 0) + 1)
                    evacuate(g, 0)

        with act.Fori(0, (NG - 1) // GB) as i:
            for u in range(GB):
                group(i * GB + u, u, False)
        group(NG - 1, 0, True)
        evacuate(NG - 1, 1)

        def turned(r, n, c, dst, scale=None, shift=None, bank0=0):
            act.wait_ge(tr_ready, NC * r + n + 1)
            if scale is None:
                ins = act.copy(dst(c), BK[bank0 + c])
            elif shift is None:
                ins = act.activation(dst(c), BK[bank0 + c], ACT.Copy, scale=scale)
            else:
                ins = act.activation(dst(c), BK[bank0 + c], ACT.Identity, scale=scale, bias=shift)
            ins.then_inc(fm_ready, 1)

        def xt(c):
            return XT[:, C * c:C * (c + 1)]

        calls = [1]

        def deviation(c, second=None):
            calls[0] += 1
            act.wait_ge(var_ready, calls[0])
            t = slice(TPC * c, TPC * (c + 1))
            if second is not None:
                e, bias = second
                act.activation(std[:, 1, t], mv[:, t, 1], ACT.Sqrt, bias=bias, scale=1.0 + e)
            act.activation(std[:, 0, t], mv[:, t, 1], ACT.Sqrt, bias=eps5[:]).then_inc(std_ready, 1)

        def weigh_rows(rows2, signal, c):
            if c == 0:
                return
            act.wait_ge(signal[c], 16)
            for k in range(2):
                for t in range(TPC * c, TPC * (c + 1)):
                    ins = act.activation(rows2[:, t, k, :], rows2[:, t, k, :], ACT.Copy, scale=wts[:, k, t:t + 1])
            ins.then_inc(rows_ready, 1)

        def norm_stage(copy=None, second=None, weigh=None, after=None):
            def dev(c):
                deviation(c, second)

            for stage, c in ((weigh, 0), (weigh, 1), (dev, 0), (weigh, 2), (dev, 1), (weigh, 3), (copy, 0), (dev, 2),
                             (copy, 1), (after, 0), (dev, 3), (copy, 2), (after, 1), (copy, 3), (after, 2), (after, 3)):
                if stage is not None:
                    stage(c)

        act.wait_ge(var_ready, 1)
        act.activation(rden[:, 0:NT * NH], ssq[:], ACT.Sqrt, bias=eps5[:],
                       scale=1.0 / (2 * HD)).then_inc(std_ready, 1)
        for n, c in enumerate(range(NC)):
            turned(0, n, c, xt)
        def rows_of(src, c):
            t = slice(TPC * c, TPC * (c + 1))
            for k in range(2):
                ins = act.copy(XI[:, t, k, 0:P], src[:, t, :])
            ins.then_inc(xi_ready, 1)

        for b in range(NB):
            pair = (2 * b, 2 * b + 1)
            for c in pair:
                deviation(c, (EPS_FFN, epsf[:]))
            for c in pair:
                turned(1, c, c, xt, VC[:, R_LNW:R_LNW + 1])
            for c in pair:
                rows_of(XS, c)
        act.wait_ge(top_diff, 1)
        act.activation(top[:, 5, :], top[:, 4, :], ACT.Exp).then_inc(r0_exp, 1)
        for c in range(NC):
            act.wait_ge(wet_ready, c + 1)
            act.copy(WET[:, C * c:C * (c + 1)], BK[c][0:E0, :]).then_inc(wet_taken, 1)
        act.wait_ge(tw_ready, 4)
        for bank, dst, n in ((0, cwt, 4), (1, w3t, 3), (2, wbt, 4), (3, wut, 4)):
            act.copy(dst[:].rearrange("p j d -> p (j d)"), BK[bank][:, 0:P * n]).then_inc(tw_taken, 1)

        def take_x0(h, t):
            act.wait_ge(xe0_ready, t + 1)
            act.activation(XT0[:, h, :], BK[6][:, 0:P], ACT.Copy, scale=VC[:, R_LNW:R_LNW + 1]).then_inc(xt0_taken, 1)

        def silu0(h, t):
            act.wait_ge(sum0_ready, t + 1)
            act.activation(SA0[:, h, :], A0[:, h, :], ACT.Silu).then_inc(silu0_done, 1)

        def take_g0(h, t):
            act.wait_ge(gt0_ready, t + 1)
            act.copy(GT0[:, h, :, :].rearrange("p f t -> p (f t)"), BK[4]).then_inc(gt0_taken, 1)

        def take_y0(b, uses, t):
            act.wait_ge(y0_ready, t + 1)
            act.wait_ge(y0_scattered[b], uses * 16 + 16)
            act.copy(YE0[:, b, :], BK[7][:, 0:P]).then_inc(y0_taken, 1)

        act.sem_inc(y0_taken, 1)
        take_x0(0, 0)
        for t in range(PEEL):
            take_x0((t + 1) % 2, t + 1)
            silu0(t % 2, t)
            if t >= 1:
                take_g0((t - 1) % 2, t - 1)
        with act.Fori(0, PASSES) as i:
            for u in range(4):
                h, b = (PEEL + u) % 2, (PEEL + u - 2) % XB
                take_x0(1 - h, i * 4 + (PEEL + u + 1))
                silu0(h, i * 4 + (PEEL + u))
                take_g0(1 - h, i * 4 + (PEEL + u - 1))
                take_y0(b, i if PEEL + u - 2 < XB else i + 1, i * 4 + (PEEL + u - 2))
        t = T0 - 1
        silu0(t % 2, t)
        take_g0((t - 1) % 2, t - 1)
        take_y0((t - 2) % XB, (t - 2) // XB, t - 2)
        take_g0(t % 2, t)
        take_y0((t - 1) % XB, (t - 1) // XB, t - 1)
        take_y0(t % XB, t // XB, t)

        act.wait_ge(in_mix, 16 * 8)
        def first_norm(c):
            act.wait_ge(tok_ready, 2 * NC + c + 1)
            for t in range(TPC * c, TPC * (c + 1)):
                ins = act.activation(X[:, t, :], X[:, t, :], ACT.Identity, scale=rstd[:, 0, t:t + 1],
                                     bias=shift[:, t:t + 1])
            ins.then_inc(x_normed, 1)

        norm_stage(
                   lambda c: turned(2, c, c, lambda c: HT[:, c // 2, 3 + C * (c % 2):3 + C * (c % 2 + 1)],
                                    VC[:, R_GB + 0:R_GB + 1], VC[:, R_GB + 1:R_GB + 2]),
                   (EPS, eps55[:]), lambda c: weigh_rows(YG0, yg0_loaded, c), first_norm)

        def take_qkv(c):
            for w in range(3):
                j = 3 * c + w
                act.wait_ge(qkv_ready, j + 1)
                act.activation((QF, KF, VF)[w][:, C * c:C * (c + 1)], BK[4 + j % 4], ACT.Identity,
                               bias=VC[:, R_BQKV + w:R_BQKV + w + 1]).then_inc(qkv_taken, 1)

        norm_stage(lambda c: turned(3, c, c, xt, VC[:, R_GB + 2:R_GB + 3], VC[:, R_GB + 3:R_GB + 4]),
                   after=take_qkv)
        norm_stage(
                   lambda c: turned(4, c, c, xt, VC[:, R_GB + 4:R_GB + 5], VC[:, R_GB + 5:R_GB + 6], 4))
        def gelu(c):
            if c >= 2:
                act.wait_ge(mo_ready, 4 * NC + c - 1)
            for f in range(4):
                j = 4 * c + f
                act.wait_ge(up_ready, j + 1)
                act.activation(G[:, c % 2, f, :], BK[j % 4], ACT.Gelu, bias=VC[:, R_BB + f:R_BB + f + 1]).then_inc(gelu_done, 1)

        def prob(b):
            t = slice(QT * b, QT * (b + 1))
            act.wait_ge(prob_sub, b + 1)
            act.activation(Lb[:, t, :], La[:, t, :], ACT.Exp).then_inc(prob_exp, 1)

        for c in range(3):
            gelu(c)
        for b in range(NB):
            pair = (2 * b, 2 * b + 1)
            for c in pair:
                deviation(c)
            if b == 0:
                gelu(3)
            for c in pair:
                turned(5, c, c, xt, bank0=4)
            prob(b)
            for c in pair:
                rows_of(X, c)
        act.sem_inc(xe_taken, 2)
        act.sem_inc(ye_taken, 2)
        for j in range(2 * NC):
            act.wait_ge(gu_ready, j + 1)
            act.activation(HS[:, j % 2, :], BK[2 * (j % 2)][0:FT, :], ACT.Silu).then_inc(h_silu, 1)

        def silu1(e):
            for f in range(2):
                act.wait_ge(gu_ready, e * 2 + (2 * NC + f + 1))
                act.activation(HS[:, f, 0:CAPN], BK[2 * f][0:FT, 0:CAPN], ACT.Silu).then_inc(h_silu, 1)

        def take_y1(b, uses, e):
            act.wait_ge(ye_ready, e + 1)
            act.wait_ge(y_scattered[b], uses * (16 * CR) + 16)
            ins = act.copy(YE[0:CP, b, :, :].rearrange("p r d -> p (r d)"), BK[4 + b % 2][0:CP, 0:P * CR])
            ins.then_inc(ye_taken, 1)

        silu1(0)
        with act.Fori(0, E1 // EB - 1) as i:
            for u in range(EB):
                silu1(i * EB + (u + 1))
                take_y1(u, i, i * EB + u)
        for e in range(E1 - EB + 1, E1):
            silu1(e)
            take_y1((e - 1) % EB, (e - 1) // EB, e - 1)
        take_y1(EB - 1, E1 // EB - 1, E1 - 1)
        norm_stage(weigh=lambda c: weigh_rows(YG, yg_loaded, c))

    @block.vector
    def _(dve):
        chain = Chain(dve, dve_step)
        dve.memset(PV[:], 0.0).then_inc(pv_zeroed, 1)
        dve.wait_ge(in_w, 16 * 2)
        for w in range(2):
            scale = HD ** -0.5 if w == 0 else 1.0
            dve.tensor_scalar(wq2[:, 2 * w, :], wqkv[:, w, :], scale, None, ALU.mult)
            src = wqkv[:, w, :].rearrange("p (h t) -> p h t", t=2)
            dst = wq2[:, 2 * w + 1, :].rearrange("p (h t) -> p h t", t=2)
            for t in range(2):
                ins = dve.tensor_scalar(dst[:, :, t], src[:, :, 1 - t], scale, None, ALU.mult)
        ins.then_inc(w2_ready, 1)
        dve.wait_ge(in_id, 16)
        dve.tensor_copy(identb[:], ident[:])
        dve.memset(PVs[:], 0.0)
        chain(dve.memset(XS[:], 0.0))
        dve.memset(empty.rearrange("p (r w) -> p r w", r=CR)[:, :, P], float(FAR))
        dve.memset(eps5[:], EPS)
        dve.memset(eps55[:], EPS * EPS)
        dve.memset(epsf[:], EPS_FFN * EPS).then_inc(const_set, 1)

        dve.wait_ge(in_tab, 32)
        for j in range(2 * NC + 1):
            if j < 2 * NC:
                c = j // 2
                tab = slice(C * (c % 2), C * (c % 2 + 1))
                r, q = ra[:, j % 4, :], rb[:, j % 2, :]
                dve.wait_ge(qk_ready, j + 1)
                if j >= 4:
                    dve.wait_ge(parts_ready, j - 3)
                dve.tensor_tensor(r, BK[2 * (j % 4)], cosT[:, tab], ALU.mult)
                dve.tensor_tensor(q, BK[2 * (j % 4) + 1], sinT[:, tab], ALU.mult).then_inc(qk_taken, 1)
                dve.wait_ge(qk_taken, j + 1)
                dve.tensor_tensor(r, r, q, ALU.add).then_inc(rot_ready, 1)
            if j:
                c, w = divmod(j - 1, 2)
                r = ra[:, (j - 1) % 4, :]
                dve.wait_ge(part0_ready, j)
                dve.tensor_tensor(r, r, parts[:, w, 0, C * c:C * (c + 1)], ALU.subtract).then_inc(rest_ready, 1)

        dve.sem_inc(s_taken, 2)

        def lambda_sums():
            dve.wait_ge(in_v, IN_V)
            for j in range(2):
                ins = dve.tensor_tensor(lamp[:, j, :], lamv[:, 2 * j, :], lamv[:, 2 * j + 1, :], ALU.mult)
            chain(ins)
            dve.reduce_sum(lams[:, 0:2], lamp[:], AX).then_inc(lam_sum, 1)

        def lambda_and_wo():
            dve.wait_ge(vec_copied, 1)
            chain(dve.tensor_scalar(gfac[:], VC[:, R_SUBLN:R_SUBLN + 1], 1.0 - LAMBDA_INIT, None, ALU.mult))
            dve.wait_ge(in_wo, 32)
            dve.tensor_scalar(wo[:], wqkv[:, 3, :], gfac[:], None, ALU.mult)
            dve.wait_ge(lam_exp, 1)
            chain(dve.scalar_tensor_tensor(lams[:, 4:5], lams[:, 3:4], -LAMBDA_INIT, lams[:, 2:3],
                                           ALU.add, ALU.subtract))

        def take_max(v, k, pos, g):
            qt, aa = divmod(k, 4)
            dve.wait_ge(s_ready, use(g, pos) + 1)
            dve.reduce_max(mx[v][:, qt, aa:aa + 1], SM[(1 + pos) % 2][:], AX).then_inc(s_taken, 1)

        def split_maxima(g, v, pos):
            dve.wait_ge(s_taken, use(g, pos) + 2)
            dve.tensor_scalar(TM[:, :, :, MAXROW], mx[v][:], -1.0, None, ALU.mult).then_inc(m_hi, 1)
            dve.wait_ge(m_hi, g + 2)
            dve.scalar_tensor_tensor(TM[:, :, :, MAXROW + 1], mx[v][:], -1.0, TM[:, :, :, MAXROW],
                                     ALU.mult, ALU.subtract).then_inc(tm_ready, 1)

        def take_rows(g, v, pos):
            dve.wait_ge(s_ready, use(g, pos) + 1)
            dve.tensor_tensor(Q2[v][:], SM[(1 + pos) % 2][:], QG[v][:], ALU.add).then_inc(s_taken, 1)

        def take_outputs(g, pos, phase):
            dve.wait_ge(s_ready, use(phase, pos) + 1)
            dve.tensor_copy(OT[:, :, bass.ds(g, 1), :, :].rearrange("p q g a v -> p q (g a) v"),
                            SM[(1 + pos) % 2][:].rearrange("p (q a r) -> p q a r", q=QT, a=4)[:, :, :, 0:VD])\
                .then_inc(s_taken, 1)

        def group(g, u):
            v, w, pos = (u + 1) % GB, (u + 2) % GB, 0
            for s in range(STEPS):
                if s == OUT_STEP:
                    take_outputs(g, pos, g)
                    pos += 1
                for what, k in PLAN[s]:
                    if what == "rows":
                        take_rows(g, v, pos)
                    else:
                        take_max(v if what == "next" else w, k, pos, g)
                    pos += 1
                    if (what, k) == ("next", 4 * QT - 1):
                        split_maxima(g, v, pos)

        dve.wait_ge(kq_loaded[0], 128)
        for k in range(4 * QT):
            take_max(0, k, k - use(-1, 0), -1)
            if k == 2 * QT:
                lambda_sums()
        split_maxima(-1, 0, 4 * QT - use(-1, 0))
        take_rows(-1, 0, 4 * QT - use(-1, 0))
        for k in range(EARLY):
            take_max(1, k, 4 * QT + 1 + k - use(-1, 0), -1)
        with dve.Fori(0, (NG - 1) // GB) as i:
            for u in range(GB):
                dve.wait_ge(kq_loaded[(u + 1) % GB], 128 * (i + (1 if (u + 1) % GB else 2)))
                group(i * GB + u, u)
        take_outputs(NG - 1, 0, NG - 1)

        def weigh_heads(lo, hi):
            o = OT[:, :, 1 + lo:1 + hi, :, :].rearrange("p q g a v -> p q (g a) v")
            rv = rden[:].rearrange("p (q m) -> p q m", q=QT)[:, :, 4 * lo:4 * hi]
            chain(dve.reciprocal(rv, o[:, :, :, 2 * HD]))
            r2 = rv.rearrange("p q (m s) -> p q m s", s=2)[:, :, :, 1]
            chain(dve.tensor_scalar(r2, r2, lams[:, 4:5], None, ALU.mult))
            nr = NRM.rearrange("p (q m d) -> p q m d", q=QT, d=8)[:, :, 4 * lo:4 * hi, :]
            chain(dve.tensor_tensor(nr, o[:, :, :, 0:2 * HD],
                                    rv.unsqueeze(3).to_broadcast([P, QT, 4 * (hi - lo), 8]), ALU.mult))
            n2 = nr.rearrange("p q (m s) d -> p q m s d", s=2)
            A = TMP[:].rearrange("p (q m d) -> p q m d", q=QT, d=8)[:, :, 2 * lo:2 * hi, :]
            chain(dve.tensor_tensor(A, n2[:, :, :, 0, :], n2[:, :, :, 1, :], ALU.add))
            chain(dve.tensor_tensor(n2[:, :, :, 0, :], A, A, ALU.mult))
            return dve.reduce_sum(ssq[:].rearrange("p (q m) -> p q m", q=QT)[:, :, 2 * lo:2 * hi],
                                  n2[:, :, :, 0, :], AX)

        lambda_and_wo()
        dve.wait_ge(s_taken, use(NG - 1, 0) + 3)
        weigh_heads(0, NG - 1)
        take_outputs(NG, 1, NG - 1)
        dve.wait_ge(s_taken, use(NG - 1, 1) + 3)
        weigh_heads(NG - 1, NG).then_inc(var_ready, 1)
        dve.wait_ge(std_ready, 1)
        rms = rden[:, NT * NH:2 * NT * NH]
        chain(dve.reciprocal(rms, rden[:, 0:NT * NH]))
        for b in range(NB):
            A = TMP[:].rearrange("p (q b h d) -> p q b h d", b=NB, h=NH, d=8)[:, :, b]
            r = rms.rearrange("p (q b h) -> p q b h", b=NB, h=NH)[:, :, b]
            chain(dve.tensor_tensor(A, A, r.unsqueeze(3).to_broadcast([P, QT, NH, 8]), ALU.mult))
            dve.sem_inc(tok_ready, 2)

        norms = [1]

        def tiles(c):
            return range(TPC * c, TPC * (c + 1))

        def norm(dst, src, signal, prepare=None, double=False, order=None):
            def begin(c):
                if prepare is not None:
                    prepare(c)
                for t in tiles(c):
                    ins = dve.bn_stats(stats[:, t, :], src[:, t, :])
                chain(ins)
                for t in tiles(c):
                    ins = dve.bn_aggr(mv[:, t, :], stats[:, t, :])
                ins.then_inc(var_ready, 1)

            def finish(c):
                norms[0] += 1
                dve.wait_ge(std_ready, norms[0])
                ts = slice(TPC * c, TPC * (c + 1))
                w = 2 if double else 1
                chain(dve.reciprocal(rstd[:, 0:w, ts], std[:, 0:w, ts]))
                if double:
                    dve.scalar_tensor_tensor(shift[:, ts], mv[:, ts, 0], -1.0, rstd[:, 0, ts], ALU.mult, ALU.mult)
                for t in tiles(c):
                    ins = dve.tensor_scalar(dst[:, t, :], src[:, t, :], mv[:, t, 0:1], rstd[:, w - 1, t:t + 1],
                                            ALU.subtract, ALU.mult)
                ins.then_inc(signal, 1)

            if order is None:
                order = lambda begin, finish: [(begin, 0), (begin, 1), (finish, 0), (begin, 2), (finish, 1),
                                               (begin, 3), (finish, 2), (finish, 3)]
            for stage, c in order(begin, finish):
                stage(c)

        def first_norm():
            for t in range(NT):
                ins = dve.tensor_scalar(X[:, t, :], X[:, t, :], mv[:, t, 0:1], rstd[:, 0, t:t + 1],
                                        ALU.subtract, ALU.mult)
            chain(ins)

        def add_chunk(dst, src, n, c, bank):
            dve.wait_ge(mo_ready, n + 1)
            dve.tensor_tensor(dst[:, TPC * c:TPC * (c + 1), :], BK[bank].rearrange("p (k d) -> p k d", d=P),
                              src[:, TPC * c:TPC * (c + 1), :], ALU.add).then_inc(mo_taken, 1)
            dve.wait_ge(mo_taken, n + 1)

        def row(v_, n=NT):
            return v_.unsqueeze(1).to_broadcast([P, n, v_.shape[-1]])

        def each(v_, e):
            return v_.unsqueeze(2).to_broadcast([P, NT, e])

        def part(b):
            return slice(QT * b, QT * (b + 1))

        def each(v_, e):
            return v_.unsqueeze(2).to_broadcast([P, QT, e])

        def select(L, Lc, rev, sa_, b, e):
            t = part(b)
            src = L
            for k in range(2):
                chain(dve.tensor_reduce(top[:, 2 * k, t], src, AX, ALU.max))
                chain(dve.tensor_tensor(sa_, src, each(top[:, 2 * k, t], e), ALU.is_equal))
                chain(dve.tensor_tensor(sa_, sa_, row(rev, QT), ALU.mult))
                chain(dve.tensor_reduce(top[:, 2 * k + 1, t], sa_, AX, ALU.max))
                chain(dve.tensor_tensor(oh[:, k, t, 0:e], sa_, each(top[:, 2 * k + 1, t], e), ALU.is_equal))
                if k == 0:
                    chain(dve.scalar_tensor_tensor(Lc, oh[:, 0, t, 0:e], -3.0e38, L, ALU.mult, ALU.add))
                    src = Lc
            sel = selx[:, 0:e, 1:QT + 1]
            chain(dve.tensor_tensor(sel.rearrange("p e t -> p t e"), oh[:, 0, t, 0:e], oh[:, 1, t, 0:e], ALU.add))
            chain(dve.tensor_tensor_scan(inclx[:, 0:e, :].rearrange("p e t -> p (e t)"), seg[:, 0:e * (QT + 1)],
                                         selx[:, 0:e, :].rearrange("p e t -> p (e t)"), 0.0, ALU.mult, ALU.add))
            dve.tensor_copy(selb[:, b, 0:e, :], sel)
            dve.tensor_copy(cumb[:, b, 0:e, :], inclx[:, 0:e, 0:QT])
            dve.tensor_copy(selx[:, 0:e, 0], inclx[:, 0:e, QT]).then_inc(sel_ready, 1)

        def pair_slots(r, b, e, base, capacity=None):
            dve.wait_ge(pos_ready, NB * r + b + 1)
            pos = BK[5 + 2 * b][:, 2 * P:2 * P + e * QT].rearrange("p (e t) -> p t e", e=e)
            slot = posx[:, 0, :, 0:e]
            if capacity is not None:
                dve.tensor_scalar(posx[:, 1, :, 0:e], pos, float(capacity), None, ALU.is_ge)
            chain(dve.tensor_tensor(slot, pos, row(base, QT), ALU.add))
            if capacity is not None:
                chain(dve.scalar_tensor_tensor(slot, posx[:, 1, :, 0:e], float(FAR), slot, ALU.mult, ALU.add))
            chain(dve.tensor_tensor(prod[:, :, :, 0:e], slot.unsqueeze(1).to_broadcast([P, 2, QT, e]),
                                    oh[:, :, part(b), 0:e], ALU.mult))
            chain(dve.reduce_sum(fidx[:], prod[:, :, :, 0:e], AX))
            dve.tensor_copy(idx[:, part(b), :].rearrange("p t k -> p k t"), fidx[:]).then_inc(idx_ready, 1)

        dve.memset(HT[:, :, 0:3], 0.0)
        dve.memset(onesS[:], 1.0)
        dve.memset(onesb[:], 1.0)
        dve.memset(selx[:], 0.0)
        dve.wait_ge(in_moe, 16 * 12)
        dve.tensor_copy(ltrib[:], ltri[:])
        dve.tensor_copy(XI[:, :, :, P], rowid[:])
        chain(dve.memset(cwm[:], 0.0))
        dve.wait_ge(in_mix, 16 * 8)
        for q in range(4):
            r = slice(32 * q, 32 * (q + 1))
            ins = dve.tensor_copy(cwm[r, :, r], cw[r, :, :].rearrange("p i t -> p t i"))
        ins.then_inc(cwm_ready, 1)

        dve.wait_ge(zeroed, 16 * 5)
        for b in range(EB):
            dve.wait_ge(y_scattered[b], 16)
            dve.wait_ge(y0_scattered[b], 16)
        def add_bias(L, b, e, bias):
            for c in (2 * b, 2 * b + 1):
                ins = dve.tensor_tensor(L[:, TPC * c:TPC * (c + 1), 0:e],
                                        BK[4 + c][:, 0:TPC * e].rearrange("p (t e) -> p t e", e=e), row(bias, TPC), ALU.add)
            chain(ins)

        def choose0(b):
            dve.wait_ge(lg_ready, 2 * b + 2)
            add_bias(L0, b, E0, bg0[:])
            select(L0[:, part(b), :], Lb[:, part(b), 0:E0], rev0[:], La[:, part(b), 0:E0], b, E0)

        def slots0(b):
            pair_slots(0, b, E0, base0[:])

        norm(XS, X, tok_ready, lambda c: add_chunk(X, X, c, c, 4 + c), True,
             lambda begin, finish: [(begin, 0), (begin, 1), (finish, 0), (finish, 1), (begin, 2), (choose0, 0),
                                    (slots0, 0), (begin, 3), (finish, 2), (finish, 3), (choose0, 1), (slots0, 1)])
        first_norm()

        dve.tensor_tensor(top[:, 4, :], top[:, 2, :], top[:, 0, :], ALU.subtract).then_inc(top_diff, 1)
        chain(dve.tensor_copy(totb[:], inclx[:, 0:E0, QT]))
        dve.sem_inc(tot_ready, 1)
        dve.wait_ge(r0_exp, 1)
        chain(dve.tensor_scalar(top[:, 6, :], top[:, 5, :], 1.0, None, ALU.add))
        chain(dve.reciprocal(wts[:, 0, :], top[:, 6, :]))
        chain(dve.tensor_tensor(wts[:, 1, :], wts[:, 0, :], top[:, 5, :], ALU.mult))
        for k in range(2):
            ins = dve.tensor_tensor((La, Lb)[k][:, :, 0:E0], oh[:, k, :, 0:E0],
                                    wts[:, k, :].unsqueeze(2).to_broadcast([P, NT, E0]), ALU.mult)
        chain(ins)
        dve.tensor_tensor(WE[:], La[:, :, 0:E0], Lb[:, :, 0:E0], ALU.add).then_inc(we_ready, 1)

        dve.wait_ge(pos0_ready, 1)
        chain(dve.tensor_tensor(over[:], BK[7][:, 3 * P:3 * P + E0].unsqueeze(2).to_broadcast([P, E0, NT]),
                                steps0[:, 0:NT].unsqueeze(1).to_broadcast([P, E0, NT]), ALU.is_gt))
        chain(dve.reduce_sum(ends[:, 0, :], over[:], AX))
        chain(dve.tensor_scalar(ends[:, 0, :], ends[:, 0, :], float(P), None, ALU.mult))
        chain(dve.tensor_tensor_scan(ends[:, 1, :], onesS[:, 0:E0], ends[:, 0, :], 0.0, ALU.mult, ALU.add))
        chain(dve.tensor_scalar(ends[:, 2, :], ends[:, 0, :], -1.0, float(N), ALU.mult, ALU.add))
        chain(dve.memset(ends[:, 2, E0 - 1:E0], 0.0))
        chain(dve.tensor_tensor(passed[:], steps0[:].unsqueeze(2).to_broadcast([P, T0, E0]),
                                ends[:, 1, :].unsqueeze(1).to_broadcast([P, T0, E0]), ALU.is_ge))
        chain(dve.reduce_sum(tile_f[:, 0, :], passed[:], AX))
        dve.tensor_scalar(tile_e[:], tile_f[:, 0, :], float(E0 - 1), None, ALU.min)
        chain(dve.tensor_tensor(skipped[:], passed[:], ends[:, 2, :].unsqueeze(1).to_broadcast([P, T0, E0]), ALU.mult))
        chain(dve.reduce_sum(tile_f[:, 1, :], skipped[:], AX))
        chain(dve.tensor_tensor(tile_f[:, 1, :], tile_f[:, 1, :], steps0[:], ALU.add))
        dve.tensor_scalar(tile_s[:], tile_f[:, 1, :], 1.0 / P, None, ALU.mult).then_inc(tiles_ready, 1)
        for c in range(NC):
            add_chunk(X, X, NC + c, c, 4 + c)

        def gate0(h, b, uses, t, free):
            e = dve.value_load(tile_e[0:1, bass.ds(t, 1)], min_val=0, max_val=E0 - 1)
            dve.wait_ge(ab0_ready, t + 1)
            dve.tensor_tensor(A0[:, h, :], BK[2 * h], B1[:, bass.ds(e, 1), 0, :].rearrange("p e f -> p (e f)"),
                              ALU.add).then_inc(sum0_ready, 1)
            if free is not None:
                dve.wait_ge(gt0_ready, free)
            dve.tensor_tensor(U0[:, h, :], BK[2 * h + 1], B1[:, bass.ds(e, 1), 1, :].rearrange("p e f -> p (e f)"),
                              ALU.add).then_inc(ab0_taken, 1)
            dve.wait_ge(y0_scattered[b], uses * 16 + 16)
            dve.tensor_copy(oid0[:, b:b + 1], XE0[:, b, P:P + 1])
            dve.wait_ge(ab0_taken, t + 1)
            dve.wait_ge(silu0_done, t + 1)
            dve.tensor_tensor(G0[:, h, :], SA0[:, h, :], U0[:, h, :], ALU.mult).then_inc(g0_done, 1)

        dve.wait_ge(tiles_ready, 1)
        dve.wait_ge(w0_loaded, 16 * 5 * E0)
        for t in range(PEEL):
            gate0(t % 2, t, 0, t, None)
        with dve.Fori(0, PASSES) as i:
            for u in range(4):
                gate0((PEEL + u) % 2, (PEEL + u) % XB, i if PEEL + u < XB else i + 1, i * 4 + (PEEL + u),
                      i * 4 + (PEEL + u - 1))
        t = T0 - 1
        gate0(t % 2, t % XB, t // XB, t, t - 1)

        def add_rows(dst, rows2, loaded, n):
            def add(c):
                t = slice(TPC * c, TPC * (c + 1))
                if c == 0:
                    dve.wait_ge(loaded[c], 16)
                    for k in range(2):
                        for i in tiles(c):
                            ins = dve.scalar_tensor_tensor(dst[:, i, :], rows2[:, i, k, :], wts[:, k, i:i + 1],
                                                           dst[:, i, :], ALU.mult, ALU.add)
                        chain(ins)
                    return
                dve.wait_ge(rows_added, (NC - 1) * n + c)
                chain(dve.tensor_tensor(dst[:, t, :], rows2[:, t, 0, :], dst[:, t, :], ALU.add))
            return add

        norm(XS, X, tok_ready, add_rows(X, YG0, yg0_loaded, 0), True)

        def add_conv(c):
            dve.wait_ge(x0_ready, c + 1)
            add_chunk(X0, X0, 2 * NC + c, c, 4 + c)

        norm(XS, X0, tok_ready, add_conv)
        for b in range(NB):
            r = slice(S * b, S * (b + 1))
            dve.wait_ge(qkv_taken, 6 * (b + 1))
            chain(dve.tensor_tensor_scan(TMP[:, r], onesS[:], QF[:, r], 0.0, ALU.mult, ALU.add))
            dve.wait_ge(kv_scaled, 2 * b + 1)
            chain(dve.tensor_tensor(TMP[:, r], TMP[:, r], KF[:, r], ALU.mult))
            chain(dve.tensor_tensor_scan(QF[:, r], onesS[:], TMP[:, r], 0.0, ALU.mult, ALU.add))
            dve.wait_ge(kv_scaled, 2 * b + 2)
            dve.tensor_tensor(QF[:, r], QF[:, r], VF[:, r], ALU.mult).then_inc(pool_done, 1)
        norm(XS, X0, tok_ready, lambda c: add_chunk(X0, X0, 3 * NC + c, c, c))
        chain(dve.tensor_tensor(X[:], X[:], X0[:], ALU.add))
        chain(dve.tensor_tensor(X[:], X[:], row(rows[:, 1, :]), ALU.add))
        dve.sem_inc(h_done, 2)
        chain(dve.memset(selx[:], 0.0))

        def choose1(b):
            t = part(b)
            dve.wait_ge(lg_ready, NC + 2 * b + 2)
            add_bias(La, b, E1, rbb[:])
            chain(dve.tensor_reduce(top[:, 4, t], La[:, t, :], AX, ALU.max))
            dve.tensor_tensor(La[:, t, :], La[:, t, :], each(top[:, 4, t], E1), ALU.subtract).then_inc(prob_sub, 1)
            dve.wait_ge(prob_exp, b + 1)
            chain(dve.reduce_sum(top[:, 4, t], Lb[:, t, :], AX))
            chain(dve.reciprocal(top[:, 5, t], top[:, 4, t]))
            chain(dve.tensor_tensor(La[:, t, :], Lb[:, t, :], each(top[:, 5, t], E1), ALU.mult))
            select(La[:, t, :], Lb[:, t, :], rev1[:], prod[:, 0, :, :], b, E1)
            pair_slots(1, b, E1, base1[:], CAP)

        norm(X, X, tok_ready, lambda c: add_chunk(X, X, 4 * NC + c, c, 4 + c), False,
             lambda begin, finish: [(begin, 0), (begin, 1), (finish, 0), (finish, 1), (choose1, 0),
                                    (begin, 2), (begin, 3), (finish, 2), (finish, 3), (choose1, 1)])
        chain(dve.tensor_tensor(top[:, 4, :], top[:, 0, :], top[:, 2, :], ALU.add))
        chain(dve.tensor_scalar(top[:, 4, :], top[:, 4, :], 1e-9, None, ALU.add))
        chain(dve.reciprocal(top[:, 5, :], top[:, 4, :]))
        for k in range(2):
            ins = dve.tensor_tensor(wts[:, k, :], top[:, 2 * k, :], top[:, 5, :], ALU.mult)
        chain(ins)

        def gate_shared(c, f):
            j = 2 * c + f
            dve.wait_ge(h_silu, j + 1)
            if c >= 2 and f == 0:
                dve.wait_ge(shared_ready, c - 1)
            dve.tensor_tensor(H[:, c % 2, f, :], HS[:, f, :], BK[2 * f + 1][0:FT, :], ALU.mult).then_inc(h_done, 1)

        def shared_out(c):
            dve.wait_ge(shared_ready, c + 1)
            dve.tensor_tensor(XS[:, TPC * c:TPC * (c + 1), :], BK[4 + c % 2].rearrange("p (k d) -> p k d", d=P),
                              XS[:, TPC * c:TPC * (c + 1), :], ALU.add).then_inc(shared_taken, 1)

        dve.sem_inc(shared_taken, 2)
        chain(dve.tensor_scalar(XS[:], X[:], 2.0, None, ALU.mult))
        for c in range(NC):
            for f in range(2):
                gate_shared(c, f)
            if c:
                shared_out(c - 1)
        shared_out(NC - 1)

        def take_tokens1(b, e):
            dve.wait_ge(xe_ready, e + 1)
            dve.tensor_copy(XET[:, b % 2, :, :].rearrange("p r c -> p (r c)"), BK[6 + b % 2][:, 0:CAPN]).then_inc(xe_taken, 1)

        def gate1(b, uses, e):
            dve.wait_ge(y_scattered[b], uses * (16 * CR) + 16)
            dve.tensor_copy(oid[0:CP, b, :], XE[0:CP, b, :, P])
            for f in range(2):
                dve.wait_ge(h_silu, e * 2 + (2 * NC + f + 1))
                if f == 0:
                    dve.wait_ge(ye_taken, e + 1)
                dve.tensor_tensor(H[:, b % 2, f, 0:CAPN], HS[:, f, 0:CAPN], BK[2 * f + 1][0:FT, 0:CAPN],
                                  ALU.mult).then_inc(h_done, 1)

        take_tokens1(0, 0)
        take_tokens1(1, 1)
        gate1(0, 0, 0)
        with dve.Fori(0, E1 // EB - 1) as i:
            for u in range(EB):
                b, e = (u + 1) % EB, i * EB + (u + 1)
                take_tokens1((b + 1) % EB, e + 1)
                gate1(b, i if u + 1 < EB else i + 1, e)
        for e in range(E1 - EB + 1, E1):
            if e + 1 < E1:
                take_tokens1((e + 1) % EB, e + 1)
            gate1(e % EB, e // EB, e)

        norm(XS, XS, result_ready, add_rows(XS, YG, yg_loaded, 1))


_NAMES = {
    "x": "L0_attn_x", "Wq": "L0_attn_Wq", "Wk": "L0_attn_Wk", "Wv": "L0_attn_Wv", "Wo": "L0_attn_Wo",
    "lq1": "L0_attn_lambda_q1", "lk1": "L0_attn_lambda_k1", "lq2": "L0_attn_lambda_q2", "lk2": "L0_attn_lambda_k2",
    "subln_g": "L0_attn_subln_g", "ln_w": "L0_ffn_ln_w", "Wg": "L0_ffn_Wg", "bg": "L0_ffn_bg",
    "W1a": "L0_ffn_W1a", "b1a": "L0_ffn_b1a", "W1b": "L0_ffn_W1b", "b1b": "L0_ffn_b1b", "W2": "L0_ffn_W2",
    "b2": "L0_ffn_b2", "ln_attn_g": "L1_attn_ln_attn_g", "ln_attn_b": "L1_attn_ln_attn_b", "mWq": "L1_attn_Wq",
    "bq": "L1_attn_bq", "mWk": "L1_attn_Wk", "bk": "L1_attn_bk", "mWv": "L1_attn_Wv", "bv": "L1_attn_bv",
    "ln_conv_g": "L1_attn_ln_conv_g", "ln_conv_b": "L1_attn_ln_conv_b", "conv_w": "L1_attn_conv_w",
    "conv_b": "L1_attn_conv_b", "ln_boom_g": "L1_attn_ln_boom_g", "ln_boom_b": "L1_attn_ln_boom_b",
    "Wb": "L1_attn_Wb", "bb": "L1_attn_bb", "Wu": "L1_attn_Wu", "bu": "L1_attn_bu",
    "router_w": "L1_ffn_router_w", "router_b": "L1_ffn_router_b", "w_gate": "L1_ffn_w_gate",
    "w_up": "L1_ffn_w_up", "w_down": "L1_ffn_w_down", "sw_gate": "L1_ffn_sw_gate", "sw_up": "L1_ffn_sw_up",
    "sw_down": "L1_ffn_sw_down",
}


def _constants(np):
    f = np.float32
    d = np.arange(P) % HD
    freq = f(1.0) / f(0.0001) ** (f(2.0) * np.arange(HD // 2, dtype=f) / f(HD))
    angle = np.arange(S, dtype=f)[None, :] * freq[d // 2][:, None]
    sign = np.where(d % 2 == 0, f(-1.0), f(1.0))[:, None]
    return {
        "ident": np.eye(P, dtype=f),
        "cos": np.cos(angle.astype(np.float64)).astype(f),
        "sin": np.sin(angle.astype(np.float64)).astype(f) * sign,
        "rev0": np.arange(E0, 0, -1).astype(f),
        "rev1": np.arange(E1, 0, -1).astype(f),
        "base1": (np.arange(E1) * CAPS).astype(f),
        "rowid": (2 * (np.arange(P)[:, None, None] + P * np.arange(NT)[None, :, None])
                  + np.arange(2)[None, None, :]).astype(f),
        "base0": (np.arange(E0) * N).astype(f),
        "seg": np.tile((np.arange(QT + 1) > 0).astype(f), E1),
        "steps0": (P * np.arange(T0)).astype(f),
        "ltri": np.triu(np.ones((P, P), f), 1),
        "invp": f(1.0) / np.arange(1, S + 1, dtype=f),
    }


def kernel(**inputs):
    import numpy as _np
    import concourse.bacc as _bacc
    from concourse import mybir as _mybir
    from concourse.bass_utils import run_bass_kernel_spmd as _run

    nc = _bacc.Bacc("TRN2", target_bir_lowering=False, num_devices=1)
    arrays, aps = {}, {}
    given = {short: _np.ascontiguousarray(inputs[name]) for short, name in _NAMES.items()}
    for name, v in {**given, **_constants(_np)}.items():
        arrays[f"in_{name}"] = v
        aps[name] = nc.dram_tensor(f"in_{name}", v.shape, _mybir.dt.from_np(v.dtype), kind="ExternalInput").ap()
    out = nc.dram_tensor("out", (NB, S, P), F32, kind="ExternalOutput").ap()
    build(nc, aps, out)
    r = _run(nc, [arrays], core_ids=[0])
    return r.results[0]["out"]
```
